# Optimizing a Trainium2 kernel written in Bass

```python
import numpy as np
import jax
import jax.numpy as jnp

def _softmax(x, axis=-1):
    return jax.nn.softmax(x, axis=axis)

def _gelu(x):
    return jax.nn.gelu(x, approximate=True)

def _silu(x):
    return jax.nn.silu(x)

def _sigmoid(x):
    return jax.nn.sigmoid(x)

def _layernorm(x, axis=-1, eps=1e-05):
    m = jnp.mean(x, axis=axis, keepdims=True)
    v = jnp.var(x, axis=axis, keepdims=True)
    return (x - m) / jnp.sqrt(v + eps)

def _scatter_add(tgt, idx, src, axis=0):
    return tgt.at[idx].add(src)

def _segment_sum(src, seg, n):
    return jax.ops.segment_sum(src, seg, n)
kernel_name = 'mk_early_fusion_d2_tok_img512_r4_c9d004'

def setup_inputs(seed: int=0):
    np.random.seed(seed)
    _w = jnp.asarray

    def _rec_inputs():
        import jax
        import jax.numpy as jnp
        _rk = jax.random.key(seed)
        x = -0.000356955 + 1 * jax.random.normal(jax.random.fold_in(_rk, 1), (64, 3, 224, 224), jnp.float32)
        txt = 0.0185972 + 1.43333 * jax.random.normal(jax.random.fold_in(_rk, 2), (64, 128, 128), jnp.float32)
        return (x, txt)
    x, txt = _rec_inputs()

    def _L0_tok_setup():
        import jax, jax.numpy as jnp
        import numpy as np
        key = jax.random.key(seed)
        k1, k2, k3 = jax.random.split(key, 3)
        B, C, H, W = (128, 3, 224, 224)
        E, p = (128, 16)
        K = C * p * p
        img = jax.random.normal(k1, (B, C, H, W), dtype=jnp.float32)
        w = jax.random.normal(k2, (E, K), dtype=jnp.float32) * (1.0 / np.sqrt(K))
        b = jax.random.normal(k3, (E,), dtype=jnp.float32)
        return {'img': img, 'w': w, 'b': b, 'patch_size': p}
    _L0_tok_all = _L0_tok_setup()
    _L0_tok_in = {k: v for k, v in _L0_tok_all.items() if k in ('w', 'b')}
    del _L0_tok_all

    def _L0_attn_setup():
        import jax, jax.numpy as jnp
        import numpy as np
        T, B, E, H = (512, 4, 128, 8)
        HD = E // H

        def _rotate_half(x):
            x1, x2 = jnp.split(x, 2, axis=-1)
            return jnp.concatenate([-x2, x1], axis=-1)
        key = jax.random.key(seed)
        ks = jax.random.split(key, 9)
        s = 0.05
        return {'query': jax.random.normal(ks[0], (T, B, E), jnp.float32), 'Wq': jax.random.normal(ks[1], (E, E), jnp.float32) * s, 'bq': jax.random.normal(ks[2], (E,), jnp.float32) * s, 'Wk': jax.random.normal(ks[3], (E, E), jnp.float32) * s, 'bk': jax.random.normal(ks[4], (E,), jnp.float32) * s, 'Wv': jax.random.normal(ks[5], (E, E), jnp.float32) * s, 'bv': jax.random.normal(ks[6], (E,), jnp.float32) * s, 'Wo': jax.random.normal(ks[7], (E, E), jnp.float32) * s, 'bo': jax.random.normal(ks[8], (E,), jnp.float32) * s}
    _L0_attn_all = _L0_attn_setup()
    _L0_attn_in = {k: v for k, v in _L0_attn_all.items() if k in ('Wq', 'bq', 'Wk', 'bk', 'Wv', 'bv', 'Wo', 'bo')}
    del _L0_attn_all

    def _L0_ffn_setup():
        import jax, jax.numpy as jnp
        import numpy as np
        E, D, H = (8, 128, 512)
        B, N = (8, 128)
        key = jax.random.key(seed)
        ks = jax.random.split(key, 4)

        def init(k, shape, fan_in):
            return jax.random.normal(k, shape, jnp.float32) * (1.0 / np.sqrt(fan_in))
        return {'x': jax.random.normal(ks[0], (B, N, D), jnp.float32), 'Wr': init(ks[1], (D, E), D), 'br': jnp.zeros((E,), jnp.float32), 'W1': init(ks[2], (E, D, H), D), 'b1': jnp.zeros((E, H), jnp.float32), 'W2': init(ks[3], (E, H, D), H), 'b2': jnp.zeros((E, D), jnp.float32)}
    _L0_ffn_all = _L0_ffn_setup()
    _L0_ffn_in = {k: v for k, v in _L0_ffn_all.items() if k in ('Wr', 'br', 'W1', 'b1', 'W2', 'b2')}
    del _L0_ffn_all

    def _L1_attn_setup():
        import jax, jax.numpy as jnp
        import numpy as np
        W_WIN = 20
        HOP = 10
        NHEAD = 8

        def _layernorm(x, g, b, eps=1e-05):
            m = x.mean(-1, keepdims=True)
            v = x.var(-1, keepdims=True)
            return (x - m) / jnp.sqrt(v + eps) * g + b

        def _mha(x, w_in, b_in, w_out, b_out):
            Bn, W, E = x.shape
            hd = E // NHEAD
            qkv = x @ w_in.T + b_in
            q, k, v = jnp.split(qkv, 3, axis=-1)
            q = q.reshape(Bn, W, NHEAD, hd)
            k = k.reshape(Bn, W, NHEAD, hd)
            v = v.reshape(Bn, W, NHEAD, hd)
            scores = jnp.einsum('bqhd,bkhd->bhqk', q, k) / jnp.sqrt(jnp.asarray(hd, x.dtype))
            attn = jax.nn.softmax(scores, axis=-1)
            out = jnp.einsum('bhqk,bkhd->bqhd', attn, v).reshape(Bn, W, E)
            return out @ w_out.T + b_out
        key = jax.random.key(seed)
        ks = jax.random.split(key, 4)
        B, L, C = (8, 1024, 128)
        x = jax.random.normal(ks[0], (B, L, C), dtype=jnp.float32)
        ln_g = jnp.ones((C,), jnp.float32)
        ln_b = jnp.zeros((C,), jnp.float32)
        w_in = jax.random.normal(ks[1], (3 * C, C), dtype=jnp.float32) * 0.02
        b_in = jnp.zeros((3 * C,), jnp.float32)
        w_out = jax.random.normal(ks[2], (C, C), dtype=jnp.float32) * 0.02
        b_out = jnp.zeros((C,), jnp.float32)
        return {'x': x, 'ln_g': ln_g, 'ln_b': ln_b, 'w_in': w_in, 'b_in': b_in, 'w_out': w_out, 'b_out': b_out}
    _L1_attn_all = _L1_attn_setup()
    _L1_attn_in = {k: v for k, v in _L1_attn_all.items() if k in ('ln_g', 'ln_b', 'w_in', 'b_in', 'w_out', 'b_out')}
    del _L1_attn_all

    def _L1_ffn_setup():
        import jax, jax.numpy as jnp
        import numpy as np
        NUM_EXPERTS = 32
        GROUP_SIZE = 4
        NUM_GROUPS = NUM_EXPERTS // GROUP_SIZE
        C_CAP = 1.0
        key = jax.random.key(seed)
        ks = jax.random.split(key, 5)
        B, S, H = (16, 512, 128)
        D_FF = int(H * 4 * (2.0 / 3.0))
        x = jax.random.normal(ks[0], (B, S, H), dtype=jnp.float32)
        W_router = jax.random.normal(ks[1], (H, NUM_EXPERTS), dtype=jnp.float32) * (1.0 / np.sqrt(H))
        b_router = jnp.zeros((NUM_EXPERTS,), dtype=jnp.float32)
        W_up = jax.random.normal(ks[2], (NUM_GROUPS, H, D_FF), dtype=jnp.float32) * (1.0 / np.sqrt(H))
        b_up = jnp.zeros((NUM_GROUPS, D_FF), dtype=jnp.float32)
        W_down = jax.random.normal(ks[3], (NUM_EXPERTS, D_FF, H), dtype=jnp.float32) * (1.0 / np.sqrt(D_FF))
        b_down = jnp.zeros((NUM_EXPERTS, H), dtype=jnp.float32)
        return {'x': x, 'W_router': W_router, 'b_router': b_router, 'W_up': W_up, 'b_up': b_up, 'W_down': W_down, 'b_down': b_down}
    _L1_ffn_all = _L1_ffn_setup()
    _L1_ffn_in = {k: v for k, v in _L1_ffn_all.items() if k in ('W_router', 'b_router', 'W_up', 'b_up', 'W_down', 'b_down')}
    del _L1_ffn_all
    return {'x': x, 'txt': txt, 'L0_tok_w': _L0_tok_in['w'], 'L0_tok_b': _L0_tok_in['b'], 'L0_attn_Wq': _L0_attn_in['Wq'], 'L0_attn_bq': _L0_attn_in['bq'], 'L0_attn_Wk': _L0_attn_in['Wk'], 'L0_attn_bk': _L0_attn_in['bk'], 'L0_attn_Wv': _L0_attn_in['Wv'], 'L0_attn_bv': _L0_attn_in['bv'], 'L0_attn_Wo': _L0_attn_in['Wo'], 'L0_attn_bo': _L0_attn_in['bo'], 'L0_ffn_Wr': _L0_ffn_in['Wr'], 'L0_ffn_br': _L0_ffn_in['br'], 'L0_ffn_W1': _L0_ffn_in['W1'], 'L0_ffn_b1': _L0_ffn_in['b1'], 'L0_ffn_W2': _L0_ffn_in['W2'], 'L0_ffn_b2': _L0_ffn_in['b2'], 'L1_attn_ln_g': _L1_attn_in['ln_g'], 'L1_attn_ln_b': _L1_attn_in['ln_b'], 'L1_attn_w_in': _L1_attn_in['w_in'], 'L1_attn_b_in': _L1_attn_in['b_in'], 'L1_attn_w_out': _L1_attn_in['w_out'], 'L1_attn_b_out': _L1_attn_in['b_out'], 'L1_ffn_W_router': _L1_ffn_in['W_router'], 'L1_ffn_b_router': _L1_ffn_in['b_router'], 'L1_ffn_W_up': _L1_ffn_in['W_up'], 'L1_ffn_b_up': _L1_ffn_in['b_up'], 'L1_ffn_W_down': _L1_ffn_in['W_down'], 'L1_ffn_b_down': _L1_ffn_in['b_down']}

def reference(x, txt, L0_tok_w, L0_tok_b, L0_attn_Wq, L0_attn_bq, L0_attn_Wk, L0_attn_bk, L0_attn_Wv, L0_attn_bv, L0_attn_Wo, L0_attn_bo, L0_ffn_Wr, L0_ffn_br, L0_ffn_W1, L0_ffn_b1, L0_ffn_W2, L0_ffn_b2, L1_attn_ln_g, L1_attn_ln_b, L1_attn_w_in, L1_attn_b_in, L1_attn_w_out, L1_attn_b_out, L1_ffn_W_router, L1_ffn_b_router, L1_ffn_W_up, L1_ffn_b_up, L1_ffn_W_down, L1_ffn_b_down):
    import jax
    import jax.numpy as jnp

    def _L0_tok_ref(img, w, b, patch_size):
        import jax, jax.numpy as jnp
        import numpy as np
        B, C, H, W = img.shape
        p = patch_size
        Hp, Wp = (H // p, W // p)
        S = Hp * Wp
        patches = img.reshape(B, C, Hp, p, Wp, p)
        patches = patches.transpose(0, 2, 4, 1, 3, 5).reshape(B, S, C * p * p)
        out = jnp.einsum('bsk,ek->bse', patches, w) + b
        return out

    def _L0_attn_ref(query, Wq, bq, Wk, bk, Wv, bv, Wo, bo):
        import jax, jax.numpy as jnp
        import numpy as np
        T, B, E, H = (512, 4, 128, 8)
        HD = E // H

        def _rotate_half(x):
            x1, x2 = jnp.split(x, 2, axis=-1)
            return jnp.concatenate([-x2, x1], axis=-1)
        t_len, bsz, e = query.shape
        scaling = HD ** (-0.5)
        q = (query @ Wq.T + bq) * scaling
        k = query @ Wk.T + bk
        v = query @ Wv.T + bv
        split = lambda x: x.reshape(t_len, bsz * H, HD).transpose(1, 0, 2)
        q, k, v = (split(q), split(k), split(v))
        inv_freq = 1.0 / 10000.0 ** (jnp.arange(0, HD, 2, dtype=jnp.float32) / HD)
        t = jnp.arange(t_len, dtype=jnp.float32)
        freqs = t[:, None] * inv_freq[None, :]
        emb = jnp.concatenate([freqs, freqs], axis=-1)
        cos, sin = (jnp.cos(emb)[None], jnp.sin(emb)[None])
        q = q * cos + _rotate_half(q) * sin
        k = k * cos + _rotate_half(k) * sin
        scores = jnp.einsum('bqd,bkd->bqk', q, k)
        w = jax.nn.softmax(scores.astype(jnp.float32), axis=-1).astype(query.dtype)
        attn = jnp.einsum('bqk,bkd->bqd', w, v)
        attn = attn.transpose(1, 0, 2).reshape(t_len, bsz, e)
        return attn @ Wo.T + bo

    def _L0_ffn_ref(x, Wr, br, W1, b1, W2, b2):
        import jax, jax.numpy as jnp
        import numpy as np
        E, D, H = (8, 128, 512)
        B, N = (8, 128)
        b, n, d = x.shape
        xt = x.reshape(-1, d)
        route_prob = jax.nn.softmax(xt.astype(jnp.float32) @ Wr + br, axis=-1)
        routes = jnp.argmax(route_prob, axis=-1)
        p_max = jnp.max(route_prob, axis=-1)

        def expert_step(acc, inp):
            w1, bb1, w2, bb2, e = inp
            h = jax.nn.gelu(xt @ w1 + bb1, approximate=False)
            y = h @ w2 + bb2
            return (acc + y * (routes == e)[:, None].astype(y.dtype), None)
        out, _ = jax.lax.scan(expert_step, jnp.zeros_like(xt), (W1, b1, W2, b2, jnp.arange(E)))
        out = out * (p_max / jax.lax.stop_gradient(p_max))[:, None]
        return out.reshape(b, n, d)

    def _L1_attn_ref(x, ln_g, ln_b, w_in, b_in, w_out, b_out):
        import jax, jax.numpy as jnp
        import numpy as np
        W_WIN = 20
        HOP = 10
        NHEAD = 8

        def _layernorm(x, g, b, eps=1e-05):
            m = x.mean(-1, keepdims=True)
            v = x.var(-1, keepdims=True)
            return (x - m) / jnp.sqrt(v + eps) * g + b

        def _mha(x, w_in, b_in, w_out, b_out):
            Bn, W, E = x.shape
            hd = E // NHEAD
            qkv = x @ w_in.T + b_in
            q, k, v = jnp.split(qkv, 3, axis=-1)
            q = q.reshape(Bn, W, NHEAD, hd)
            k = k.reshape(Bn, W, NHEAD, hd)
            v = v.reshape(Bn, W, NHEAD, hd)
            scores = jnp.einsum('bqhd,bkhd->bhqk', q, k) / jnp.sqrt(jnp.asarray(hd, x.dtype))
            attn = jax.nn.softmax(scores, axis=-1)
            out = jnp.einsum('bhqk,bkhd->bqhd', attn, v).reshape(Bn, W, E)
            return out @ w_out.T + b_out
        B, L, C = x.shape
        starts = np.arange(0, L - W_WIN + 1, HOP)
        S = starts.shape[0]
        idx = starts[:, None] + np.arange(W_WIN)
        segs = x[:, idx].reshape(B * S, W_WIN, C)
        normed = _layernorm(segs, ln_g, ln_b)
        segs_out = normed + _mha(normed, w_in, b_in, w_out, b_out)
        chunks = segs_out.reshape(S, B, W_WIN, C)
        vals = chunks.transpose(1, 0, 2, 3).reshape(B, S * W_WIN, C)
        flat_idx = idx.reshape(-1)
        out = jnp.zeros_like(x).at[:, flat_idx].add(vals)
        cnt = jnp.zeros((B, L), x.dtype).at[:, flat_idx].add(1.0)
        return out / jnp.clip(cnt, 1.0)[..., None] + x

    def _L1_ffn_ref(x, W_router, b_router, W_up, b_up, W_down, b_down):
        import jax, jax.numpy as jnp
        import numpy as np
        NUM_EXPERTS = 32
        GROUP_SIZE = 4
        NUM_GROUPS = NUM_EXPERTS // GROUP_SIZE
        C_CAP = 1.0
        B, S, H = x.shape
        bs = B * S
        E = NUM_EXPERTS
        k = min(int(bs * C_CAP) // E, bs)
        xf = x.reshape(bs, H)
        h = xf @ W_router + b_router
        Sm = jax.nn.softmax(h, axis=-1)
        G_ek, idx_ek = jax.lax.top_k(Sm.T, k)
        tokens = xf[idx_ek]
        D_FF = W_up.shape[-1]
        tok_g = tokens.reshape(NUM_GROUPS, GROUP_SIZE, k, H)
        up = jnp.einsum('gjkh,ghf->gjkf', tok_g, W_up) + b_up[:, None, None, :]
        act = jax.nn.silu(up).reshape(E, k, D_FF)
        Eout = jnp.einsum('ekf,efh->ekh', act, W_down) + b_down[:, None, :]
        weighted = G_ek[..., None] * Eout
        y = jnp.zeros((bs, H), dtype=x.dtype).at[idx_ek.reshape(-1)].add(weighted.reshape(-1, H))
        return y.reshape(B, S, H)
    h = _L0_tok_ref(x, L0_tok_w, L0_tok_b, 16)
    h = jnp.concatenate([h, txt], axis=1)
    h = h + _L0_attn_ref(_layernorm(h, axis=-1), L0_attn_Wq, L0_attn_bq, L0_attn_Wk, L0_attn_bk, L0_attn_Wv, L0_attn_bv, L0_attn_Wo, L0_attn_bo)
    h = h + _L0_ffn_ref(_layernorm(h, axis=-1), L0_ffn_Wr, L0_ffn_br, L0_ffn_W1, L0_ffn_b1, L0_ffn_W2, L0_ffn_b2)
    h = h + _L1_attn_ref(_layernorm(h, axis=-1), L1_attn_ln_g, L1_attn_ln_b, L1_attn_w_in, L1_attn_b_in, L1_attn_w_out, L1_attn_b_out)
    h = h + _L1_ffn_ref(_layernorm(h, axis=-1), L1_ffn_W_router, L1_ffn_b_router, L1_ffn_W_up, L1_ffn_b_up, L1_ffn_W_down, L1_ffn_b_down)
    return h

_drawn_inputs = setup_inputs


def setup_inputs(seed=0):
    import zlib

    import numpy as np

    out = dict(_drawn_inputs(seed))
    spreads = {'L0_ffn_br': (0.0, 0.1),
     'L0_ffn_b1': (0.0, 0.1),
     'L0_ffn_b2': (0.0, 0.1),
     'L1_attn_ln_g': (1.0, 0.2),
     'L1_attn_ln_b': (0.0, 0.1),
     'L1_attn_b_in': (0.0, 0.8),
     'L1_attn_b_out': (0.0, 0.1),
     'L1_ffn_b_router': (0.0, 0.8),
     'L1_ffn_b_up': (0.0, 2.0),
     'L1_ffn_b_down': (0.0, 0.8)}
    factors = {'L0_attn_bq': 5.227, 'L0_attn_bk': 20.929, 'L1_attn_w_in': 5.117, 'L1_attn_w_out': 4.272}
    for name, (base, spread) in spreads.items():
        noise = np.random.default_rng([zlib.crc32(name.encode()), seed]).standard_normal(out[name].shape)
        drawn = base * np.exp(spread * noise) if base else spread * noise
        out[name] = jnp.asarray(drawn.astype(out[name].dtype))
    for name, factor in factors.items():
        out[name] = (out[name] * factor).astype(out[name].dtype)
    return out
```

```python
from contextlib import ExitStack

import numpy as np

import concourse.bass as bass
from concourse import mybir

F32 = mybir.dt.float32
BF16 = mybir.dt.bfloat16
I32 = mybir.dt.int32
U32 = mybir.dt.uint32
ALU = mybir.AluOpType
ACT = mybir.ActivationFunctionType
AX_X = mybir.AxisListType.X

P = 128
B = 64
E = 128
NPATCH = 196
NTEXT = 128
L = NPATCH + NTEXT
TOK = B * L
NT = TOK // P
KP = 768 // P
NH = 8
HD = E // NH
EPS = 1e-5


def wait_for(eng, sem, count):
    if isinstance(count, int) and count <= 0:
        return
    eng.wait_ge(sem, count)


class Scope:

    def __init__(self, nc, name):
        self.nc, self.name, self.stack = nc, name, ExitStack()

    def __enter__(self):
        self.stack.__enter__()
        return self

    def __exit__(self, *error):
        return self.stack.__exit__(*error)

    def sb(self, name, shape, dt=F32):
        return self.stack.enter_context(self.nc.sbuf_tensor(f"{self.name}_{name}", shape, dt))

    def ps(self, name, shape, dt=F32):
        return self.stack.enter_context(self.nc.psum_tensor(f"{self.name}_{name}", shape, dt))

    def sem(self, name):
        return self.stack.enter_context(self.nc.semaphore(f"{self.name}_{name}"))

    def block(self):
        return self.stack.enter_context(self.nc.Block())


def tile_of(h, j):
    return h[:, bass.ds(j * E, E)]


def clear_semaphores(nc):
    free = sorted(nc.released_uncleared_semaphores)
    with nc.Block() as block:
        @block.gpsimd
        def _(pool):
            pool.sem_clear(range(free[0], free[-1] + 1))


def make_identity(nc, ident):
    with Scope(nc, "id") as s:
        zeroed, done = s.sem("zeroed"), s.sem("done")
        block = s.block()

        @block.gpsimd
        def _(pool):
            pool.memset(ident[:, :], 0.0).then_inc(zeroed, 1)
            pool.wait_ge(zeroed, 1)
            pool.affine_select(out=ident[:, :], in_=ident[:, :], compare_op=ALU.not_equal, fill=1.0, base=0,
                               pattern=[[-1, P]], channel_multiplier=1).then_inc(done, 1)
            pool.wait_ge(done, 1)


def finish_statistics(nc, name, stats, mean, rstd, scale2=None):
    with Scope(nc, name) as s:
        t1, t2, v = s.sb("t1", [P, NT]), s.sb("t2", [P, NT]), s.sb("v", [P, NT])
        sd, var = s.sb("sd", [P, NT]), s.sb("var", [P, NT])
        step, root = s.sem("step"), s.sem("root")
        block = s.block()
        st = stats[:, :].rearrange("p (t k) -> p t k", k=6)

        @block.scalar
        def _(act):
            act.wait_ge(step, 7)
            act.activation(sd[:, :], v[:, :], ACT.Sqrt).then_inc(root, 1)
            if scale2 is not None:
                act.wait_ge(step, 15)
                act.activation(sd[:, :], v[:, :], ACT.Sqrt).then_inc(root, 1)

        @block.vector
        def _(dve):
            count = [0]

            def link(ins):
                count[0] += 1
                ins.then_inc(step, 1)
                dve.wait_ge(step, count[0])

            def invert(out, n):
                dve.wait_ge(root, n)
                link(dve.reciprocal(out[:, :], sd[:, :]))
                link(dve.tensor_tensor(t1[:, :], out[:, :], out[:, :], ALU.mult))
                link(dve.tensor_tensor(t1[:, :], t1[:, :], v[:, :], ALU.mult))
                link(dve.tensor_scalar(t1[:, :], t1[:, :], -0.5, 1.5, ALU.mult, ALU.add))
                link(dve.tensor_tensor(out[:, :], out[:, :], t1[:, :], ALU.mult))

            link(dve.tensor_tensor(t1[:, :], st[:, :, 1], st[:, :, 4], ALU.add))
            link(dve.tensor_scalar(mean[:, :], t1[:, :], 0.5, None, ALU.mult))
            link(dve.tensor_tensor(t2[:, :], st[:, :, 1], st[:, :, 4], ALU.subtract))
            link(dve.scalar_tensor_tensor(out=t1[:, :], in0=t2[:, :], scalar=0.25, in1=t2[:, :],
                                          op0=ALU.mult, op1=ALU.mult))
            link(dve.tensor_tensor(t2[:, :], st[:, :, 2], st[:, :, 5], ALU.add))
            link(dve.scalar_tensor_tensor(out=var[:, :], in0=t2[:, :], scalar=1.0 / E, in1=t1[:, :],
                                          op0=ALU.mult, op1=ALU.add))
            link(dve.tensor_scalar(v[:, :], var[:, :], EPS, None, ALU.add))
            invert(rstd, 1)
            if scale2 is not None:
                link(dve.tensor_tensor(t2[:, :], rstd[:, :], rstd[:, :], ALU.mult))
                link(dve.tensor_tensor(t2[:, :], t2[:, :], var[:, :], ALU.mult))
                link(dve.tensor_scalar(v[:, :], t2[:, :], EPS, None, ALU.add))
                invert(scale2, 2)
                link(dve.tensor_tensor(scale2[:, :], scale2[:, :], rstd[:, :], ALU.mult))


def embed_tokens(nc, patches, text, w, bias, h, stats):
    U = 7
    NPT = NPATCH * B // P
    assert NPT % U == 0
    with Scope(nc, "tok") as s:
        x = [s.sb(f"x{u}", [P, KP * P]) for u in range(U)]
        w_sb = s.sb("w", [P, KP * E])
        b_sb = s.sb("b", [P, E])
        acc = s.ps("acc", [P, U, 512])
        loaded = [s.sem(f"loaded{u}") for u in range(U)]
        weights, text_in = s.sem("weights"), s.sem("text_in")
        product, added, counted = s.sem("product"), s.sem("added"), s.sem("counted")
        block = s.block()

        @block.sync
        def _(sp):
            sp.dma_start(w_sb[:, :], w).then_inc(weights, 16)
            sp.dma_start(b_sb[:, :], bias).then_inc(weights, 16)
            for u in range(U):
                sp.dma_start(x[u][:, :], patches[u * P:(u + 1) * P, :]).then_inc(loaded[u], 16)
            with sp.Fori(1, NPT // U) as i:
                for u in range(U):
                    sp.wait_ge(product, (i - 1) * U + u + 1)
                    sp.dma_start(x[u][:, :], patches[bass.ds((i * U + u) * P, P), :]).then_inc(loaded[u], 16)

        @block.scalar
        def _(act):
            q = (NT - NPT) // 4
            for k in range(4):
                act.dma_start(h[:, (NPT + k * q) * E:(NPT + (k + 1) * q) * E].rearrange("p (t e) -> p t e", e=E),
                               text[k * q:(k + 1) * q, :, :].rearrange("t p e -> p t e")).then_inc(text_in, 16)
            act.wait_ge(text_in, 64)

        @block.tensor
        def _(pe):
            pe.wait_ge(weights, 32)

            def products(i, u):
                pe.wait_ge(loaded[u], (i + 1) * 16)
                wait_for(pe, added, (i - 1) * U + u + 1)
                for k in range(KP):
                    last = pe.matmul(acc[:, u, 0:E], x[u][:, k * P:(k + 1) * P], w_sb[:, k * E:(k + 1) * E],
                                     start=(k == 0), stop=(k == KP - 1))
                last.then_inc(product, 1)

            for u in range(U):
                products(0, u)
            with pe.Fori(1, NPT // U) as i:
                for u in range(U):
                    products(i, u)

        @block.vector
        def _(dve):
            st = stats[:, :].rearrange("p (t k) -> p t k", k=6)
            with dve.Fori(0, NPT // U) as i:
                for u in range(U):
                    dve.wait_ge(product, i * U + u + 1)
                    dve.tensor_tensor(tile_of(h, i * U + u), acc[:, u, 0:E], b_sb[:, :], ALU.add)\
                       .then_inc(added, 1)
                    if u >= 1:
                        dve.wait_ge(added, i * U + u)
                        dve.bn_stats(stats[:, bass.ds((i * U + u - 1) * 6, 6)], tile_of(h, i * U + u - 1))\
                           .then_inc(counted, 1)
                dve.wait_ge(added, i * U + U)
                dve.bn_stats(stats[:, bass.ds((i * U + U - 1) * 6, 6)], tile_of(h, i * U + U - 1))\
                   .then_inc(counted, 1)
            dve.wait_ge(text_in, 64)
            with dve.Fori(NPT // 8, NT // 8) as i:
                for u in range(8):
                    dve.bn_stats(stats[:, bass.ds((i * 8 + 2 + u) * 6, 6)], tile_of(h, i * 8 + 2 + u))\
                       .then_inc(counted, 1)


def image_attention(nc, c, h, stats, mean, rstd):
    G = NT // 2
    N = 2 * P
    NP = 4
    with Scope(nc, "at0") as s:
        wq, wqr, wk, wkr, wv, wo = [s.sb(n, [P, E]) for n in ("wq", "wqr", "wk", "wkr", "wv", "wo")]
        cols = s.sb("cols", [P, 5 + NH])
        rope = s.sb("rope", [P, 4 * B])
        bo = s.sb("bo", [P, N])
        sel = s.sb("sel", [P, 2 * P])
        xn = s.sb("xn", [P, N])
        xt = s.sb("xt", [P, NP, 2, B])
        q1, q2, k1, k2 = [s.sb(n, [P, N]) for n in ("q1", "q2", "k1", "k2")]
        q, k = s.sb("q", [P, N]), s.sb("k", [P, N])
        qm = s.sb("qm", [P, NP, NH, B])
        vb = s.sb("vb", [P, NP, 2, P])
        mx = s.sb("mx", [P, NP, 4])
        pr = s.sb("pr", [P, NP, 4, B])
        pt = s.sb("pt", [P, NP, 2, P])
        rc = s.sb("rc", [P, NP, 2, 2])
        on = s.sb("on", [P, NP, E])
        ot = s.sb("ot", [P, N])

        bank = s.ps("bank", [P, 8, 512])
        S = [bank[:, n, :].rearrange("p (i t) -> p i t", t=P) for n in range(NP)]
        PT = bank[:, 0:2, :].rearrange("p a (b c d) -> p a b c d", b=2, c=2)
        AV = bank[:, 2:4, :].rearrange("p a (b c d) -> p a b c d", b=2, c=2)
        Q, QR, K, KR = bank[:, 4, 0:N], bank[:, 4, N:2 * N], bank[:, 5, 0:N], bank[:, 5, N:2 * N]
        V = bank[:, 6, :].rearrange("p (n e) -> p n e", n=NP)
        XT, OT = bank[:, 7, 0:N], bank[:, 7, N:2 * N]
        Y = bank[:, 0, 0:N]

        const_in, cleared, ones_set = s.sem("const_in"), s.sem("cleared"), s.sem("ones_set")
        normed, xt_ps, xt_in = s.sem("normed"), s.sem("xt_ps"), s.sem("xt_in")
        qk_ps, v_ps, roped, qk_in, masked = s.sem("qk_ps"), s.sem("v_ps"), s.sem("roped"), s.sem("qk_in"), s.sem("masked")
        bias_added, v_in = s.sem("bias_added"), s.sem("v_in")
        scored, maxed, shifted, raised = s.sem("scored"), s.sem("maxed"), s.sem("shifted"), s.sem("raised")
        pt_ps, pt_in, av_ps, inverted, on_in = s.sem("pt_ps"), s.sem("pt_in"), s.sem("av_ps"), s.sem("inverted"), s.sem("on_in")
        ot_ps, ot_in, y_ps, h_in, counted = s.sem("ot_ps"), s.sem("ot_in"), s.sem("y_ps"), s.sem("h_in"), s.sem("counted")
        block = s.block()

        def run(eng, front, back):
            front(0)
            back(0, front)
            with eng.Fori(1, G - 1) as g:
                back(g, front)
            back(G - 1, None)

        @block.sync
        def _(sp):
            for n, t in enumerate((wq, wqr, wk, wkr, wv, wo)):
                sp.dma_start(t[:, :], c["at0_w"][n, :, :]).then_inc(const_in, 16)
            sp.dma_start(cols[:, :], c["at0_cols"]).then_inc(const_in, 16)
            sp.dma_start(rope[:, :], c["rope"]).then_inc(const_in, 16)
            sp.dma_start(sel[:, :], c["sel"]).then_inc(const_in, 16)
            for n in range(2):
                sp.dma_start(bo[:, n * E:(n + 1) * E], c["at0_bo"]).then_inc(const_in, 16)
            sp.wait_ge(const_in, 16 * 11)

        @block.gpsimd
        def _(pool):
            pool.memset(vb[:, :, :, :], 0.0).then_inc(cleared, 1)
            pool.memset(on[:, :, :], 0.0).then_inc(cleared, 1)
            pool.wait_ge(cleared, 2)
            for half in range(2):
                pool.memset(vb[64 * half:64 * half + 64, :, :, 64 * half + 32:64 * half + 33], 1.0)\
                    .then_inc(ones_set, 1)
                pool.wait_ge(ones_set, half + 1)
            pool.wait_ge(const_in, 16 * 11)

            def front(g):
                pool.wait_ge(normed, 2 * (g + 1))
                pool.tensor_tensor(h[:, bass.ds(g * N, N)], h[:, bass.ds(g * N, N)], bo[:, :], ALU.add)\
                    .then_inc(bias_added, 1)
                wait_for(pool, masked, NH * g)
                pool.wait_ge(roped, 4 * g + 2)
                pool.tensor_tensor(q[:, :], q1[:, :], q2[:, :], ALU.add).then_inc(qk_in, 1)
                wait_for(pool, scored, NP * g)
                pool.wait_ge(roped, 4 * g + 4)
                pool.tensor_tensor(k[:, :], k1[:, :], k2[:, :], ALU.add).then_inc(qk_in, 1)

            def back(g, then):
                if then:
                    then(g + 1)

            run(pool, front, back)

        @block.tensor
        def _(pe):
            pe.wait_ge(const_in, 16 * 11)

            def front(g):
                pe.wait_ge(normed, 2 * (g + 1))
                wait_for(pe, xt_in, g)
                for t in range(2):
                    last = pe.transpose(XT[:, t * P:(t + 1) * P], xn[:, t * P:(t + 1) * P], c["ident"][:, :])
                last.then_inc(xt_ps, 1)
                pe.wait_ge(xt_in, g + 1)
                wait_for(pe, roped, 4 * g)
                for ps, wt in ((Q, wq), (QR, wqr), (K, wk), (KR, wkr)):
                    pe.matmul(ps, wt[:, :], xt[:, :, 0, :], start=True, stop=True).then_inc(qk_ps, 1)
                wait_for(pe, v_in, 2 * g)
                for n in range(NP):
                    last = pe.matmul(V[:, n, :], xt[:, n, :, :], wv[:, :], start=True, stop=True)
                last.then_inc(v_ps, 1)

            def back(g, then):
                pe.wait_ge(masked, NH * (g + 1))
                pe.wait_ge(qk_in, 2 * (g + 1))
                wait_for(pe, h_in, g)
                for n in range(NP):
                    if n == 2:
                        wait_for(pe, on_in, 2 * g)
                    for i in range(4):
                        last = pe.matmul(S[n][:, i, :], qm[:, n, 2 * i:2 * i + 2, :],
                                         k[:, (n // 2) * P:(n // 2) * P + P], start=True, stop=True)
                    last.then_inc(scored, 1)
                if then:
                    then(g + 1)
                pe.wait_ge(raised, NP * (g + 1))
                pe.wait_ge(shifted, NP * (g + 1))
                for n in range(NP):
                    for i in range(2):
                        last = pe.transpose(PT[:, n // 2, n % 2, i, :], pr[:, n, 2 * i:2 * i + 2, :],
                                            c["ident"][:, :])
                    if n % 2:
                        last.then_inc(pt_ps, 1)
                pe.wait_ge(v_in, 2 * (g + 1))
                for n in range(NP):
                    if n % 2 == 0:
                        pe.wait_ge(pt_in, 2 * g + n // 2 + 1)
                    for i in range(2):
                        last = pe.matmul(AV[:, n // 2, n % 2, i, :], pt[:, n, i, :], vb[:, n, i, :],
                                         start=True, stop=True)
                last.then_inc(av_ps, 1)
                pe.wait_ge(on_in, 2 * (g + 1))
                wait_for(pe, ot_in, g)
                for t in range(2):
                    for pp in range(2):
                        last = pe.matmul(OT[:, t * P:(t + 1) * P], on[:, 2 * t + pp, :],
                                         sel[:, pp * P:(pp + 1) * P], start=(pp == 0), stop=(pp == 1))
                last.then_inc(ot_ps, 1)
                pe.wait_ge(ot_in, g + 1)
                for t in range(2):
                    last = pe.matmul(Y[:, t * P:(t + 1) * P], ot[:, t * P:(t + 1) * P], wo[:, :],
                                     start=True, stop=True)
                last.then_inc(y_ps, 1)

            run(pe, front, back)

        @block.scalar
        def _(act):
            act.wait_ge(const_in, 16 * 11)
            act.wait_ge(ones_set, 2)

            def evacuate_v(g):
                act.wait_ge(v_ps, g + 1)
                wait_for(act, av_ps, g)
                for half in range(2):
                    rows = slice(64 * half, 64 * half + 64)
                    src = V[rows, :, :].rearrange("p n (i c) -> p (n i) c", c=64)[:, :, 32 * half:32 * half + 32]
                    dst = vb[rows, :, :, :].rearrange("p n i c -> p (n i) c")[:, :, 64 * half:64 * half + 32]
                    act.activation(dst, src, ACT.Copy).then_inc(v_in, 1)

            def front(g):
                act.wait_ge(xt_ps, g + 1)
                wait_for(act, v_ps, g)
                act.activation(xt[:, :, :, :], XT.rearrange("p (n b) -> p n b", b=B).unsqueeze(2)
                               .broadcast_to([P, NP, 2, B]), ACT.Copy).then_inc(xt_in, 1)

            def back(g, then):
                if then:
                    then(g + 1)
                for n in range(NP):
                    act.wait_ge(shifted, NP * g + n + 1)
                    act.activation(pr[:, n, :, :], pr[:, n, :, :], ACT.Exp).then_inc(raised, 1)
                wait_for(act, av_ps, g)
                for n in range(2):
                    act.wait_ge(pt_ps, 2 * g + n + 1)
                    act.activation(pt[:, 2 * n:2 * n + 2, :, :], PT[:, n, :, :, :], ACT.Copy).then_inc(pt_in, 1)
                if then:
                    act.wait_ge(av_ps, g + 1)
                    evacuate_v(g + 1)
                act.wait_ge(ot_ps, g + 1)
                wait_for(act, y_ps, g)
                act.activation(ot[:, :], OT, ACT.Identity, bias=cols[:, 4:5]).then_inc(ot_in, 1)

            front(0)
            evacuate_v(0)
            back(0, front)
            with act.Fori(1, G - 1) as g:
                back(g, front)
            back(G - 1, None)

        @block.vector
        def _(dve):
            dve.wait_ge(const_in, 16 * 11)
            dve.wait_ge(cleared, 2)
            tab = rope[:, :].rearrange("p (k b) -> p k b", k=4)

            def normalise(g):
                wait_for(dve, xt_ps, g)
                for t in range(2):
                    j = 2 * g + t
                    dve.tensor_scalar(xn[:, t * E:(t + 1) * E], tile_of(h, j), mean[:, bass.ds(j, 1)],
                                      rstd[:, bass.ds(j, 1)], ALU.subtract, ALU.mult).then_inc(normed, 1)

            def rotate(g):
                wait_for(dve, qk_in, 2 * g)
                for n, (ps, to) in enumerate(((Q, q1), (QR, q2), (K, k1), (KR, k2))):
                    dve.wait_ge(qk_ps, 4 * g + (2 if n < 2 else 4))
                    dve.scalar_tensor_tensor(out=to[:, :].rearrange("p (n b) -> p n b", b=B),
                                             in0=ps.rearrange("p (n b) -> p n b", b=B), scalar=cols[:, n:n + 1],
                                             in1=tab[:, n:n + 1, :].broadcast_to([P, NP, B]),
                                             op0=ALU.add, op1=ALU.mult).then_inc(roped, 1)
                dve.wait_ge(qk_in, 2 * g + 1)
                wait_for(dve, scored, NP * g)
                for n in range(NH):
                    dve.tensor_scalar(qm[:, :, n, :], q[:, :].rearrange("p (n b) -> p n b", b=B), cols[:, 5 + n:6 + n], None, ALU.mult)\
                       .then_inc(masked, 1)

            def front(g):
                normalise(g)
                rotate(g)

            def back(g, then):
                if then:
                    normalise(g + 1)
                wait_for(dve, pt_ps, 2 * g)
                for n in range(NP):
                    own = S[n][:, :, (n % 2) * B:(n % 2) * B + B]
                    dve.wait_ge(scored, NP * g + n + 1)
                    dve.tensor_reduce(mx[:, n, :], own, AX_X, ALU.max).then_inc(maxed, 1)
                for n in range(NP):
                    own = S[n][:, :, (n % 2) * B:(n % 2) * B + B]
                    dve.wait_ge(maxed, NP * g + n + 1)
                    dve.tensor_tensor(pr[:, n, :, :], own, mx[:, n, :].unsqueeze(2).broadcast_to([P, 4, B]),
                                      ALU.subtract).then_inc(shifted, 1)
                if then:
                    rotate(g + 1)
                dve.wait_ge(av_ps, g + 1)
                dve.reciprocal(rc[:, :, :, :].rearrange("p n i k -> p (n i) k"),
                               AV.rearrange("p a b c (k d) -> p (a b c) k d", k=2)[:, :, :, 32])\
                   .then_inc(inverted, 1)
                dve.wait_ge(inverted, g + 1)
                for par in range(2):
                    rows = slice(64 * par, 64 * par + 64)
                    src = AV.rearrange("p a b c (k d) -> p (a b c) k d", k=2)[rows, :, :, HD * par:HD * par + HD]
                    dst = on[rows, :, :].rearrange("p n (i k d) -> p (n i) k d", i=2, k=2)[:, :, :, HD * par:HD * par + HD]
                    inv = rc[rows, :, :, :].rearrange("p n i k -> p (n i) k").unsqueeze(3).broadcast_to([64, 8, 2, HD])
                    dve.tensor_tensor(dst, src, inv, ALU.mult).then_inc(on_in, 1)
                dve.wait_ge(y_ps, g + 1)
                dve.wait_ge(bias_added, g + 1)
                dve.tensor_tensor(h[:, bass.ds(g * N, N)], Y, h[:, bass.ds(g * N, N)], ALU.add).then_inc(h_in, 1)
                dve.wait_ge(h_in, g + 1)
                for t in range(2):
                    dve.bn_stats(stats[:, bass.ds((2 * g + t) * 6, 6)], tile_of(h, 2 * g + t)).then_inc(counted, 1)

            run(dve, front, back)
def token_logits(nc, name, c, h, mean, rstd, w, bias, ne, logits, rows_out=None, h_out=None):
    W = 3
    N = W * P
    NG = NT // W
    with Scope(nc, name) as s:
        w_sb, b_sb = s.sb("w", [P, P]), s.sb("b", [P, ne])
        xn, xt = [s.sb(f"xn{u}", [P, N]) for u in range(2)], [s.sb(f"xt{u}", [P, N]) for u in range(2)]
        xps, lps = [s.ps(f"xps{u}", [P, 512]) for u in range(2)], [s.ps(f"lps{u}", [P, 512]) for u in range(2)]
        const_in, h_stored = s.sem("const_in"), s.sem("h_stored")
        stored = [s.sem(f"stored{u}") for u in range(2)]
        normed, turned, xt_in, product, added = (s.sem(n) for n in ("normed", "turned", "xt_in", "product", "added"))
        block = s.block()

        def run(eng, step):
            for u in range(2):
                step(u, u)
            with eng.Fori(1, NG // 2) as i:
                for u in range(2):
                    step(2 * i + u, u, i)

        @block.sync
        def _(sp):
            sp.dma_start(w_sb[:, :], w).then_inc(const_in, 16)
            sp.dma_start(b_sb[:, :], bias).then_inc(const_in, 16)
            if h_out is not None:
                for k in range(6):
                    q = NT // 6
                    sp.dma_start(h_out[k * q * P:(k + 1) * q * P, :].rearrange("(t p) e -> p t e", p=P),
                                 h[:, k * q * E:(k + 1) * q * E].rearrange("p (t e) -> p t e", e=E))\
                      .then_inc(h_stored, 16)
            if rows_out is not None:
                def step(g, u, i=0):
                    sp.wait_ge(normed, W * (g + 1))
                    dst = rows_out[bass.ds(g * N, N), 0:E].rearrange("(t p) e -> p t e", p=P)
                    sp.dma_start(dst, xn[u][:, :].rearrange("p (t e) -> p t e", e=E)).then_inc(stored[u], 16)
                run(sp, step)
                for u in range(2):
                    sp.wait_ge(stored[u], 16 * (NG // 2))
            if h_out is not None:
                sp.wait_ge(h_stored, 16 * 6)

        @block.vector
        def _(dve):
            dve.wait_ge(const_in, 32)

            def norm(g, u, i=0):
                wait_for(dve, turned, g - 1)
                if rows_out is not None:
                    wait_for(dve, stored[u], 16 * i)
                for t in range(W):
                    j = W * g + t
                    dve.tensor_scalar(xn[u][:, t * E:(t + 1) * E], tile_of(h, j), mean[:, bass.ds(j, 1)],
                                      rstd[:, bass.ds(j, 1)], ALU.subtract, ALU.mult).then_inc(normed, 1)

            def add(g, u):
                dve.wait_ge(product, g + 1)
                lg = logits[:, bass.ds(g * W * ne, W * ne)].rearrange("p (t n) -> p t n", n=ne)
                dve.tensor_tensor(lg, lps[u][:, 0:N].rearrange("p (t n) -> p t n", n=P)[:, :, 0:ne],
                                  b_sb[:, :].unsqueeze(1).broadcast_to([P, W, ne]), ALU.add).then_inc(added, 1)

            norm(0, 0)
            norm(1, 1)
            with dve.Fori(1, NG // 2) as i:
                for u in range(2):
                    norm(2 * i + u, u, i)
                    add(2 * i + u - 2, u)
            add(NG - 2, 0)
            add(NG - 1, 1)

        @block.tensor
        def _(pe):
            pe.wait_ge(const_in, 32)

            def turn(g, u, i=0):
                pe.wait_ge(normed, W * (g + 1))
                wait_for(pe, xt_in, g - 1)
                for t in range(W):
                    last = pe.transpose(xps[u][:, t * P:(t + 1) * P], xn[u][:, t * P:(t + 1) * P], c["ident"][:, :])
                last.then_inc(turned, 1)

            def multiply(g, u):
                pe.wait_ge(xt_in, g + 1)
                wait_for(pe, added, g - 1)
                for t in range(W):
                    last = pe.matmul(lps[u][:, t * P:(t + 1) * P], xt[u][:, t * P:(t + 1) * P], w_sb[:, :],
                                     start=True, stop=True)
                last.then_inc(product, 1)

            turn(0, 0)
            turn(1, 1)
            multiply(0, 0)
            turn(2, 0)
            multiply(1, 1)
            with pe.Fori(1, NG // 2 - 1) as i:
                for u in range(2):
                    turn(2 * i + u + 1, 1 - u)
                    multiply(2 * i + u, u)
            turn(NG - 1, 1)
            multiply(NG - 2, 0)
            multiply(NG - 1, 1)

        @block.scalar
        def _(act):
            def step(g, u, i=0):
                act.wait_ge(turned, g + 1)
                wait_for(act, product, g - 1)
                act.activation(xt[u][:, :], xps[u][:, 0:N], ACT.Copy).then_inc(xt_in, 1)
            run(act, step)


NE0 = 8
FT = 256
NFT = TOK // FT + NE0 - 1
H0 = 512
WB0 = H0 + H0 + 4 + E


def route_top1(nc, c, logits, dest, ratio, tile_expert, room):
    N = NT * NE0
    with Scope(nc, "rt0") as s:
        mx, sm = s.sb("mx", [P, NT]), s.sb("sm", [P, NT])
        key, hot, ex, cum, tot = (room[:, n * N:(n + 1) * N] for n in range(5))
        hot16 = s.sb("hot16", [P, N], BF16)
        tri, ones = s.sb("tri", [P, P], BF16), s.sb("ones", [P, P], BF16)
        small = s.sb("small", [P, 8, NE0])
        zero = s.sb("zero", [P, N])
        cnt = s.sb("cnt", [P, NE0], I32)
        tid, le = s.sb("tid", [P, NFT]), s.sb("le", [P, NFT, NE0 - 1])
        tef = s.sb("tef", [P, NFT])
        ranks, totals = s.ps("ranks", [P, 3, 512]), s.ps("totals", [P, 3, 512])
        const_in, consts, step, raised, counted = (s.sem(n) for n in ("const_in", "consts", "step", "raised", "counted"))
        block = s.block()
        by_te = lambda a: a[:, :].rearrange("p (t e) -> p t e", e=NE0)
        by_et = lambda a: a[:, :].rearrange("p (e t) -> p e t", t=NT)

        @block.sync
        def _(sp):
            sp.dma_start(small[:, 0, :], c["falling"]).then_inc(const_in, 16)

        @block.gpsimd
        def _(pool):
            pool.memset(tri[:, :], 1.0).then_inc(consts, 1)
            pool.memset(ones[:, :], 1.0).then_inc(consts, 1)
            pool.wait_ge(consts, 2)
            pool.affine_select(out=tri[:, :], in_=tri[:, :], compare_op=ALU.is_gt, fill=0.0, base=0,
                               pattern=[[1, P]], channel_multiplier=-1).then_inc(consts, 1)
            pool.iota(tid[:, :], pattern=[[1, NFT]], base=0, channel_multiplier=0,
                      allow_small_or_imprecise_dtypes=True).then_inc(consts, 1)

        @block.tensor
        def _(pe):
            pe.wait_ge(consts, 4)
            pe.wait_ge(step, 6)
            third = N // 3
            for n in range(3):
                pe.matmul(ranks[:, n, 0:third], tri[:, :], hot16[:, n * third:(n + 1) * third], start=True, stop=True)
                last = pe.matmul(totals[:, n, 0:third], ones[:, :], hot16[:, n * third:(n + 1) * third],
                                 start=True, stop=True)
            last.then_inc(counted, 1)

        @block.scalar
        def _(act):
            act.wait_ge(step, 7)
            act.activation(ex[:, :], ex[:, :], ACT.Exp).then_inc(raised, 1)

        @block.vector
        def _(dve):
            n = [0]

            def link(ins):
                n[0] += 1
                ins.then_inc(step, 1)
                dve.wait_ge(step, n[0])

            dve.wait_ge(const_in, 16)
            mx_b = mx[:, :].unsqueeze(2).broadcast_to([P, NT, NE0])
            link(dve.tensor_reduce(mx[:, :], by_te(logits), AX_X, ALU.max))
            link(dve.tensor_tensor(by_te(key), by_te(logits), mx_b, ALU.is_ge))
            link(dve.tensor_tensor(by_te(key), by_te(key), small[:, 0:1, :].broadcast_to([P, NT, NE0]), ALU.mult))
            link(dve.tensor_reduce(sm[:, :], by_te(key), AX_X, ALU.max))
            link(dve.tensor_tensor(by_te(hot), by_te(key), sm[:, :].unsqueeze(2).broadcast_to([P, NT, NE0]),
                                   ALU.is_equal))
            link(dve.tensor_copy(hot16[:, :], hot[:, :]))
            link(dve.tensor_tensor(by_te(ex), by_te(logits), mx_b, ALU.subtract))
            link(dve.memset(zero[:, :], 0.0))
            dve.wait_ge(raised, 1)
            link(dve.tensor_reduce(sm[:, :], by_te(ex), AX_X, ALU.add))
            link(dve.reciprocal(mx[:, :], sm[:, :]))
            link(dve.reciprocal(sm[:, :], mx[:, :]))
            link(dve.tensor_tensor(ratio[:, :], mx[:, :], sm[:, :], ALU.mult))
            dve.wait_ge(counted, 1)
            third = NT // 3
            for k in range(3):
                dst = by_et(tot)[:, :, k * third:(k + 1) * third].rearrange("p e t -> p t e")
                link(dve.tensor_copy(dst, totals[:, k, 0:third * NE0].rearrange("p (t e) -> p t e", e=NE0)))
            link(dve.tensor_tensor_scan(cum[:, :], tot[:, :], zero[:, :], 0.0, ALU.add, ALU.add))
            first, ends = small[:, 1, :], by_et(cum)[:, :, NT - 1]
            link(dve.memset(small[:, 1:8, :], 0.0))
            link(dve.tensor_copy(first[:, 1:NE0], ends[:, 0:NE0 - 1]))
            link(dve.tensor_tensor(small[:, 2, :], ends, first, ALU.subtract))
            link(dve.tensor_scalar(cnt[:, :], small[:, 2, :], float(FT - 1), None, ALU.add))
            link(dve.tensor_scalar(cnt[:, :], cnt[:, :], 8, None, ALU.logical_shift_right))
            link(dve.tensor_copy(small[:, 3, :], cnt[:, :]))
            link(dve.tensor_tensor_scan(small[:, 4, :], small[:, 3, :], small[:, 7, :], 0.0, ALU.add, ALU.add))
            link(dve.tensor_tensor(small[:, 5, :], small[:, 4, :], small[:, 3, :], ALU.subtract))
            link(dve.scalar_tensor_tensor(out=small[:, 6, :], in0=small[:, 5, :], scalar=float(FT), in1=first,
                                          op0=ALU.mult, op1=ALU.subtract))
            link(dve.tensor_tensor(cum[:, :], cum[:, :], tot[:, :], ALU.subtract))
            link(dve.tensor_tensor(by_et(cum), by_et(cum), small[:, 6, :].unsqueeze(2).broadcast_to([P, NE0, NT]),
                                   ALU.add))
            for k in range(3):
                part = by_te(key)[:, k * third:(k + 1) * third, :]
                link(dve.tensor_tensor(part, ranks[:, k, 0:third * NE0].rearrange("p (t e) -> p t e", e=NE0),
                                       by_et(cum)[:, :, k * third:(k + 1) * third].rearrange("p e t -> p t e"),
                                       ALU.add))
            link(dve.tensor_tensor(key[:, :], key[:, :], hot[:, :], ALU.mult))
            link(dve.tensor_reduce(sm[:, :], by_te(key), AX_X, ALU.add))
            link(dve.tensor_copy(dest[:, :], sm[:, :]))
            dve.wait_ge(consts, 4)
            link(dve.tensor_tensor(le[:, :, :], tid[:, :].unsqueeze(2).broadcast_to([P, NFT, NE0 - 1]),
                                   small[:, 4:5, 0:NE0 - 1].broadcast_to([P, NFT, NE0 - 1]), ALU.is_ge))
            link(dve.tensor_reduce(tef[:, :], le[:, :, :], AX_X, ALU.add))
            link(dve.tensor_copy(tile_expert[:, :], tef[:, :]))


def scatter_rows(nc, h, mean, rstd, dest, sorted_rows):
    U = 6
    with Scope(nc, "scat") as s:
        xn = [s.sb(f"xn{u}", [P, E]) for u in range(U)]
        at = [s.sb(f"at{u}", [P, 1], U32) for u in range(U)]
        normed, issued = s.sem("normed"), s.sem("issued")
        sent = [s.sem(f"sent{u}") for u in range(U)]
        block = s.block()

        @block.vector
        def _(dve):
            def step(i, u):
                j = i * U + u
                wait_for(dve, sent[u], 16 * i)
                dve.tensor_copy(at[u][:, :], dest[:, bass.ds(j, 1)]).then_inc(normed, 1)
                dve.tensor_scalar(xn[u][:, :], tile_of(h, j), mean[:, bass.ds(j, 1)], rstd[:, bass.ds(j, 1)],
                                  ALU.subtract, ALU.mult).then_inc(normed, 1)
            for u in range(U):
                step(0, u)
            with dve.Fori(1, NT // U) as i:
                for u in range(U):
                    step(i, u)

        @block.gpsimd
        def _(pool):
            with pool.Fori(0, NT // U) as i:
                for u in range(U):
                    pool.wait_ge(normed, 2 * (i * U + u + 1))
                    pool.sem_inc(issued, 1)
                    pool.indirect_dma_start(out=sorted_rows[:, :],
                                            out_offset=bass.IndirectOffsetOnAxis(ap=at[u][:, 0:1], axis=0),
                                            in_=xn[u][:, :], in_offset=None).then_inc(sent[u], 16)
            for u in range(U):
                pool.wait_ge(sent[u], 16 * (NT // U))


def sorted_ffn(nc, c, tile_expert, sorted_rows, sorted_out):
    HC = H0 // P
    with Scope(nc, "ffn0") as s:
        wb = [s.sb(f"wb{u}", [P, WB0]) for u in range(2)]
        x = [s.sb(f"x{u}", [P, 2, E]) for u in range(2)]
        xt = [s.sb(f"xt{u}", [P, FT]) for u in range(2)]
        hid = [s.sb(f"hid{u}", [P, HC, FT]) for u in range(2)]
        y = [s.sb(f"y{u}", [P, 2, E]) for u in range(2)]
        xps = s.ps("xps", [P, 512])
        up = [s.ps(f"up{u}", [P, 2, 512]) for u in range(2)]
        yps = s.ps("yps", [P, 512])
        w_in, x_in, y_out = ([s.sem(f"{n}{u}") for u in range(2)] for n in ("w_in", "x_in", "y_out"))
        turned, xt_in, upped, gelued, downed, y_in = (s.sem(n) for n in ("turned", "xt_in", "upped", "gelued", "downed", "y_in"))
        block = s.block()

        def rows(t):
            return bass.ds(t * FT, FT)

        def run(eng, step):
            step(0, 0, 0)
            step(1, 1, 0)
            with eng.Fori(1, NFT // 2) as i:
                for u in range(2):
                    step(2 * i + u, u, i)
            if NFT % 2:
                step(NFT - 1, 0, NFT // 2)

        @block.sync
        def _(sp):
            def step(t, u, i):
                expert = sp.value_load(tile_expert[0:1, bass.ds(t, 1)], min_val=0, max_val=NE0 - 1)
                wait_for(sp, y_in, t - 1)
                sp.dma_start(wb[u][:, :], c["ffn0_wb"][bass.ds(expert * P, P), :]).then_inc(w_in[u], 16)
                sp.dma_start(x[u][:, :, :], sorted_rows[rows(t), :].rearrange("(p r) e -> p r e", r=2))\
                  .then_inc(x_in[u], 16)
            run(sp, step)

        @block.gpsimd
        def _(pool):
            def step(t, u, i):
                pool.wait_ge(y_in, t + 1)
                pool.dma_start(sorted_out[rows(t), :].rearrange("(p r) e -> p r e", r=2), y[u][:, :, :])\
                    .then_inc(y_out[u], 16)
            run(pool, step)
            pool.wait_ge(y_out[0], 16 * ((NFT + 1) // 2))
            pool.wait_ge(y_out[1], 16 * (NFT // 2))

        @block.tensor
        def _(pe):
            def turn(t, u, i):
                pe.wait_ge(x_in[u], 16 * (i + 1))
                wait_for(pe, xt_in, t)
                for r in range(2):
                    last = pe.transpose(xps[:, r * P:(r + 1) * P], x[u][:, r, :], c["ident"][:, :])
                last.then_inc(turned, 1)

            def widen(t, u, i):
                pe.wait_ge(w_in[u], 16 * (i + 1))
                pe.wait_ge(xt_in, t + 1)
                wait_for(pe, gelued, HC * (t - 1))
                for m in range(HC):
                    pe.matmul(up[u][:, m // 2, (m % 2) * FT:(m % 2) * FT + FT], wb[u][:, m * P:(m + 1) * P],
                              xt[u][:, :], start=True, stop=True).then_inc(upped, 1)

            def narrow(t, u):
                pe.wait_ge(gelued, HC * (t + 1))
                wait_for(pe, y_in, t)
                for r in range(2):
                    for m in range(HC):
                        last = pe.matmul(yps[:, r * E:(r + 1) * E], hid[u][:, m, r * P:(r + 1) * P],
                                         wb[u][:, H0 + m * E:H0 + (m + 1) * E], start=(m == 0), stop=(m == HC - 1))
                last.then_inc(downed, 1)

            turn(0, 0, 0)
            widen(0, 0, 0)
            turn(1, 1, 0)
            widen(1, 1, 0)
            narrow(0, 0)
            with pe.Fori(1, NFT // 2) as i:
                for u in range(2):
                    turn(2 * i + u, u, i)
                    widen(2 * i + u, u, i)
                    narrow(2 * i + u - 1, 1 - u)
            if NFT % 2:
                turn(NFT - 1, 0, NFT // 2)
                widen(NFT - 1, 0, NFT // 2)
                narrow(NFT - 2, 1)
            narrow(NFT - 1, (NFT - 1) % 2)

        @block.scalar
        def _(act):
            def step(t, u, i):
                wait_for(act, downed, t - 1)
                for m in range(HC):
                    act.wait_ge(upped, HC * t + 2 * (m // 2) + 2)
                    act.activation(hid[u][:, m, :], up[u][:, m // 2, (m % 2) * FT:(m % 2) * FT + FT], ACT.Gelu,
                                   bias=wb[u][:, 2 * H0 + m:2 * H0 + m + 1]).then_inc(gelued, 1)
            run(act, step)

        @block.vector
        def _(dve):
            def evacuate(t, u):
                dve.wait_ge(turned, t + 1)
                wait_for(dve, upped, HC * (t - 1))
                dve.tensor_copy(xt[u][:, :], xps[:, 0:FT]).then_inc(xt_in, 1)

            def finish(t, u, i):
                dve.wait_ge(downed, t + 1)
                wait_for(dve, y_out[u], 16 * i)
                b2 = wb[u][:, 2 * H0 + 4:WB0].unsqueeze(1).broadcast_to([P, 2, E])
                dve.tensor_tensor(y[u][:, :, :], yps[:, 0:2 * E].rearrange("p (r e) -> p r e", e=E), b2, ALU.add)\
                   .then_inc(y_in, 1)

            evacuate(0, 0)
            evacuate(1, 1)
            finish(0, 0, 0)
            evacuate(2, 0)
            finish(1, 1, 0)
            with dve.Fori(1, (NFT - 1) // 2) as i:
                for u in range(2):
                    evacuate(2 * i + u + 1, 1 - u)
                    finish(2 * i + u, u, i)
            for t in range(2 * ((NFT - 1) // 2), NFT):
                if t + 1 < NFT:
                    evacuate(t + 1, (t + 1) % 2)
                finish(t, t % 2, t // 2)


def gather_rows(nc, h, dest, ratio, sorted_out, stats):
    U = 6
    with Scope(nc, "gath") as s:
        y = [s.sb(f"y{u}", [P, E]) for u in range(U)]
        at = [s.sb(f"at{u}", [P, 1], U32) for u in range(U)]
        issued, index_in, added, counted = s.sem("issued"), s.sem("index_in"), s.sem("added"), s.sem("counted")
        got = [s.sem(f"got{u}") for u in range(U)]
        block = s.block()

        @block.gpsimd
        def _(pool):
            def step(i, u):
                pool.wait_ge(index_in, i * U + u + 1)
                pool.sem_inc(issued, 1)
                pool.indirect_dma_start(out=y[u][:, :], out_offset=None, in_=sorted_out[:, :],
                                        in_offset=bass.IndirectOffsetOnAxis(ap=at[u][:, 0:1], axis=0))\
                    .then_inc(got[u], 16)
            with pool.Fori(0, NT // U) as i:
                for u in range(U):
                    step(i, u)

        @block.vector
        def _(dve):
            for u in range(U):
                dve.tensor_copy(at[u][:, :], dest[:, u:u + 1]).then_inc(index_in, 1)

            def step(i, u, more):
                j = i * U + u
                dve.wait_ge(got[u], 16 * (i + 1))
                dve.scalar_tensor_tensor(out=tile_of(h, j), in0=y[u][:, :], scalar=ratio[:, bass.ds(j, 1)],
                                         in1=tile_of(h, j), op0=ALU.mult, op1=ALU.add).then_inc(added, 1)
                dve.wait_ge(added, j + 1)
                if more:
                    dve.tensor_copy(at[u][:, :], dest[:, bass.ds(j + U, 1)]).then_inc(index_in, 1)
                dve.bn_stats(stats[:, bass.ds(j * 6, 6)], tile_of(h, j)).then_inc(counted, 1)

            with dve.Fori(0, NT // U - 1) as i:
                for u in range(U):
                    step(i, u, True)
            for u in range(U):
                step(NT // U - 1, u, False)



def clear_rows(nc, rows):
    n = rows.shape[0] // P
    k = 11
    assert n % k == 0
    with Scope(nc, "clr") as s:
        zero = s.sb("zero", [P, n // k * E])
        cleared, stored = s.sem("cleared"), s.sem("stored")
        block = s.block()

        @block.vector
        def _(dve):
            dve.memset(zero[:, :], 0.0).then_inc(cleared, 1)

        @block.sync
        def _(sp):
            sp.wait_ge(cleared, 1)
            for m in range(k):
                sp.dma_start(rows[m * P * (n // k):(m + 1) * P * (n // k), :].rearrange("(p r) e -> p (r e)", p=P),
                             zero[:, :]).then_inc(stored, 16)
            sp.wait_ge(stored, 16 * k)


WIN, HOP = 20, 10
NW = (L - WIN) // HOP + 1
NB = L // HOP
WP = 32
NTC = B * L + 2 * WP


def turn_rows(nc, c, h, mean, scale, turned_rows, h_keep):
    W = 3
    N = W * P
    NG = NT // W
    with Scope(nc, "turn") as s:
        gb = s.sb("gb", [P, 2])
        xn = [s.sb(f"xn{u}", [P, N]) for u in range(2)]
        xps = [s.ps(f"xps{u}", [P, 512]) for u in range(2)]
        const_in, stored, cleared = s.sem("const_in"), s.sem("stored"), s.sem("cleared")
        normed, turned, placed = s.sem("normed"), s.sem("turned"), s.sem("placed")
        block = s.block()

        def run(eng, step):
            for u in range(2):
                step(u, u)
            with eng.Fori(1, NG // 2) as i:
                for u in range(2):
                    step(2 * i + u, u)

        @block.sync
        def _(sp):
            sp.dma_start(gb[:, :], c["at1_gb"]).then_inc(const_in, 16)
            q = NT // 6
            for k in range(6):
                sp.dma_start(h_keep[k * q * P:(k + 1) * q * P, :].rearrange("(t p) e -> p t e", p=P),
                             h[:, k * q * E:(k + 1) * q * E].rearrange("p (t e) -> p t e", e=E)).then_inc(stored, 16)
            sp.wait_ge(stored, 16 * 6)

        @block.gpsimd
        def _(pool):
            pool.memset(turned_rows[:, B * L:NTC], 0.0).then_inc(cleared, 1)

        @block.vector
        def _(dve):
            def step(g, u):
                wait_for(dve, turned, g - 1)
                for t in range(W):
                    j = W * g + t
                    dve.tensor_scalar(xn[u][:, t * E:(t + 1) * E], tile_of(h, j), mean[:, bass.ds(j, 1)],
                                      scale[:, bass.ds(j, 1)], ALU.subtract, ALU.mult).then_inc(normed, 1)
            run(dve, step)

        @block.tensor
        def _(pe):
            def step(g, u):
                pe.wait_ge(normed, W * (g + 1))
                wait_for(pe, placed, g - 1)
                for t in range(W):
                    last = pe.transpose(xps[u][:, t * P:(t + 1) * P], xn[u][:, t * P:(t + 1) * P], c["ident"][:, :])
                last.then_inc(turned, 1)
            run(pe, step)

        @block.scalar
        def _(act):
            act.wait_ge(const_in, 16)

            def step(g, u):
                act.wait_ge(turned, g + 1)
                by_image = turned_rows[:, 0:B * L].rearrange("p (b l) -> p l b", l=L)
                act.activation(by_image[:, bass.ds(2 * W * g, 2 * W), :],
                               xps[u][:, 0:N].rearrange("p (l b) -> p l b", b=B), ACT.Identity,
                               bias=gb[:, 1:2], scale=gb[:, 0:1]).then_inc(placed, 1)
            run(act, step)


def window_attention(nc, c, turned_rows, window_rows):
    GW = 4
    NGR = NB // GW
    Q8 = NH * HOP
    SB = 11
    KX = HOP * (NB + 7)
    VC = 65
    with Scope(nc, "at1") as s:
        wq, wk, wv, wo = (s.sb(n, [P, E]) for n in ("wq", "wk", "wv", "wo"))
        cols = s.sb("cols", [P, 3 + NH + 4])
        bo = s.sb("bo", [P, E])
        sel = s.sb("sel", [P, GW, P])
        xw = [s.sb(f"xw{u}", [P, NB, WP]) for u in range(2)]
        kx = [s.sb(f"kx{u}", [P, KX]) for u in range(2)]
        qs = s.sb("qs", [P, NB * HOP])
        qm = [s.sb(f"qm{u}", [P, NB, NH, HOP]) for u in range(2)]
        bm = s.sb("bm", [P, NB, 3])
        mx = s.sb("mx", [P, NB, 2])
        pr = [s.sb(f"pr{u}", [P, 2, NB + 1, WP]) for u in range(2)]
        pt = [s.sb(f"pt{u}", [P, 2, 2, 4 * HOP]) for u in range(2)]
        vb = [s.sb(f"vb{u}", [P, 2, GW, VC]) for u in range(2)]
        rc, rm = s.sb("rc", [P, 2, GW]), s.sb("rm", [P, 2, GW, 4])
        om = s.sb("om", [P, GW, E])
        ot = s.sb("ot", [P, P])
        y = [s.sb(f"y{u}", [P, NGR, E]) for u in range(2)]

        bank = s.ps("bank", [P, 8, 512])
        AV = bank[:, 3:5, 0:GW * VC].rearrange("p t (w c) -> p t w c", c=VC)
        V, PT = bank[:, 5, 0:E], bank[:, 5, E:E + 2 * Q8].rearrange("p (a k) -> p a k", a=2)
        OT, Y = bank[:, 6, 0:P], bank[:, 7, 0:E]

        const_in, cleared, primed = s.sem("const_in"), s.sem("cleared"), s.sem("primed")
        spread, qk_ps, k_in, q_in, masked = (s.sem(n) for n in ("spread", "qk_ps", "k_in", "q_in", "masked"))
        scored, blocked, maxed, shifted, raised = (s.sem(n) for n in ("scored", "blocked", "maxed", "shifted", "raised"))
        vt_ps, pt_in, vb_in, av_ps, inverted = (s.sem(n) for n in ("vt_ps", "pt_in", "vb_in", "av_ps", "inverted"))
        rm_in, om_in, ot_ps, ot_in, y_ps, y_in = (s.sem(n) for n in ("rm_in", "om_in", "ot_ps", "ot_in", "y_ps", "y_in"))
        stored = [s.sem(f"stored{u}") for u in range(2)]
        block = s.block()

        banks = [(n, n * SB, min(SB, NB - n * SB)) for n in range(3)]

        def images(eng, one):
            one(0, 0, 0, True, False)
            one(1, 1, 0, False, False)
            with eng.Fori(1, B // 2 - 1) as i:
                for u in range(2):
                    one(2 * i + u, u, i, False, False)
            one(B - 2, 0, B // 2 - 1, False, False)
            one(B - 1, 1, B // 2 - 1, False, True)

        @block.sync
        def _(sp):
            for n, t in enumerate((wq, wk, wv, wo)):
                sp.dma_start(t[:, :], c["at1_w"][n, :, :]).then_inc(const_in, 16)
            sp.dma_start(cols[:, :], c["at1_cols"]).then_inc(const_in, 16)
            sp.dma_start(bo[:, :], c["at1_bo"]).then_inc(const_in, 16)
            sp.dma_start(sel[:, :, :], c["at1_sel"].rearrange("p (w c) -> p w c", w=GW)).then_inc(const_in, 16)

            def store(b, u, i, first, last):
                rows = window_rows[bass.ds(b * NW * WP, NW * WP), :]
                sp.wait_ge(y_in, NGR * (b + 1))
                full = (NGR - 1) * P
                sp.dma_start(rows[0:full, :].rearrange("(n p) e -> p n e", p=P), y[u][:, 0:NGR - 1, :])\
                  .then_inc(stored[u], 16)
                sp.dma_start(rows[full:NW * WP, :], y[u][0:NW * WP - full, NGR - 1, :]).then_inc(stored[u], 16)

            images(sp, store)
            for u in range(2):
                sp.wait_ge(stored[u], 32 * (B // 2))

        @block.gpsimd
        def _(pool):
            def spread_rows(b, u, i, first, last):
                wait_for(pool, y_ps, NGR * (b - 1))
                cols_ = turned_rows[:, bass.ds(b * L, NB * HOP + WP - HOP)]
                src = bass.AP(tensor=cols_.tensor, offset=cols_.offset, ap=[list(cols_.ap[0]), [HOP, NB], [1, WP]])
                pool.tensor_copy(xw[u][:, :, :], src).then_inc(spread, 1)
            images(pool, spread_rows)

        @block.tensor
        def _(pe):
            pe.wait_ge(const_in, 16 * 7)
            pe.wait_ge(primed, 4)

            def project(b):
                wait_for(pe, shifted, 3 * b)
                src = turned_rows[:, bass.ds(b * L, L)]
                pe.matmul(bank[:, 0, 0:L], wk[:, :], src, start=True, stop=True).then_inc(qk_ps, 1)
                pe.matmul(bank[:, 1, 0:L], wq[:, :], src, start=True, stop=True).then_inc(qk_ps, 1)

            def score(b, u):
                pe.wait_ge(masked, NH * (b + 1))
                pe.wait_ge(k_in, b + 1)
                for n, j0, nb in banks:
                    for j in range(j0, j0 + nb):
                        last = pe.matmul(bank[0:Q8, n, 3 * HOP * (j - j0):3 * HOP * (j - j0) + 8 * HOP],
                                         qm[u][:, j, :, :], kx[u][:, HOP * j:HOP * (j + 8)], start=True, stop=True)
                    last.then_inc(scored, 1)

            def turn(b, u, n):
                m = NGR * b + n
                pe.wait_ge(spread, b + 1)
                pe.wait_ge(raised, 3 * (b + 1) if n >= 5 else 3 * b + (1 if n < 2 else 2))
                wait_for(pe, pt_in, m)
                wait_for(pe, vb_in, GW * m)
                pe.matmul(V, xw[u][:, GW * n:GW * (n + 1), :], wv[:, :], start=True, stop=True)
                pe.transpose(PT[:, 0, :], pr[u][0:Q8, 0, GW * n + 1:GW * n + 5, :], c["ident"][0:Q8, 0:Q8])
                pe.transpose(PT[:, 1, :], pr[u][0:Q8, 1, GW * n:GW * n + 4, :], c["ident"][0:Q8, 0:Q8])\
                  .then_inc(vt_ps, 1)

            def attend(b, n):
                m = NGR * b + n
                pe.wait_ge(pt_in, m + 1)
                pe.wait_ge(vb_in, GW * (m + 1))
                wait_for(pe, om_in, 2 * m)
                for t in range(2):
                    last = pe.matmul(AV[0:Q8, t, :, :], pt[n % 2][:, t, :, :], vb[n % 2][:, t, :, :],
                                     start=True, stop=True)
                last.then_inc(av_ps, 1)

            def gather_heads(b, n):
                m = NGR * b + n
                pe.wait_ge(om_in, 2 * (m + 1))
                wait_for(pe, ot_in, m)
                for w in range(GW):
                    last = pe.matmul(OT, om[:, w, :], sel[:, w, :], start=(w == 0), stop=(w == GW - 1))
                last.then_inc(ot_ps, 1)

            def project_out(b, u, n):
                m = NGR * b + n
                pe.wait_ge(ot_in, m + 1)
                wait_for(pe, y_in, m)
                pe.matmul(Y, xw[u][:, GW * n:GW * (n + 1), :], c["ident"][:, :], start=True, stop=False)
                pe.matmul(Y, ot[:, :], wo[:, :], start=False, stop=True).then_inc(y_ps, 1)

            def one(b, u, i, first, last):
                for n in range(NGR):
                    if n == 1 and not last:
                        project(b + 1)
                    if n == 4 and not last:
                        score(b + 1, 1 - u)
                    if n < NGR - 1:
                        turn(b, u, n + 1)
                    elif not last:
                        turn(b + 1, 1 - u, 0)
                    if n:
                        gather_heads(b, n - 1)
                    elif not first:
                        gather_heads(b - 1, NGR - 1)
                    attend(b, n)
                    if n:
                        project_out(b, u, n - 1)
                    elif not first:
                        project_out(b - 1, 1 - u, NGR - 1)

            project(0)
            score(0, 0)
            turn(0, 0, 0)
            images(pe, one)
            gather_heads(B - 1, NGR - 1)
            project_out(B - 1, 1, NGR - 1)

        @block.scalar
        def _(act):
            act.wait_ge(const_in, 16 * 7)
            act.wait_ge(primed, 4)

            def keys(b, u):
                act.wait_ge(qk_ps, 2 * b + 1)
                wait_for(act, scored, 3 * (b - 1))
                act.activation(kx[u][:, HOP:HOP + L], bank[:, 0, 0:L], ACT.Identity, bias=cols[:, 1:2])\
                   .then_inc(k_in, 1)

            def raise_scores(b, u):
                for n, j0, nb in banks:
                    act.wait_ge(shifted, 3 * b + n + 1)
                    act.activation(pr[u][0:Q8, :, j0:j0 + nb, 0:WIN], pr[u][0:Q8, :, j0:j0 + nb, 0:WIN], ACT.Exp)\
                       .then_inc(raised, 1)

            def evacuate(b, n):
                m = NGR * b + n
                act.wait_ge(vt_ps, m + 1)
                wait_for(act, av_ps, m - 1)
                act.activation(pt[n % 2][:, :, :, :].rearrange("p t a k -> p a t k"),
                               PT.rearrange("p a (t k) -> p a t k", t=2), ACT.Copy).then_inc(pt_in, 1)
                for w in range(GW):
                    rows = slice(WP * w, WP * w + WP)
                    act.activation(vb[n % 2][rows, :, w, 0:64], V[rows, :].rearrange("p (t k) -> p t k", t=2),
                                   ACT.Copy).then_inc(vb_in, 1)

            def heads(b, n):
                m = NGR * b + n
                act.wait_ge(ot_ps, m + 1)
                wait_for(act, y_ps, m)
                act.activation(ot[:, :], OT, ACT.Identity, bias=cols[:, 2:3]).then_inc(ot_in, 1)

            def one(b, u, i, first, last):
                for n in range(NGR):
                    if n == 1 and not last:
                        keys(b + 1, 1 - u)
                    if n == 4 and not last:
                        raise_scores(b + 1, 1 - u)
                    if n < NGR - 1:
                        evacuate(b, n + 1)
                    elif not last:
                        evacuate(b + 1, 0)
                    if n:
                        heads(b, n - 1)
                    elif not first:
                        heads(b - 1, NGR - 1)

            keys(0, 0)
            raise_scores(0, 0)
            evacuate(0, 0)
            images(act, one)
            heads(B - 1, NGR - 1)

        @block.vector
        def _(dve):
            for t in (kx[0], kx[1], vb[0], vb[1], om, pr[0], pr[1]):
                flat = t[:, :] if len(t.shape) == 2 else t[:, :, :] if len(t.shape) == 3 else t[:, :, :, :]
                dve.memset(flat, 0.0).then_inc(cleared, 1)
            dve.wait_ge(cleared, 7)
            for u in range(2):
                dve.memset(pr[u][:, 0, NB, 0:WIN], 1.0).then_inc(primed, 1)
                for w in range(GW):
                    ins = dve.memset(vb[u][WP * w:WP * w + WP, :, w, VC - 1:VC], 1.0)
                ins.then_inc(primed, 1)
            dve.wait_ge(const_in, 16 * 7)

            def mask(b, u):
                dve.wait_ge(qk_ps, 2 * b + 2)
                wait_for(dve, masked, NH * b)
                dve.tensor_scalar(qs[:, :], bank[:, 1, 0:NB * HOP], cols[:, 0:1], HD ** -0.5, ALU.add, ALU.mult)\
                   .then_inc(q_in, 1)
                dve.wait_ge(q_in, b + 1)
                wait_for(dve, scored, 3 * (b - 1))
                for n in range(NH):
                    dve.tensor_scalar(qm[u][:, :, n, :], qs[:, :].rearrange("p (j q) -> p j q", q=HOP),
                                      cols[:, 3 + n:4 + n], None, ALU.mult).then_inc(masked, 1)

            def softmax(b, u):
                wait_for(dve, vt_ps, NGR * (b - 1))
                for n, j0, nb in banks:
                    sc = bank[0:Q8, n, 0:3 * HOP * nb].rearrange("p (j k q) -> p j k q", k=3, q=HOP)
                    dve.wait_ge(scored, 3 * b + n + 1)
                    wait_for(dve, maxed, 3 * b + n)
                    dve.tensor_reduce(bm[0:Q8, j0:j0 + nb, :], sc, AX_X, ALU.max).then_inc(blocked, 1)
                    dve.wait_ge(blocked, 3 * b + n + 1)
                    wait_for(dve, shifted, 3 * b + n)
                    dve.tensor_tensor(mx[0:Q8, j0:j0 + nb, :], bm[0:Q8, j0:j0 + nb, 0:2], bm[0:Q8, j0:j0 + nb, 1:3],
                                      ALU.max).then_inc(maxed, 1)
                    dve.wait_ge(maxed, 3 * b + n + 1)
                    base = bank[0:Q8, n, 0:3 * HOP * nb]
                    both = bass.AP(tensor=base.tensor, offset=base.offset,
                                   ap=[list(base.ap[0]), [HOP, 2], [3 * HOP, nb], [1, WIN]])
                    dve.tensor_tensor(pr[u][0:Q8, :, j0:j0 + nb, 0:WIN], both,
                                      mx[0:Q8, j0:j0 + nb, :].rearrange("p j a -> p a j").unsqueeze(3)
                                      .broadcast_to([Q8, 2, nb, WIN]),
                                      ALU.subtract).then_inc(shifted, 1)

            def scale(b, n):
                m = NGR * b + n
                dve.wait_ge(av_ps, m + 1)
                wait_for(dve, rm_in, m)
                dve.reciprocal(rc[0:Q8, :, :], AV[0:Q8, :, :, VC - 1]).then_inc(inverted, 1)
                dve.wait_ge(inverted, m + 1)
                wait_for(dve, om_in, 2 * m)
                gm = cols[0:Q8, 3 + NH:7 + NH].unsqueeze(1).broadcast_to([Q8, 2 * GW, 4])
                dve.tensor_tensor(rm[0:Q8, :, :, :].rearrange("p t w g -> p (t w) g"),
                                  rc[0:Q8, :, :].rearrange("p t w -> p (t w)").unsqueeze(2).broadcast_to([Q8, 2 * GW, 4]),
                                  gm, ALU.mult).then_inc(rm_in, 1)
                dve.wait_ge(rm_in, m + 1)
                for t in range(2):
                    dve.tensor_tensor(om[0:Q8, :, 64 * t:64 * t + 64].rearrange("p w (g d) -> p w g d", g=4),
                                      AV[0:Q8, t, :, 0:64].rearrange("p w (g d) -> p w g d", g=4),
                                      rm[0:Q8, t, :, :].unsqueeze(3).broadcast_to([Q8, GW, 4, HD]),
                                      ALU.mult).then_inc(om_in, 1)

            def finish(b, u, i, n):
                m = NGR * b + n
                dve.wait_ge(y_ps, m + 1)
                if n == 0:
                    wait_for(dve, stored[u], 32 * i)
                dve.tensor_tensor(y[u][:, n, :], Y, bo[:, :], ALU.add).then_inc(y_in, 1)

            def one(b, u, i, first, last):
                for n in range(NGR):
                    if n == 1 and not last:
                        mask(b + 1, 1 - u)
                    if n == 4 and not last:
                        softmax(b + 1, 1 - u)
                    scale(b, n)
                    if n:
                        finish(b, u, i, n - 1)
                    elif not first:
                        finish(b - 1, 1 - u, i - 1 + u, NGR - 1)

            mask(0, 0)
            softmax(0, 0)
            images(dve, one)
            finish(B - 1, 1, B // 2 - 1, NGR - 1)


def combine_windows(nc, h, h_keep, mean, rstd, window_rows, stats):
    T = HOP // 2
    TAIL = NT - T * NB
    with Scope(nc, "comb") as s:
        wa, wb_ = ([s.sb(f"{n}{u}", [P, T * E]) for u in range(2)] for n in ("a", "b"))
        x = [s.sb(f"x{u}", [P, T * E]) for u in range(2)]
        t1 = [s.sb(f"t{u}", [P, T * E]) for u in range(2)]
        h_in = s.sem("h_in")
        a_in, b_in = ([s.sem(f"{n}_in{u}") for u in range(2)] for n in ("a", "b"))
        summed, normed, kept, halved, added, counted = (s.sem(n) for n in ("summed", "normed", "kept", "halved", "added", "counted"))
        block = s.block()
        PARTS = 8
        q = NT // PARTS + 1

        def load(eng, buf, sem, window, row0, b_):
            for pp in range(2):
                src = window_rows[bass.ds(window * B * WP, B * WP), :].rearrange("(b w) e -> b w e", w=WP)
                src = src[:, row0:row0 + HOP, :].rearrange("b (t k) e -> b k t e", k=2)[:, pp, :, :]
                eng.dma_start(buf[pp * B:(pp + 1) * B, :].rearrange("p (t e) -> p t e", e=E), src).then_inc(sem, 16)

        def blocks(eng, one):
            one(0, 0, 0)
            one(1, 1, 0)
            with eng.Fori(1, NB // 2 - 1) as i:
                for u in range(2):
                    one(2 * i + u, u, i)
            one(NB - 2, 0, NB // 2 - 1)
            one(NB - 1, 1, NB // 2 - 1)

        def has(k, window):
            return not (isinstance(k, int) and k == (NB - 1 if window == "a" else 0))

        @block.scalar
        def _(act):
            for n in range(PARTS):
                lo, hi = n * q, min(NT, (n + 1) * q)
                act.dma_start(h[:, lo * E:hi * E].rearrange("p (t e) -> p t e", e=E),
                              h_keep[lo * P:hi * P, :].rearrange("(t p) e -> p t e", p=P)).then_inc(h_in, 16)

        @block.sync
        def _(sp):
            def one(k, u, i):
                if has(k, "a"):
                    wait_for(sp, halved, k - 1)
                    load(sp, wa[u], a_in[u], k, 0, k)
                if has(k, "b"):
                    wait_for(sp, halved, k - 1)
                    load(sp, wb_[u], b_in[u], k - 1, HOP, k)
            blocks(sp, one)

        @block.gpsimd
        def _(pool):
            def one(k, u, i):
                if has(k, "a") and has(k, "b"):
                    pool.wait_ge(a_in[u], 32 * (i + 1))
                    pool.wait_ge(b_in[u], 32 * (i + u))
                    wait_for(pool, halved, k - 1)
                    pool.tensor_tensor(t1[u][:, :], wa[u][:, :], wb_[u][:, :], ALU.add).then_inc(summed, 1)
            blocks(pool, one)

        @block.vector
        def _(dve):
            dve.wait_ge(h_in, 16 * PARTS)

            def norms(j0, n, x_, before):
                for t in range(n):
                    dve.tensor_scalar(x_[:, t * E:(t + 1) * E], tile_of(h, j0 + t), mean[:, bass.ds(j0 + t, 1)],
                                      rstd[:, bass.ds(j0 + t, 1)], ALU.subtract, ALU.mult).then_inc(normed, 1)
                dve.wait_ge(normed, before + n)
                hh = h[:, bass.ds(j0 * E, n * E)]
                dve.tensor_tensor(hh, hh, x_[:, 0:n * E], ALU.add).then_inc(kept, 1)

            def one(k, u, i):
                wait_for(dve, halved, k)
                norms(k * T, T, x[u], k * T)
                dve.wait_ge(kept, k + 1)
                hh = h[:, bass.ds(k * T * E, T * E)]
                if has(k, "a") and has(k, "b"):
                    dve.wait_ge(summed, k)
                    ins = dve.scalar_tensor_tensor(out=hh, in0=t1[u][:, :], scalar=0.5, in1=hh, op0=ALU.mult, op1=ALU.add)
                else:
                    only, sem = (wa, a_in) if has(k, "a") else (wb_, b_in)
                    dve.wait_ge(sem[u], 32 * (i + 1))
                    ins = dve.tensor_tensor(hh, only[u][:, :], hh, ALU.add)
                ins.then_inc(halved, 1)
                dve.wait_ge(halved, k + 1)
                for t in range(T):
                    dve.bn_stats(stats[:, bass.ds((k * T + t) * 6, 6)], tile_of(h, k * T + t)).then_inc(counted, 1)

            blocks(dve, one)
            norms(NB * T, TAIL, x[0], NB * T)
            dve.wait_ge(kept, NB + 1)
            for t in range(TAIL):
                j = NB * T + t
                dve.bn_stats(stats[:, j * 6:j * 6 + 6], tile_of(h, j)).then_inc(counted, 1)


NE1 = 32
CAP = TOK // NE1
GE = 4
XG = E + NE1
HALF = L // 2
LO = 41
HI = 16
SLOTS = HI * LO


def expert_softmax(nc, logits, rows):
    with Scope(nc, "sm1") as s:
        mx, sm, inv = s.sb("mx", [P, NT]), s.sb("sm", [P, NT]), s.sb("inv", [P, NT])
        step, raised, stored = s.sem("step"), s.sem("raised"), s.sem("stored")
        block = s.block()
        lg = logits[:, :].rearrange("p (t e) -> p t e", e=NE1)
        wide = lambda a: a[:, :].unsqueeze(2).broadcast_to([P, NT, NE1])
        PARTS = 6
        q = NT // PARTS

        @block.vector
        def _(dve):
            n = [0]

            def link(ins):
                n[0] += 1
                ins.then_inc(step, 1)
                dve.wait_ge(step, n[0])

            link(dve.tensor_reduce(mx[:, :], lg, AX_X, ALU.max))
            link(dve.tensor_tensor(lg, lg, wide(mx), ALU.subtract))
            dve.wait_ge(raised, 1)
            link(dve.tensor_reduce(sm[:, :], lg, AX_X, ALU.add))
            link(dve.reciprocal(inv[:, :], sm[:, :]))
            link(dve.tensor_tensor(lg, lg, wide(inv), ALU.mult))

        @block.scalar
        def _(act):
            act.wait_ge(step, 2)
            act.activation(logits[:, :], logits[:, :], ACT.Exp).then_inc(raised, 1)

        @block.sync
        def _(sp):
            sp.wait_ge(step, 5)
            for k in range(PARTS):
                sp.dma_start(rows[k * q * P:(k + 1) * q * P, E:XG].rearrange("(t p) e -> p t e", p=P),
                             lg[:, k * q:(k + 1) * q, :]).then_inc(stored, 16)
            sp.wait_ge(stored, 16 * PARTS)


def choose_tokens(nc, c, rows, slot):
    N = HALF * NE1
    BITS = 30
    with Scope(nc, "top") as s:
        val, cum = s.sb("val", [P, N]), s.sb("cum", [P, N])
        sel, eq = s.sb("sel", [P, N]), s.sb("eq", [P, N])
        mask = s.sb("mask", [P, N], BF16)
        zero = s.sb("zero", [P, N], BF16)
        tri, ones = s.sb("tri", [P, P], BF16), s.sb("ones", [P, P], BF16)
        low, cand, take, bit = (s.sb(n, [P, NE1], I32) for n in ("low", "cand", "take", "bit"))
        cnt, need, first, base = (s.sb(n, [P, NE1]) for n in ("cnt", "need", "first", "base"))
        own = s.sb("own", [P, NE1])
        own16 = s.sb("own16", [P, 2 * NE1], BF16)
        total = s.ps("total", [P, 512])
        before = s.ps("before", [P, 512])
        val_in, consts, ready = s.sem("val_in"), s.sem("consts"), s.sem("ready")
        tried, masked, counted, step = s.sem("tried"), s.sem("masked"), s.sem("counted"), s.sem("step")
        own_in, prefixed = s.sem("own_in"), s.sem("prefixed")
        block = s.block()
        by_fe = lambda a: a[:, :].rearrange("p (f e) -> p f e", e=NE1)
        by_ef = lambda a: a[:, :].rearrange("p (e f) -> p e f", f=HALF)
        swapped = lambda a: by_fe(a).rearrange("p f e -> p e f")
        wide = lambda a: a.unsqueeze(1).broadcast_to([P, HALF, NE1])
        tall = lambda a: a.unsqueeze(2).broadcast_to([P, NE1, HALF])
        chunks = [(k, min(512, N - k)) for k in range(0, N, 512)]
        PARTS = 3
        third = HALF // PARTS

        @block.sync
        def _(sp):
            for half in range(2):
                for k in range(6):
                    q = HALF // 6
                    src = rows[(half * HALF + k * q) * B:(half * HALF + (k + 1) * q) * B, E:XG]
                    sp.dma_start(by_fe(val)[half::2, k * q:(k + 1) * q, :], src.rearrange("(f b) e -> b f e", b=B))\
                      .then_inc(val_in, 16)

        @block.gpsimd
        def _(pool):
            pool.memset(tri[:, :], 1.0).then_inc(consts, 1)
            pool.memset(ones[:, :], 1.0).then_inc(consts, 1)
            pool.wait_ge(consts, 2)
            pool.affine_select(out=tri[:, :], in_=tri[:, :], compare_op=ALU.is_gt, fill=0.0, base=0,
                               pattern=[[1, P]], channel_multiplier=-1).then_inc(consts, 1)

        @block.tensor
        def _(pe):
            pe.wait_ge(consts, 3)

            def count(n):
                wait_for(pe, counted, n)
                for k, w in chunks:
                    pe.wait_ge(masked, PARTS * n + min(PARTS, (k + w + third * NE1 - 1) // (third * NE1)))
                    last = pe.matmul(total[:, 0:w], ones[:, :], mask[:, k:k + w], start=(k == 0),
                                     stop=(k + w == N))
                last.then_inc(tried, 1)

            count(0)
            with pe.Fori(1, BITS) as n:
                count(n)
            count(BITS)
            for n in range(2):
                pe.wait_ge(own_in, n + 1)
                pe.matmul(before[:, 0:NE1], tri[:, :], own16[:, n * NE1:(n + 1) * NE1], start=True, stop=True).then_inc(prefixed, 1)

        @block.vector
        def _(dve):
            dve.memset(low[:, :], 0).then_inc(ready, 1)
            dve.memset(bit[:, :], 1 << (BITS - 1)).then_inc(ready, 1)
            dve.memset(zero[:, :], 0.0).then_inc(ready, 1)
            dve.memset(first[:, :], 0.0).then_inc(ready, 1)
            dve.wait_ge(ready, 4)
            dve.wait_ge(val_in, 16 * 12)
            STEPS = 5

            def compare(n, against, op):
                wait_for(dve, tried, n)
                for k in range(PARTS):
                    f = slice(k * third, (k + 1) * third)
                    dve.tensor_tensor(by_fe(mask)[:, f, :], by_fe(val)[:, f, :], wide(against)[:, f, :], op)\
                       .then_inc(masked, 1)

            def total_of(n):
                dve.wait_ge(tried, n + 1)
                dve.tensor_reduce(cnt[:, :], total[:, :].rearrange("p (f e) -> p e f", e=NE1), AX_X, ALU.add)\
                   .then_inc(counted, 1)
                dve.wait_ge(counted, n + 1)

            def one_bit(n):
                link = lambda k, ins: (ins.then_inc(step, 1), dve.wait_ge(step, STEPS * n + k))
                link(1, dve.tensor_tensor(cand[:, :], low[:, :], bit[:, :], ALU.bitwise_or))
                compare(n, cand[:, :].bitcast(F32), ALU.is_ge)
                total_of(n)
                link(2, dve.tensor_scalar(take[:, :], cnt[:, :], float(CAP), None, ALU.is_ge))
                link(3, dve.tensor_tensor(take[:, :], take[:, :], bit[:, :], ALU.mult))
                link(4, dve.tensor_tensor(low[:, :], low[:, :], take[:, :], ALU.bitwise_or))
                link(5, dve.tensor_scalar(bit[:, :], bit[:, :], 1, None, ALU.logical_shift_right))

            one_bit(0)
            with dve.Fori(1, BITS) as n:
                one_bit(n)

            m = [STEPS * BITS]

            def link(ins):
                m[0] += 1
                ins.then_inc(step, 1)
                dve.wait_ge(step, m[0])

            least = low[:, :].bitcast(F32)
            compare(BITS, least, ALU.is_gt)
            total_of(BITS)
            link(dve.tensor_scalar(need[:, :], cnt[:, :], -1.0, float(CAP), ALU.mult, ALU.add))
            link(dve.tensor_tensor(by_ef(eq), swapped(val), tall(least), ALU.is_equal))
            dve.wait_ge(masked, PARTS * (BITS + 1))
            link(dve.tensor_copy(by_ef(sel), swapped(mask)))

            def ranks(of, n):
                link(dve.tensor_tensor_scan(cum[:, :], of[:, :], zero[:, :], 0.0, ALU.add, ALU.add))
                link(dve.tensor_copy(first[:, 1:NE1], by_ef(cum)[:, 0:NE1 - 1, HALF - 1]))
                link(dve.tensor_tensor(own[:, :], by_ef(cum)[:, :, HALF - 1], first[:, :], ALU.subtract))
                dve.tensor_copy(own16[:, n * NE1:(n + 1) * NE1], own[:, :]).then_inc(own_in, 1)
                dve.wait_ge(prefixed, n + 1)
                link(dve.tensor_tensor(base[:, :], before[:, 0:NE1], first[:, :], ALU.subtract))
                link(dve.tensor_tensor(by_ef(cum), by_ef(cum), tall(base[:, :]), ALU.add))

            ranks(eq, 0)
            link(dve.tensor_tensor(by_ef(cum), by_ef(cum), tall(need[:, :]), ALU.is_le))
            link(dve.tensor_tensor(eq[:, :], eq[:, :], cum[:, :], ALU.mult))
            link(dve.tensor_tensor(sel[:, :], sel[:, :], eq[:, :], ALU.add))
            ranks(sel, 1)
            link(dve.tensor_scalar(sel[:, :], sel[:, :], -2.0 * SLOTS, 2.0 * SLOTS - 1, ALU.mult, ALU.add))
            link(dve.tensor_tensor(swapped(slot), by_ef(cum), by_ef(sel), ALU.add))


def list_tokens(nc, slot, lists):
    N = HALF * NE1
    NG = NE1 // GE
    FB = 2
    with Scope(nc, "list") as s:
        si, hi_i = s.sb("si", [P, N], I32), s.sb("hi_i", [P, N], I32)
        hi, lo = s.sb("hi", [P, N], BF16), s.sb("lo", [P, N], BF16)
        iota16, iota41, nf = s.sb("iota16", [P, HI]), s.sb("iota41", [P, LO]), s.sb("nf", [P, HALF])
        d16, d41, np_ = s.sb("d16", [P, HI], BF16), s.sb("d41", [P, LO], BF16), s.sb("np", [P, 1])
        hot = [s.sb(f"hot{u}", [P, FB, NE1, HI], BF16) for u in range(2)]
        left = [s.sb(f"left{u}", [P, FB, NG, 2, GE, HI], BF16) for u in range(2)]
        right = [s.sb(f"right{u}", [P, FB, NE1, LO], BF16) for u in range(2)]
        out = s.sb("out", [P, NG, GE * LO])
        acc = s.ps("acc", [P, NG, 512])
        consts, step, hot_in, left_in, right_in = (s.sem(n) for n in ("consts", "step", "hot_in", "left_in", "right_in"))
        product, out_in, stored = s.sem("product"), s.sem("out_in"), s.sem("stored")
        block = s.block()
        ng = HALF // FB

        def run(eng, one):
            for u in range(2):
                one(u, u)
            with eng.Fori(1, ng // 2) as i:
                for u in range(2):
                    one(2 * i + u, u)
            if ng % 2:
                one(ng - 1, 0)

        @block.gpsimd
        def _(pool):
            pool.iota(iota16[:, :], pattern=[[1, HI]], base=0, channel_multiplier=0,
                      allow_small_or_imprecise_dtypes=True).then_inc(consts, 1)
            pool.iota(iota41[:, :], pattern=[[1, LO]], base=0, channel_multiplier=0,
                      allow_small_or_imprecise_dtypes=True).then_inc(consts, 1)
            pool.iota(nf[:, :], pattern=[[1, HALF]], base=0, channel_multiplier=0,
                      allow_small_or_imprecise_dtypes=True).then_inc(consts, 1)
            pool.iota(np_[:, :], pattern=[[0, 1]], base=0, channel_multiplier=1,
                      allow_small_or_imprecise_dtypes=True).then_inc(consts, 1)

        @block.vector
        def _(dve):
            dve.wait_ge(consts, 4)
            n = [0]

            def link(ins):
                n[0] += 1
                ins.then_inc(step, 1)
                dve.wait_ge(step, n[0])

            link(dve.tensor_copy(d16[:, :], iota16[:, :]))
            link(dve.tensor_copy(d41[:, :], iota41[:, :]))
            link(dve.tensor_scalar(si[:, :], slot[:, :], 1599.0, None, ALU.mult))
            link(dve.tensor_scalar(hi_i[:, :], si[:, :], 16, None, ALU.logical_shift_right))
            link(dve.tensor_copy(hi[:, :], hi_i[:, :]))
            link(dve.scalar_tensor_tensor(out=lo[:, :], in0=hi_i[:, :], scalar=-float(LO), in1=slot[:, :],
                                          op0=ALU.mult, op1=ALU.add))

            def one(g, u):
                wait_for(dve, left_in, g - 1)
                wait_for(dve, product, g - 1)
                h_ = hi[:, bass.ds(g * FB * NE1, FB * NE1)].unsqueeze(2).broadcast_to([P, FB * NE1, HI])
                l_ = lo[:, bass.ds(g * FB * NE1, FB * NE1)].unsqueeze(2).broadcast_to([P, FB * NE1, LO])
                flat = lambda t: t[:, :, :, :].rearrange("p f e d -> p (f e) d")
                dve.tensor_tensor(flat(hot[u]), h_, d16[:, :].unsqueeze(1).broadcast_to([P, FB * NE1, HI]),
                                  ALU.is_equal).then_inc(hot_in, 1)
                dve.tensor_tensor(flat(right[u]), l_, d41[:, :].unsqueeze(1).broadcast_to([P, FB * NE1, LO]),
                                  ALU.is_equal).then_inc(right_in, 1)
            run(dve, one)
            dve.wait_ge(product, ng)
            dve.tensor_copy(out[:, :, :], acc[:, :, 0:GE * LO]).then_inc(out_in, 1)

        @block.scalar
        def _(act):
            act.wait_ge(consts, 4)

            def one(g, u):
                act.wait_ge(hot_in, g + 1)
                wait_for(act, product, g - 1)
                src = hot[u][:, :, :, :].rearrange("p f (g e) d -> p (f g) (e d)", g=NG)
                dst = left[u][:, :, :, :, :, :].rearrange("p f g a e d -> p (f g) a (e d)")
                act.activation(dst[:, :, 0, :], src, ACT.Copy, scale=np_[:, 0:1])
                for f in range(FB):
                    src = hot[u][:, f, :, :].rearrange("p (g e) d -> p g (e d)", g=NG)
                    dst = left[u][:, f, :, 1, :, :].rearrange("p g e d -> p g (e d)")
                    last = act.activation(dst, src, ACT.Copy, scale=nf[:, bass.ds(g * FB + f, 1)])
                last.then_inc(left_in, 1)
            run(act, one)

        @block.tensor
        def _(pe):
            def one(g, u, first=False, last_=False):
                pe.wait_ge(left_in, g + 1)
                pe.wait_ge(right_in, g + 1)
                for f in range(FB):
                    for m in range(NG):
                        last = pe.matmul(acc[:, m, 0:GE * LO],
                                         left[u][:, f, m, :, :, :].rearrange("p a e d -> p (a e d)"),
                                         right[u][:, f, GE * m:GE * (m + 1), :].rearrange("p e d -> p (e d)"),
                                         start=first and f == 0, stop=last_ and f == FB - 1)
                last.then_inc(product, 1)
            one(0, 0, True)
            one(1, 1)
            with pe.Fori(1, (ng - 1) // 2) as i:
                for u in range(2):
                    one(2 * i + u, u)
            for g in range(2 * ((ng - 1) // 2), ng):
                one(g, g % 2, False, g == ng - 1)

        @block.sync
        def _(sp):
            sp.wait_ge(out_in, 1)
            for a in range(2):
                for e in range(GE):
                    r0 = (a * GE + e) * HI
                    dst = lists[a, :, :].rearrange("(g e) (d l) -> e d g l", e=GE, l=LO)[e, :, :, :]
                    sp.dma_start(dst, out[r0:r0 + HI, :, e * LO:(e + 1) * LO]).then_inc(stored, 16)
            sp.wait_ge(stored, 16 * 2 * GE)


RC = 108
NC = CAP // RC
D1 = 341
D1C = 3
LASTC = 96
WU = 2 * P + LASTC
WE = WU + D1C


def list_rows(nc, c, lists, index):
    R = NE1 * NC // 2
    with Scope(nc, "lrow") as s:
        q, f = s.sb("q", [R, 2, RC]), s.sb("f", [R, 2, RC])
        qi, odd = s.sb("qi", [R, 2, RC], I32), s.sb("odd", [R, 2, RC], I32)
        ps = s.ps("ps", [P, 2, 512])
        loaded, step, turned = s.sem("loaded"), s.sem("step"), s.sem("turned")
        block = s.block()

        @block.sync
        def _(sp):
            for a, t in enumerate((q, f)):
                for m in range(2):
                    for e in range(NE1 // 2):
                        src = lists[a, m * (NE1 // 2) + e, 0:CAP].rearrange("(n r) -> n r", r=RC)
                        sp.dma_start(t[e * NC:(e + 1) * NC, m, :], src).then_inc(loaded, 16)

        @block.vector
        def _(dve):
            n = [0]

            def link(ins):
                n[0] += 1
                ins.then_inc(step, 1)
                dve.wait_ge(step, n[0])

            dve.wait_ge(loaded, 16 * 2 * NE1)
            link(dve.tensor_copy(qi[:, :, :], q[:, :, :]))
            link(dve.tensor_scalar(odd[:, :, :], qi[:, :, :], 1, None, ALU.bitwise_and))
            link(dve.tensor_scalar(qi[:, :, :], qi[:, :, :], 1, None, ALU.logical_shift_right))
            link(dve.tensor_copy(q[:, :, :], odd[:, :, :]))
            link(dve.scalar_tensor_tensor(out=f[:, :, :], in0=f[:, :, :], scalar=float(B), in1=qi[:, :, :],
                                          op0=ALU.mult, op1=ALU.add))
            link(dve.scalar_tensor_tensor(out=f[:, :, :], in0=q[:, :, :], scalar=float(HALF * B), in1=f[:, :, :],
                                          op0=ALU.mult, op1=ALU.add))
            dve.wait_ge(turned, 1)
            link(dve.tensor_copy(index[0:RC, :].rearrange("p (m k) -> p m k", m=2), ps[0:RC, :, 0:R]))

        @block.tensor
        def _(pe):
            pe.wait_ge(step, 6)
            for m in range(2):
                last = pe.transpose(ps[0:RC, m, 0:R], f[:, m, :], c["ident"][0:R, 0:R])
            last.then_inc(turned, 1)


def expert_choice_ffn(nc, c, index, rows, out):
    H3 = NC // 2
    N = H3 * RC
    UPG = 2 * GE
    XB = UPG
    with Scope(nc, "ffn1") as s:
        wu = [s.sb(f"wu{u}", [P, WE]) for u in range(2)]
        wd = [s.sb(f"wd{u}", [P, D1C * E]) for u in range(2)]
        at = [[s.sb(f"at{u}_{r}", [RC, 1], U32) for r in range(H3)] for u in range(XB)]
        x = [s.sb(f"x{u}", [RC, H3, XG]) for u in range(XB)]
        xt = [s.sb(f"xt{u}", [P, N]) for u in range(2)]
        hid = [s.sb(f"hid{u}", [P, D1C, N]) for u in range(2)]
        y = [s.sb(f"y{u}", [RC, H3, E]) for u in range(2)]
        up = [s.ps(f"up{u}", [P, D1C, 512]) for u in range(2)]
        xps, yps = s.ps("xps", [P, 512]), s.ps("yps", [P, 512])
        w_in = [s.sem(f"w_in{u}") for u in range(2)]
        got = [s.sem(f"got{u}") for u in range(XB)]
        sent = [s.sem(f"sent{par}") for par in range(2)]
        index_in, issued = s.sem("index_in"), s.sem("issued")
        primed, ones_set = s.sem("primed"), s.sem("ones_set")
        turned, xt_in, upped, raised, downed, y_in = (s.sem(n) for n in ("turned", "xt_in", "upped", "raised", "downed", "y_in"))
        block = s.block()
        GROUPS = NE1 // GE

        def run(eng, one):
            for c_ in range(UPG):
                one(0, c_)
            with eng.Fori(1, GROUPS - 1) as i:
                for c_ in range(UPG):
                    one(i, c_)
            for c_ in range(UPG):
                one(GROUPS - 1, c_)

        def unit(i, c_, ahead=0):
            k = c_ + ahead
            i, k = i + k // UPG, k % UPG
            if isinstance(i, int) and (i < 0 or i >= GROUPS):
                return None
            return i, k

        @block.sync
        def _(sp):
            def one(i, c_):
                if c_ % 2:
                    return
                v = c_ // 2
                u = v % 2
                wait_for(sp, downed, UPG * i + c_ - 2)
                sp.dma_start(wu[u][:, :], c["ffn1_wu"][bass.ds(i * P, P), :]).then_inc(w_in[u], 16)
                sp.dma_start(wd[u][:, :], c["ffn1_wd"][bass.ds((i * GE + v) * P, P), :]).then_inc(w_in[u], 16)
            run(sp, one)

        @block.gpsimd
        def _(pool):
            def gather(i, c_):
                pool.wait_ge(index_in, H3 * (UPG * i + c_ + 1))
                pool.sem_inc(issued, 1)
                for r in range(H3):
                    pool.indirect_dma_start(out=x[c_][:, r, :], out_offset=None, in_=rows[:, :],
                                            in_offset=bass.IndirectOffsetOnAxis(ap=at[c_][r][:, 0:1], axis=0))\
                        .then_inc(got[c_], 16)

            def one(i, c_):
                nxt = unit(i, c_, XB - 3)
                if nxt:
                    gather(*nxt)
                k = UPG * i + c_
                pool.wait_ge(y_in, k + 1)
                if c_ % 2 == 0:
                    for par in range(2):
                        wait_for(pool, sent[par], 16 * H3 * (GE * i + c_ // 2))
                pool.sem_inc(issued, 1)
                for r in range(H3):
                    pool.indirect_dma_start(out=out[:, :],
                                            out_offset=bass.IndirectOffsetOnAxis(ap=at[c_][r][:, 0:1], axis=0),
                                            in_=y[c_ % 2][:, r, :], in_offset=None, compute_op=ALU.add)\
                        .then_inc(sent[c_ % 2], 16)

            for c_ in range(XB - 3):
                gather(0, c_)
            run(pool, one)
            for par in range(2):
                pool.wait_ge(sent[par], 16 * H3 * NE1)

        @block.tensor
        def _(pe):
            pe.wait_ge(ones_set, 2)

            def turn(i, c_):
                k = UPG * i + c_
                pe.wait_ge(got[c_], 16 * H3 * (i + 1))
                wait_for(pe, xt_in, k)
                for r in range(H3):
                    last = pe.transpose(xps[:, r * RC:(r + 1) * RC], x[c_][:, r, 0:E], c["ident"][0:RC, 0:RC])
                last.then_inc(turned, 1)

            def widen(i, c_):
                k = UPG * i + c_
                v = c_ // 2
                pe.wait_ge(w_in[v % 2], 32 * (2 * i + v // 2 + 1))
                pe.wait_ge(xt_in, k + 1)
                wait_for(pe, raised, D1C * (k - 1))
                for m in range(D1C):
                    M = P if m < D1C - 1 else LASTC
                    pe.matmul(up[c_ % 2][0:M, m, 0:N], wu[v % 2][:, m * P:m * P + M], xt[c_ % 2][:, :],
                              start=True, stop=True).then_inc(upped, 1)

            def narrow(i, c_):
                k = UPG * i + c_
                u = c_ // 2 % 2
                pe.wait_ge(raised, D1C * (k + 1))
                wait_for(pe, y_in, k)
                for r in range(H3):
                    for m in range(D1C):
                        last = pe.matmul(yps[0:RC, r * E:(r + 1) * E], hid[c_ % 2][:, m, r * RC:(r + 1) * RC],
                                         wd[u][:, m * E:(m + 1) * E], start=(m == 0), stop=(m == D1C - 1))
                last.then_inc(downed, 1)

            def one(i, c_):
                widen(i, c_)
                nxt, before = unit(i, c_, 1), unit(i, c_, -1)
                if nxt:
                    turn(*nxt)
                if before:
                    narrow(*before)

            turn(0, 0)
            run(pe, one)
            narrow(GROUPS - 1, UPG - 1)

        @block.scalar
        def _(act):
            def one(i, c_):
                k = UPG * i + c_
                u = c_ // 2 % 2
                wait_for(act, downed, k - 1)
                for m in range(D1C):
                    M = P if m < D1C - 1 else LASTC
                    act.wait_ge(upped, D1C * k + m + 1)
                    act.activation(hid[c_ % 2][0:M, m, :], up[c_ % 2][0:M, m, 0:N], ACT.Silu,
                                   bias=wu[u][0:M, WU + m:WU + m + 1]).then_inc(raised, 1)
            act.wait_ge(ones_set, 2)
            run(act, one)

        @block.vector
        def _(dve):
            for u in range(2):
                dve.memset(hid[u][LASTC:P, D1C - 1, :], 0.0).then_inc(primed, 1)
            dve.wait_ge(primed, 2)
            for u in range(2):
                dve.memset(hid[u][LASTC:LASTC + 1, D1C - 1, :], 1.0).then_inc(ones_set, 1)

            def indices(i, c_):
                for r in range(H3):
                    dve.tensor_copy(at[c_][r][:, :],
                                    index[0:RC, bass.ds((UPG * i + c_) * H3 + r, 1)]).then_inc(index_in, 1)

            def one(i, c_):
                k = UPG * i + c_
                dve.wait_ge(turned, k + 1)
                wait_for(dve, upped, D1C * (k - 1))
                dve.tensor_copy(xt[c_ % 2][:, :], xps[:, 0:N]).then_inc(xt_in, 1)
                before = unit(i, c_, -1)
                if before:
                    finish(*before)

            def finish(i, c_):
                k = UPG * i + c_
                dve.wait_ge(downed, k + 1)
                wait_for(dve, sent[c_ % 2], 16 * H3 * (GE * i + c_ // 2))
                g = x[c_][:, :, bass.ds(E + GE * i + c_ // 2, 1)].broadcast_to([RC, H3, E])
                dve.tensor_tensor(y[c_ % 2][:, :, :], yps[0:RC, 0:H3 * E].rearrange("p (r e) -> p r e", e=E), g,
                                  ALU.mult).then_inc(y_in, 1)
                ahead = unit(i, c_, XB - 2)
                if ahead and unit(i, c_, -2):
                    indices(*ahead)

            for c_ in range(XB):
                indices(0, c_)
            run(dve, one)
            finish(GROUPS - 1, UPG - 1)
def early_fusion(nc, ap, out):
    dram = lambda name, shape: nc.dram_tensor(name, shape, F32).ap()
    sorted_rows, sorted_out = dram("sorted_rows", [NFT * FT, E]), dram("sorted_out", [NFT * FT, E])
    h_keep, window_rows = dram("h_keep", [TOK, E]), dram("window_rows", [B * NW * WP, E])
    expert_rows, lists = dram("expert_rows", [TOK, XG]), dram("lists", [2, NE1, SLOTS])
    with Scope(nc, "all") as s:
        ident, stats = s.sb("ident", [P, P]), s.sb("stats", [P, NT * 6])
        mean, rstd, rstd2 = (s.sb(n, [P, NT]) for n in ("mean", "rstd", "rstd2"))
        make_identity(nc, ident)
        c = dict(ap)
        c["ident"] = ident
        with Scope(nc, "wide") as wide:
            turned_rows = wide.sb("turned_rows", [P, NTC])
            with Scope(nc, "front") as front:
                h = front.sb("h", [P, NT * E])
                embed_tokens(nc, ap["patches"], ap["text"], ap["tok_w"], ap["tok_b"], h, stats)
                finish_statistics(nc, "ln0", stats, mean, rstd)
                image_attention(nc, c, h, stats, mean, rstd)
                with Scope(nc, "route") as r:
                    logits, ratio = r.sb("logits", [P, NT * NE0]), r.sb("ratio", [P, NT])
                    dest, tile_expert = r.sb("dest", [P, NT], U32), r.sb("tile_expert", [P, NFT], I32)
                    clear_rows(nc, sorted_rows)
                    finish_statistics(nc, "ln1", stats, mean, rstd)
                    token_logits(nc, "lg0", c, h, mean, rstd, ap["ffn0_r"], ap["ffn0_br"], NE0, logits)
                    route_top1(nc, c, logits, dest, ratio, tile_expert, turned_rows)
                    scatter_rows(nc, h, mean, rstd, dest, sorted_rows)
                    sorted_ffn(nc, c, tile_expert, sorted_rows, sorted_out)
                    gather_rows(nc, h, dest, ratio, sorted_out, stats)
                finish_statistics(nc, "ln2", stats, mean, rstd, rstd2)
                turn_rows(nc, c, h, mean, rstd2, turned_rows, h_keep)
            window_attention(nc, c, turned_rows, window_rows)
        clear_semaphores(nc)
        with Scope(nc, "back") as back:
            logits = back.sb("logits1", [P, NT * NE1])
            h = back.sb("h1", [P, NT * E])
            combine_windows(nc, h, h_keep, mean, rstd, window_rows, stats)
            finish_statistics(nc, "ln3", stats, mean, rstd)
            token_logits(nc, "lg1", c, h, mean, rstd, ap["ffn1_r"], ap["ffn1_br"], NE1, logits, expert_rows, out)
            expert_softmax(nc, logits, expert_rows)
        index = s.sb("index", [P, NE1 * NC], U32)
        with Scope(nc, "choice") as choice:
            slot = choice.sb("slot", [P, HALF * NE1])
            choose_tokens(nc, c, expert_rows, slot)
            list_tokens(nc, slot, lists)
        list_rows(nc, c, lists, index)
        expert_choice_ffn(nc, c, index, expert_rows, out)


def tables():
    r = np.arange(P)
    heads = (r[:, None] // HD == np.arange(NH)[None]).astype(np.float32)
    inv = (1.0 / (np.float32(10000.0) ** (np.arange(0, HD, 2, dtype=np.float32) / np.float32(HD)))).astype(np.float32)
    angle = np.arange(B, dtype=np.float32)[:, None] * inv[None]
    angle = np.concatenate([angle, angle], -1).T
    cos, sin = np.tile(np.cos(angle), (NH, 1)), np.tile(np.sin(angle), (NH, 1))
    sign = np.where(r % HD < HD // 2, -1, 1).astype(np.float32)[:, None]
    qs = np.float32(HD ** -0.5)
    same = (r[:, None] % B == np.arange(B)[None]).astype(np.float32)
    none = np.zeros_like(same)
    q8 = NH * HOP
    row_head = ((r[:, None] // HOP % 4 == np.arange(4)[None]) & (r[:, None] < q8)).astype(np.float32)
    row_query = np.zeros((P, 4, P), np.float32)
    for row in range(q8):
        second = row < q8 // 2
        for w in range(4):
            row_query[row, w, WP * w + (HOP if second else 0) + row % HOP] = 1
    return {"heads": heads, "rope": np.concatenate([cos * qs, sin * sign * qs, cos, sin * sign], 1).astype(np.float32),
            "sel": np.concatenate([same, none, none, same], 1), "row_head": row_head,
            "at1_sel": row_query.reshape(P, 4 * P),
            "falling": np.broadcast_to(NE0 - np.arange(NE0, dtype=np.float32), (P, NE0))}


def layouts(i):
    t = tables()
    rows = lambda v: np.broadcast_to(v, (P, v.shape[-1]))
    turned = lambda names: [i[n].T for n in names]
    rot = np.arange(E).reshape(NH, 2, HD // 2)[:, ::-1].reshape(-1)
    o = {k: t[k] for k in ("rope", "sel", "at1_sel", "falling")}
    x = i["x"].reshape(B, 3, 14, 16, 14, 16).transpose(2, 4, 0, 1, 3, 5).reshape(NPATCH * B // P, P, KP, P)
    o["patches"] = x.transpose(0, 3, 2, 1).reshape(-1, KP * P)
    o["text"] = i["txt"].transpose(1, 0, 2).reshape(NTEXT * B // P, P, E)
    o["tok_w"] = i["L0_tok_w"].T.reshape(KP, P, E).transpose(1, 0, 2).reshape(P, KP * E)
    o["tok_b"] = rows(i["L0_tok_b"])
    wq, wk, wv, wo = (i[f"L0_attn_W{n}"] for n in "qkvo")
    bq, bk, bv = (i[f"L0_attn_b{n}"] for n in "qkv")
    o["at0_w"] = np.stack([wq.T, wq[rot].T, wk.T, wk[rot].T, wv.T, wo.T])
    o["at0_cols"] = np.concatenate([np.stack([bq, bq[rot], bk, bk[rot], bv], 1), t["heads"]], 1)
    o["at0_bo"] = rows(i["L0_attn_bo"])
    o["ffn0_r"] = np.pad(i["L0_ffn_Wr"], ((0, 0), (0, P - NE0)))
    o["ffn0_br"] = rows(i["L0_ffn_br"])
    w2 = i["L0_ffn_W2"].reshape(NE0, H0 // P, P, E).transpose(0, 2, 1, 3).reshape(NE0, P, H0)
    b1 = i["L0_ffn_b1"].reshape(NE0, H0 // P, P).transpose(0, 2, 1)
    b2 = np.broadcast_to(i["L0_ffn_b2"][:, None], (NE0, P, E))
    o["ffn0_wb"] = np.concatenate([i["L0_ffn_W1"], w2, b1, b2], 2).reshape(NE0 * P, WB0)
    w_in, b_in = i["L1_attn_w_in"].reshape(3, E, E), i["L1_attn_b_in"].reshape(3, E)
    o["at1_w"] = np.stack([w_in[0].T, w_in[1].T, w_in[2].T, i["L1_attn_w_out"].T])
    o["at1_cols"] = np.concatenate([b_in.T, t["heads"], t["row_head"]], 1)
    o["at1_bo"] = rows(i["L1_attn_b_out"])
    o["at1_gb"] = np.stack([i["L1_attn_ln_g"], i["L1_attn_ln_b"]], 1)
    o["ffn1_r"] = np.pad(i["L1_ffn_W_router"], ((0, 0), (0, P - NE1)))
    o["ffn1_br"] = rows(i["L1_ffn_b_router"])
    ng = NE1 // GE
    w_up = np.pad(i["L1_ffn_W_up"], ((0, 0), (0, 0), (0, WU - D1)))
    b_up = np.pad(i["L1_ffn_b_up"], ((0, 0), (0, D1C * P - D1))).reshape(ng, D1C, P).transpose(0, 2, 1)
    o["ffn1_wu"] = np.concatenate([w_up, b_up], 2).reshape(ng * P, WE)
    zeros = lambda n: np.zeros((NE1, n, E), np.float32)
    w_down = np.concatenate([i["L1_ffn_W_down"], zeros(WU - D1), i["L1_ffn_b_down"][:, None],
                             zeros(D1C * P - WU - 1)], 1)
    o["ffn1_wd"] = w_down.reshape(NE1, D1C, P, E).transpose(0, 2, 1, 3).reshape(NE1 * P, D1C * E)
    return {k: np.ascontiguousarray(v) for k, v in o.items()}


def kernel(**inputs):
    import concourse.bacc as bacc
    from concourse.bass_utils import run_bass_kernel_spmd

    nc = bacc.Bacc("TRN2", target_bir_lowering=False, num_devices=1)
    arrays, ap = {}, {}
    for name, a in layouts({k: np.asarray(v) for k, v in inputs.items()}).items():
        arrays[f"in_{name}_dram"] = a
        ap[name] = nc.dram_tensor(f"in_{name}_dram", a.shape, mybir.dt.from_np(a.dtype), kind="ExternalInput").ap()
    out = nc.dram_tensor("out_0_dram", [TOK, E], F32, kind="ExternalOutput").ap()
    early_fusion(nc, ap, out)
    r = run_bass_kernel_spmd(nc, [arrays], core_ids=[0])
    return r.results[0]["out_0_dram"].reshape(L, B, E).transpose(1, 0, 2)
```

```python
from contextlib import ExitStack

import numpy as np

import concourse.bass as bass
from concourse import mybir

F32 = mybir.dt.float32
BF16 = mybir.dt.bfloat16
I32 = mybir.dt.int32
U32 = mybir.dt.uint32
ALU = mybir.AluOpType
ACT = mybir.ActivationFunctionType
AX_X = mybir.AxisListType.X

P = 128
B = 64
E = 128
NPATCH = 196
NTEXT = 128
L = NPATCH + NTEXT
TOK = B * L
NT = TOK // P
KP = 768 // P
NH = 8
HD = E // NH
EPS = 1e-5

NE0 = 8
FT = 256
NFT = TOK // FT + NE0 - 1
XS = E + 4
BLANK = 2048


def wait_for(eng, sem, count):
    if isinstance(count, int) and count <= 0:
        return
    eng.wait_ge(sem, count)


def neighbour(i, c, ahead, per, loops):
    i, c = i + (c + ahead) // per, (c + ahead) % per
    if isinstance(i, int) and (i < 0 or i >= loops):
        return None
    return i, c


class Scope:

    def __init__(self, nc, name):
        self.nc, self.name, self.stack = nc, name, ExitStack()

    def __enter__(self):
        self.stack.__enter__()
        return self

    def __exit__(self, *error):
        return self.stack.__exit__(*error)

    def sb(self, name, shape, dt=F32):
        return self.stack.enter_context(self.nc.sbuf_tensor(f"{self.name}_{name}", shape, dt))

    def ps(self, name, shape, dt=F32):
        return self.stack.enter_context(self.nc.psum_tensor(f"{self.name}_{name}", shape, dt))

    def sem(self, name):
        return self.stack.enter_context(self.nc.semaphore(f"{self.name}_{name}"))

    def block(self):
        return self.stack.enter_context(self.nc.Block())


def tile_of(h, j):
    return h[:, bass.ds(j * E, E)]


def clear_semaphores(nc):
    free = sorted(nc.released_uncleared_semaphores)
    with nc.Block() as block:
        @block.gpsimd
        def _(pool):
            pool.sem_clear(range(free[0], free[-1] + 1))


def make_identity(nc, ident):
    with Scope(nc, "id") as s:
        zeroed, done = s.sem("zeroed"), s.sem("done")
        block = s.block()

        @block.gpsimd
        def _(pool):
            pool.memset(ident[:, :], 0.0).then_inc(zeroed, 1)
            pool.wait_ge(zeroed, 1)
            pool.affine_select(out=ident[:, :], in_=ident[:, :], compare_op=ALU.not_equal, fill=1.0, base=0,
                               pattern=[[-1, P]], channel_multiplier=1).then_inc(done, 1)
            pool.wait_ge(done, 1)


def finish_statistics(nc, name, stats, mean, rstd, scale2=None):
    with Scope(nc, name) as s:
        t1, t2, v = s.sb("t1", [P, NT]), s.sb("t2", [P, NT]), s.sb("v", [P, NT])
        sd, var = s.sb("sd", [P, NT]), s.sb("var", [P, NT])
        step, root = s.sem("step"), s.sem("root")
        block = s.block()
        st = stats[:, :].rearrange("p (t k) -> p t k", k=6)

        @block.scalar
        def _(act):
            act.wait_ge(step, 7)
            act.activation(sd[:, :], v[:, :], ACT.Sqrt).then_inc(root, 1)
            if scale2 is not None:
                act.wait_ge(step, 15)
                act.activation(sd[:, :], v[:, :], ACT.Sqrt).then_inc(root, 1)

        @block.vector
        def _(dve):
            count = [0]

            def link(ins):
                count[0] += 1
                ins.then_inc(step, 1)
                dve.wait_ge(step, count[0])

            def invert(out, n):
                dve.wait_ge(root, n)
                link(dve.reciprocal(out[:, :], sd[:, :]))
                link(dve.tensor_tensor(t1[:, :], out[:, :], out[:, :], ALU.mult))
                link(dve.tensor_tensor(t1[:, :], t1[:, :], v[:, :], ALU.mult))
                link(dve.tensor_scalar(t1[:, :], t1[:, :], -0.5, 1.5, ALU.mult, ALU.add))
                link(dve.tensor_tensor(out[:, :], out[:, :], t1[:, :], ALU.mult))

            link(dve.tensor_tensor(t1[:, :], st[:, :, 1], st[:, :, 4], ALU.add))
            link(dve.tensor_scalar(mean[:, :], t1[:, :], 0.5, None, ALU.mult))
            link(dve.tensor_tensor(t2[:, :], st[:, :, 1], st[:, :, 4], ALU.subtract))
            link(dve.scalar_tensor_tensor(out=t1[:, :], in0=t2[:, :], scalar=0.25, in1=t2[:, :],
                                          op0=ALU.mult, op1=ALU.mult))
            link(dve.tensor_tensor(t2[:, :], st[:, :, 2], st[:, :, 5], ALU.add))
            link(dve.scalar_tensor_tensor(out=var[:, :], in0=t2[:, :], scalar=1.0 / E, in1=t1[:, :],
                                          op0=ALU.mult, op1=ALU.add))
            link(dve.tensor_scalar(v[:, :], var[:, :], EPS, None, ALU.add))
            invert(rstd, 1)
            if scale2 is not None:
                link(dve.tensor_tensor(t2[:, :], rstd[:, :], rstd[:, :], ALU.mult))
                link(dve.tensor_tensor(t2[:, :], t2[:, :], var[:, :], ALU.mult))
                link(dve.tensor_scalar(v[:, :], t2[:, :], EPS, None, ALU.add))
                invert(scale2, 2)
                link(dve.tensor_tensor(scale2[:, :], scale2[:, :], rstd[:, :], ALU.mult))


def embed_tokens(nc, patches, text, w, bias, h, stats):
    U = 7
    NPT = NPATCH * B // P
    assert NPT % U == 0
    with Scope(nc, "tok") as s:
        x = [s.sb(f"x{u}", [P, KP * P]) for u in range(U)]
        w_sb = s.sb("w", [P, KP * E])
        b_sb = s.sb("b", [P, E])
        acc = s.ps("acc", [P, U, 512])
        loaded = [s.sem(f"loaded{u}") for u in range(U)]
        weights, text_in = s.sem("weights"), s.sem("text_in")
        product, added, counted = s.sem("product"), s.sem("added"), s.sem("counted")
        block = s.block()

        @block.sync
        def _(sp):
            sp.dma_start(w_sb[:, :], w).then_inc(weights, 16)
            sp.dma_start(b_sb[:, :], bias).then_inc(weights, 16)
            for u in range(U):
                sp.dma_start(x[u][:, :], patches[u * P:(u + 1) * P, :]).then_inc(loaded[u], 16)
            with sp.Fori(1, NPT // U) as i:
                for u in range(U):
                    sp.wait_ge(product, (i - 1) * U + u + 1)
                    sp.dma_start(x[u][:, :], patches[bass.ds((i * U + u) * P, P), :]).then_inc(loaded[u], 16)

        @block.scalar
        def _(act):
            q = (NT - NPT) // 4
            for k in range(4):
                act.dma_start(h[:, (NPT + k * q) * E:(NPT + (k + 1) * q) * E].rearrange("p (t e) -> p t e", e=E),
                               text[k * q:(k + 1) * q, :, :].rearrange("t p e -> p t e")).then_inc(text_in, 16)
            act.wait_ge(text_in, 64)

        @block.tensor
        def _(pe):
            pe.wait_ge(weights, 32)

            def products(i, u):
                pe.wait_ge(loaded[u], (i + 1) * 16)
                wait_for(pe, added, (i - 1) * U + u + 1)
                for k in range(KP):
                    last = pe.matmul(acc[:, u, 0:E], x[u][:, k * P:(k + 1) * P], w_sb[:, k * E:(k + 1) * E],
                                     start=(k == 0), stop=(k == KP - 1))
                last.then_inc(product, 1)

            for u in range(U):
                products(0, u)
            with pe.Fori(1, NPT // U) as i:
                for u in range(U):
                    products(i, u)

        @block.vector
        def _(dve):
            st = stats[:, :].rearrange("p (t k) -> p t k", k=6)
            with dve.Fori(0, NPT // U) as i:
                for u in range(U):
                    dve.wait_ge(product, i * U + u + 1)
                    dve.tensor_tensor(tile_of(h, i * U + u), acc[:, u, 0:E], b_sb[:, :], ALU.add)\
                       .then_inc(added, 1)
                    if u >= 1:
                        dve.wait_ge(added, i * U + u)
                        dve.bn_stats(stats[:, bass.ds((i * U + u - 1) * 6, 6)], tile_of(h, i * U + u - 1))\
                           .then_inc(counted, 1)
                dve.wait_ge(added, i * U + U)
                dve.bn_stats(stats[:, bass.ds((i * U + U - 1) * 6, 6)], tile_of(h, i * U + U - 1))\
                   .then_inc(counted, 1)
            dve.wait_ge(text_in, 64)
            with dve.Fori(NPT // 8, NT // 8) as i:
                for u in range(8):
                    dve.bn_stats(stats[:, bass.ds((i * 8 + 2 + u) * 6, 6)], tile_of(h, i * 8 + 2 + u))\
                       .then_inc(counted, 1)


def image_attention(nc, c, h, stats, mean, rstd, blank, sorted_rows):
    G = NT // 2
    N = 2 * P
    NP = 4
    with Scope(nc, "at0") as s:
        wq, wqr, wk, wkr, wv, wo = [s.sb(n, [P, E]) for n in ("wq", "wqr", "wk", "wkr", "wv", "wo")]
        cols = s.sb("cols", [P, 5 + NH])
        rope = s.sb("rope", [P, 4 * B])
        bo = s.sb("bo", [P, N])
        sel = s.sb("sel", [P, 2 * P])
        xn = s.sb("xn", [P, N])
        xt = s.sb("xt", [P, NP, 2, B])
        q1, q2, k1, k2 = [s.sb(n, [P, N]) for n in ("q1", "q2", "k1", "k2")]
        q, k = s.sb("q", [P, N]), s.sb("k", [P, N])
        qm = s.sb("qm", [P, NP, NH, B])
        vb = s.sb("vb", [P, NP, 2, P])
        mx = s.sb("mx", [P, NP, 4])
        pr = s.sb("pr", [P, NP, 4, B])
        pt = s.sb("pt", [P, NP, 2, P])
        rc = s.sb("rc", [P, NP, 2, 2])
        on = s.sb("on", [P, NP, E])
        ot = s.sb("ot", [P, N])

        bank = s.ps("bank", [P, 8, 512])
        S = [bank[:, n, :].rearrange("p (i t) -> p i t", t=P) for n in range(NP)]
        PT = bank[:, 0:2, :].rearrange("p a (b c d) -> p a b c d", b=2, c=2)
        AV = bank[:, 2:4, :].rearrange("p a (b c d) -> p a b c d", b=2, c=2)
        Q, QR, K, KR = bank[:, 4, 0:N], bank[:, 4, N:2 * N], bank[:, 5, 0:N], bank[:, 5, N:2 * N]
        V = bank[:, 6, :].rearrange("p (n e) -> p n e", n=NP)
        XT, OT = bank[:, 7, 0:N], bank[:, 7, N:2 * N]
        Y = bank[:, 0, 0:N]

        const_in, cleared, ones_set = s.sem("const_in"), s.sem("cleared"), s.sem("ones_set")
        blanked, blank_out = s.sem("blanked"), s.sem("blank_out")
        normed, xt_ps, xt_in = s.sem("normed"), s.sem("xt_ps"), s.sem("xt_in")
        qk_ps, v_ps, roped, qk_in, masked = s.sem("qk_ps"), s.sem("v_ps"), s.sem("roped"), s.sem("qk_in"), s.sem("masked")
        bias_added, v_in = s.sem("bias_added"), s.sem("v_in")
        scored, maxed, shifted, raised = s.sem("scored"), s.sem("maxed"), s.sem("shifted"), s.sem("raised")
        pt_ps, pt_in, av_ps, inverted, on_in = s.sem("pt_ps"), s.sem("pt_in"), s.sem("av_ps"), s.sem("inverted"), s.sem("on_in")
        ot_ps, ot_in, y_ps, h_in, counted = s.sem("ot_ps"), s.sem("ot_in"), s.sem("y_ps"), s.sem("h_in"), s.sem("counted")
        block = s.block()

        def run(eng, front, back):
            front(0)
            back(0, front)
            with eng.Fori(1, G - 1) as g:
                back(g, front)
            back(G - 1, None)

        @block.sync
        def _(sp):
            for n, t in enumerate((wq, wqr, wk, wkr, wv, wo)):
                sp.dma_start(t[:, :], c["at0_w"][n, :, :]).then_inc(const_in, 16)
            sp.dma_start(cols[:, :], c["at0_cols"]).then_inc(const_in, 16)
            sp.dma_start(rope[:, :], c["rope"]).then_inc(const_in, 16)
            sp.dma_start(sel[:, :], c["sel"]).then_inc(const_in, 16)
            for n in range(2):
                sp.dma_start(bo[:, n * E:(n + 1) * E], c["at0_bo"]).then_inc(const_in, 16)
            sp.wait_ge(const_in, 16 * 11)
            n = BLANK // P
            sp.wait_ge(blanked, 2)
            for k in range(NFT * FT // BLANK):
                sp.dma_start(sorted_rows[k * BLANK:(k + 1) * BLANK, :].rearrange("(p r) e -> p (r e)", p=P),
                             blank[:, 0:n * XS]).then_inc(blank_out, 16)
            sp.wait_ge(blank_out, 16 * (NFT * FT // BLANK))

        @block.gpsimd
        def _(pool):
            n = BLANK // P
            pool.memset(blank[:, 0:n * XS], 0.0).then_inc(blanked, 1)
            pool.wait_ge(blanked, 1)
            pool.iota(blank[:, 0:n * XS].rearrange("p (r e) -> p r e", e=XS)[:, :, E], pattern=[[1, n]], base=TOK,
                      channel_multiplier=n, allow_small_or_imprecise_dtypes=True).then_inc(blanked, 1)
            pool.memset(vb[:, :, :, :], 0.0).then_inc(cleared, 1)
            pool.memset(on[:, :, :], 0.0).then_inc(cleared, 1)
            pool.wait_ge(cleared, 2)
            for half in range(2):
                pool.memset(vb[64 * half:64 * half + 64, :, :, 64 * half + 32:64 * half + 33], 1.0)\
                    .then_inc(ones_set, 1)
                pool.wait_ge(ones_set, half + 1)
            pool.wait_ge(const_in, 16 * 11)

            def front(g):
                pool.wait_ge(normed, 2 * (g + 1))
                pool.tensor_tensor(h[:, bass.ds(g * N, N)], h[:, bass.ds(g * N, N)], bo[:, :], ALU.add)\
                    .then_inc(bias_added, 1)
                wait_for(pool, masked, NH * g)
                pool.wait_ge(roped, 4 * g + 2)
                pool.tensor_tensor(q[:, :], q1[:, :], q2[:, :], ALU.add).then_inc(qk_in, 1)
                wait_for(pool, scored, NP * g)
                pool.wait_ge(roped, 4 * g + 4)
                pool.tensor_tensor(k[:, :], k1[:, :], k2[:, :], ALU.add).then_inc(qk_in, 1)

            def back(g, then):
                if then:
                    then(g + 1)

            run(pool, front, back)

        @block.tensor
        def _(pe):
            pe.wait_ge(const_in, 16 * 11)

            def front(g):
                pe.wait_ge(normed, 2 * (g + 1))
                wait_for(pe, xt_in, g)
                for t in range(2):
                    last = pe.transpose(XT[:, t * P:(t + 1) * P], xn[:, t * P:(t + 1) * P], c["ident"][:, :])
                last.then_inc(xt_ps, 1)
                pe.wait_ge(xt_in, g + 1)
                wait_for(pe, roped, 4 * g)
                for ps, wt in ((Q, wq), (QR, wqr), (K, wk), (KR, wkr)):
                    pe.matmul(ps, wt[:, :], xt[:, :, 0, :], start=True, stop=True).then_inc(qk_ps, 1)
                wait_for(pe, v_in, 2 * g)
                for n in range(NP):
                    last = pe.matmul(V[:, n, :], xt[:, n, :, :], wv[:, :], start=True, stop=True)
                last.then_inc(v_ps, 1)

            def back(g, then):
                pe.wait_ge(masked, NH * (g + 1))
                pe.wait_ge(qk_in, 2 * (g + 1))
                wait_for(pe, h_in, g)
                for n in range(NP):
                    if n == 2:
                        wait_for(pe, on_in, 2 * g)
                    for i in range(4):
                        last = pe.matmul(S[n][:, i, :], qm[:, n, 2 * i:2 * i + 2, :],
                                         k[:, (n // 2) * P:(n // 2) * P + P], start=True, stop=True)
                    last.then_inc(scored, 1)
                if then:
                    then(g + 1)
                pe.wait_ge(raised, NP * (g + 1))
                pe.wait_ge(shifted, NP * (g + 1))
                for n in range(NP):
                    for i in range(2):
                        last = pe.transpose(PT[:, n // 2, n % 2, i, :], pr[:, n, 2 * i:2 * i + 2, :],
                                            c["ident"][:, :])
                    if n % 2:
                        last.then_inc(pt_ps, 1)
                pe.wait_ge(v_in, 2 * (g + 1))
                for n in range(NP):
                    if n % 2 == 0:
                        pe.wait_ge(pt_in, 2 * g + n // 2 + 1)
                    for i in range(2):
                        last = pe.matmul(AV[:, n // 2, n % 2, i, :], pt[:, n, i, :], vb[:, n, i, :],
                                         start=True, stop=True)
                last.then_inc(av_ps, 1)
                pe.wait_ge(on_in, 2 * (g + 1))
                wait_for(pe, ot_in, g)
                for t in range(2):
                    for pp in range(2):
                        last = pe.matmul(OT[:, t * P:(t + 1) * P], on[:, 2 * t + pp, :],
                                         sel[:, pp * P:(pp + 1) * P], start=(pp == 0), stop=(pp == 1))
                last.then_inc(ot_ps, 1)
                pe.wait_ge(ot_in, g + 1)
                for t in range(2):
                    last = pe.matmul(Y[:, t * P:(t + 1) * P], ot[:, t * P:(t + 1) * P], wo[:, :],
                                     start=True, stop=True)
                last.then_inc(y_ps, 1)

            run(pe, front, back)

        @block.scalar
        def _(act):
            act.wait_ge(const_in, 16 * 11)
            act.wait_ge(ones_set, 2)

            def evacuate_v(g):
                act.wait_ge(v_ps, g + 1)
                wait_for(act, av_ps, g)
                for half in range(2):
                    rows = slice(64 * half, 64 * half + 64)
                    src = V[rows, :, :].rearrange("p n (i c) -> p (n i) c", c=64)[:, :, 32 * half:32 * half + 32]
                    dst = vb[rows, :, :, :].rearrange("p n i c -> p (n i) c")[:, :, 64 * half:64 * half + 32]
                    act.activation(dst, src, ACT.Copy).then_inc(v_in, 1)

            def front(g):
                act.wait_ge(xt_ps, g + 1)
                wait_for(act, v_ps, g)
                act.activation(xt[:, :, :, :], XT.rearrange("p (n b) -> p n b", b=B).unsqueeze(2)
                               .broadcast_to([P, NP, 2, B]), ACT.Copy).then_inc(xt_in, 1)

            def back(g, then):
                if then:
                    then(g + 1)
                for n in range(NP):
                    act.wait_ge(shifted, NP * g + n + 1)
                    act.activation(pr[:, n, :, :], pr[:, n, :, :], ACT.Exp).then_inc(raised, 1)
                wait_for(act, av_ps, g)
                for n in range(2):
                    act.wait_ge(pt_ps, 2 * g + n + 1)
                    act.activation(pt[:, 2 * n:2 * n + 2, :, :], PT[:, n, :, :, :], ACT.Copy).then_inc(pt_in, 1)
                if then:
                    act.wait_ge(av_ps, g + 1)
                    evacuate_v(g + 1)
                act.wait_ge(ot_ps, g + 1)
                wait_for(act, y_ps, g)
                act.activation(ot[:, :], OT, ACT.Identity, bias=cols[:, 4:5]).then_inc(ot_in, 1)

            front(0)
            evacuate_v(0)
            back(0, front)
            with act.Fori(1, G - 1) as g:
                back(g, front)
            back(G - 1, None)

        @block.vector
        def _(dve):
            dve.wait_ge(const_in, 16 * 11)
            dve.wait_ge(cleared, 2)
            tab = rope[:, :].rearrange("p (k b) -> p k b", k=4)

            def normalise(g):
                wait_for(dve, xt_ps, g)
                for t in range(2):
                    j = 2 * g + t
                    dve.tensor_scalar(xn[:, t * E:(t + 1) * E], tile_of(h, j), mean[:, bass.ds(j, 1)],
                                      rstd[:, bass.ds(j, 1)], ALU.subtract, ALU.mult).then_inc(normed, 1)

            def rotate(g):
                wait_for(dve, qk_in, 2 * g)
                for n, (ps, to) in enumerate(((Q, q1), (QR, q2), (K, k1), (KR, k2))):
                    dve.wait_ge(qk_ps, 4 * g + (2 if n < 2 else 4))
                    dve.scalar_tensor_tensor(out=to[:, :].rearrange("p (n b) -> p n b", b=B),
                                             in0=ps.rearrange("p (n b) -> p n b", b=B), scalar=cols[:, n:n + 1],
                                             in1=tab[:, n:n + 1, :].broadcast_to([P, NP, B]),
                                             op0=ALU.add, op1=ALU.mult).then_inc(roped, 1)
                dve.wait_ge(qk_in, 2 * g + 1)
                wait_for(dve, scored, NP * g)
                for n in range(NH):
                    dve.tensor_scalar(qm[:, :, n, :], q[:, :].rearrange("p (n b) -> p n b", b=B), cols[:, 5 + n:6 + n], None, ALU.mult)\
                       .then_inc(masked, 1)

            def front(g):
                normalise(g)
                rotate(g)

            def back(g, then):
                if then:
                    normalise(g + 1)
                wait_for(dve, pt_ps, 2 * g)
                for n in range(NP):
                    own = S[n][:, :, (n % 2) * B:(n % 2) * B + B]
                    dve.wait_ge(scored, NP * g + n + 1)
                    dve.tensor_reduce(mx[:, n, :], own, AX_X, ALU.max).then_inc(maxed, 1)
                for n in range(NP):
                    own = S[n][:, :, (n % 2) * B:(n % 2) * B + B]
                    dve.wait_ge(maxed, NP * g + n + 1)
                    dve.tensor_tensor(pr[:, n, :, :], own, mx[:, n, :].unsqueeze(2).broadcast_to([P, 4, B]),
                                      ALU.subtract).then_inc(shifted, 1)
                if then:
                    rotate(g + 1)
                dve.wait_ge(av_ps, g + 1)
                dve.reciprocal(rc[:, :, :, :].rearrange("p n i k -> p (n i) k"),
                               AV.rearrange("p a b c (k d) -> p (a b c) k d", k=2)[:, :, :, 32])\
                   .then_inc(inverted, 1)
                dve.wait_ge(inverted, g + 1)
                for par in range(2):
                    rows = slice(64 * par, 64 * par + 64)
                    src = AV.rearrange("p a b c (k d) -> p (a b c) k d", k=2)[rows, :, :, HD * par:HD * par + HD]
                    dst = on[rows, :, :].rearrange("p n (i k d) -> p (n i) k d", i=2, k=2)[:, :, :, HD * par:HD * par + HD]
                    inv = rc[rows, :, :, :].rearrange("p n i k -> p (n i) k").unsqueeze(3).broadcast_to([64, 8, 2, HD])
                    dve.tensor_tensor(dst, src, inv, ALU.mult).then_inc(on_in, 1)
                dve.wait_ge(y_ps, g + 1)
                dve.wait_ge(bias_added, g + 1)
                dve.tensor_tensor(h[:, bass.ds(g * N, N)], Y, h[:, bass.ds(g * N, N)], ALU.add).then_inc(h_in, 1)
                dve.wait_ge(h_in, g + 1)
                for t in range(2):
                    dve.bn_stats(stats[:, bass.ds((2 * g + t) * 6, 6)], tile_of(h, 2 * g + t)).then_inc(counted, 1)

            run(dve, front, back)
def token_logits(nc, name, c, h, mean, rstd, w, bias, ne, logits, rows_out=None, h_out=None):
    W = 3
    N = W * P
    NG = NT // W
    with Scope(nc, name) as s:
        w_sb, b_sb = s.sb("w", [P, P]), s.sb("b", [P, ne])
        xn, xt = [s.sb(f"xn{u}", [P, N]) for u in range(2)], [s.sb(f"xt{u}", [P, N]) for u in range(2)]
        xps, lps = [s.ps(f"xps{u}", [P, 512]) for u in range(2)], [s.ps(f"lps{u}", [P, 512]) for u in range(2)]
        const_in, h_stored = s.sem("const_in"), s.sem("h_stored")
        stored = [s.sem(f"stored{u}") for u in range(2)]
        normed, turned, xt_in, product, added = (s.sem(n) for n in ("normed", "turned", "xt_in", "product", "added"))
        block = s.block()

        def run(eng, step):
            for u in range(2):
                step(u, u)
            with eng.Fori(1, NG // 2) as i:
                for u in range(2):
                    step(2 * i + u, u, i)

        @block.sync
        def _(sp):
            sp.dma_start(w_sb[:, :], w).then_inc(const_in, 16)
            sp.dma_start(b_sb[:, :], bias).then_inc(const_in, 16)
            if h_out is not None:
                for k in range(6):
                    q = NT // 6
                    sp.dma_start(h_out[k * q * P:(k + 1) * q * P, :].rearrange("(t p) e -> p t e", p=P),
                                 h[:, k * q * E:(k + 1) * q * E].rearrange("p (t e) -> p t e", e=E))\
                      .then_inc(h_stored, 16)
            if rows_out is not None:
                def step(g, u, i=0):
                    sp.wait_ge(normed, W * (g + 1))
                    dst = rows_out[bass.ds(g * N, N), 0:E].rearrange("(t p) e -> p t e", p=P)
                    sp.dma_start(dst, xn[u][:, :].rearrange("p (t e) -> p t e", e=E)).then_inc(stored[u], 16)
                run(sp, step)
                for u in range(2):
                    sp.wait_ge(stored[u], 16 * (NG // 2))
            if h_out is not None:
                sp.wait_ge(h_stored, 16 * 6)

        @block.vector
        def _(dve):
            dve.wait_ge(const_in, 32)

            def norm(g, u, i=0):
                wait_for(dve, turned, g - 1)
                if rows_out is not None:
                    wait_for(dve, stored[u], 16 * i)
                for t in range(W):
                    j = W * g + t
                    dve.tensor_scalar(xn[u][:, t * E:(t + 1) * E], tile_of(h, j), mean[:, bass.ds(j, 1)],
                                      rstd[:, bass.ds(j, 1)], ALU.subtract, ALU.mult).then_inc(normed, 1)

            def add(g, u):
                dve.wait_ge(product, g + 1)
                lg = logits[:, bass.ds(g * W * ne, W * ne)].rearrange("p (t n) -> p t n", n=ne)
                dve.tensor_tensor(lg, lps[u][:, 0:N].rearrange("p (t n) -> p t n", n=P)[:, :, 0:ne],
                                  b_sb[:, :].unsqueeze(1).broadcast_to([P, W, ne]), ALU.add).then_inc(added, 1)

            norm(0, 0)
            norm(1, 1)
            with dve.Fori(1, NG // 2) as i:
                for u in range(2):
                    norm(2 * i + u, u, i)
                    add(2 * i + u - 2, u)
            add(NG - 2, 0)
            add(NG - 1, 1)

        @block.tensor
        def _(pe):
            pe.wait_ge(const_in, 32)

            def turn(g, u, i=0):
                pe.wait_ge(normed, W * (g + 1))
                wait_for(pe, xt_in, g - 1)
                for t in range(W):
                    last = pe.transpose(xps[u][:, t * P:(t + 1) * P], xn[u][:, t * P:(t + 1) * P], c["ident"][:, :])
                last.then_inc(turned, 1)

            def multiply(g, u):
                pe.wait_ge(xt_in, g + 1)
                wait_for(pe, added, g - 1)
                for t in range(W):
                    last = pe.matmul(lps[u][:, t * P:(t + 1) * P], xt[u][:, t * P:(t + 1) * P], w_sb[:, :],
                                     start=True, stop=True)
                last.then_inc(product, 1)

            turn(0, 0)
            turn(1, 1)
            multiply(0, 0)
            turn(2, 0)
            multiply(1, 1)
            with pe.Fori(1, NG // 2 - 1) as i:
                for u in range(2):
                    turn(2 * i + u + 1, 1 - u)
                    multiply(2 * i + u, u)
            turn(NG - 1, 1)
            multiply(NG - 2, 0)
            multiply(NG - 1, 1)

        @block.scalar
        def _(act):
            def step(g, u, i=0):
                act.wait_ge(turned, g + 1)
                wait_for(act, product, g - 1)
                act.activation(xt[u][:, :], xps[u][:, 0:N], ACT.Copy).then_inc(xt_in, 1)
            run(act, step)


H0 = 512
WB0 = H0 + H0 + 4 + E


def route_top1(nc, c, logits, dest, ratio, tile_expert, room):
    N = NT * NE0
    with Scope(nc, "rt0") as s:
        mx, sm = s.sb("mx", [P, NT]), s.sb("sm", [P, NT])
        key, hot, ex, cum, tot = (room[:, n * N:(n + 1) * N] for n in range(5))
        hot16 = s.sb("hot16", [P, N], BF16)
        tri, ones = s.sb("tri", [P, P], BF16), s.sb("ones", [P, P], BF16)
        small = s.sb("small", [P, 8, NE0])
        zero = s.sb("zero", [P, N])
        cnt = s.sb("cnt", [P, NE0], I32)
        tid, le = s.sb("tid", [P, NFT]), s.sb("le", [P, NFT, NE0 - 1])
        tef = s.sb("tef", [P, NFT])
        ranks, totals = s.ps("ranks", [P, 3, 512]), s.ps("totals", [P, 3, 512])
        const_in, consts, step, raised, counted = (s.sem(n) for n in ("const_in", "consts", "step", "raised", "counted"))
        block = s.block()
        by_te = lambda a: a[:, :].rearrange("p (t e) -> p t e", e=NE0)
        by_et = lambda a: a[:, :].rearrange("p (e t) -> p e t", t=NT)

        @block.sync
        def _(sp):
            sp.dma_start(small[:, 0, :], c["falling"]).then_inc(const_in, 16)

        @block.gpsimd
        def _(pool):
            pool.memset(tri[:, :], 1.0).then_inc(consts, 1)
            pool.memset(ones[:, :], 1.0).then_inc(consts, 1)
            pool.wait_ge(consts, 2)
            pool.affine_select(out=tri[:, :], in_=tri[:, :], compare_op=ALU.is_gt, fill=0.0, base=0,
                               pattern=[[1, P]], channel_multiplier=-1).then_inc(consts, 1)
            pool.iota(tid[:, :], pattern=[[1, NFT]], base=0, channel_multiplier=0,
                      allow_small_or_imprecise_dtypes=True).then_inc(consts, 1)

        @block.tensor
        def _(pe):
            pe.wait_ge(consts, 4)
            pe.wait_ge(step, 6)
            third = N // 3
            for n in range(3):
                pe.matmul(ranks[:, n, 0:third], tri[:, :], hot16[:, n * third:(n + 1) * third], start=True, stop=True)
                last = pe.matmul(totals[:, n, 0:third], ones[:, :], hot16[:, n * third:(n + 1) * third],
                                 start=True, stop=True)
            last.then_inc(counted, 1)

        @block.scalar
        def _(act):
            act.wait_ge(step, 7)
            act.activation(ex[:, :], ex[:, :], ACT.Exp).then_inc(raised, 1)

        @block.vector
        def _(dve):
            n = [0]

            def link(ins):
                n[0] += 1
                ins.then_inc(step, 1)
                dve.wait_ge(step, n[0])

            dve.wait_ge(const_in, 16)
            mx_b = mx[:, :].unsqueeze(2).broadcast_to([P, NT, NE0])
            link(dve.tensor_reduce(mx[:, :], by_te(logits), AX_X, ALU.max))
            link(dve.tensor_tensor(by_te(key), by_te(logits), mx_b, ALU.is_ge))
            link(dve.tensor_tensor(by_te(key), by_te(key), small[:, 0:1, :].broadcast_to([P, NT, NE0]), ALU.mult))
            link(dve.tensor_reduce(sm[:, :], by_te(key), AX_X, ALU.max))
            link(dve.tensor_tensor(by_te(hot), by_te(key), sm[:, :].unsqueeze(2).broadcast_to([P, NT, NE0]),
                                   ALU.is_equal))
            link(dve.tensor_copy(hot16[:, :], hot[:, :]))
            link(dve.tensor_tensor(by_te(ex), by_te(logits), mx_b, ALU.subtract))
            link(dve.memset(zero[:, :], 0.0))
            dve.wait_ge(raised, 1)
            link(dve.tensor_reduce(sm[:, :], by_te(ex), AX_X, ALU.add))
            link(dve.reciprocal(mx[:, :], sm[:, :]))
            link(dve.reciprocal(sm[:, :], mx[:, :]))
            link(dve.tensor_tensor(ratio[:, :], mx[:, :], sm[:, :], ALU.mult))
            dve.wait_ge(counted, 1)
            third = NT // 3
            for k in range(3):
                dst = by_et(tot)[:, :, k * third:(k + 1) * third].rearrange("p e t -> p t e")
                link(dve.tensor_copy(dst, totals[:, k, 0:third * NE0].rearrange("p (t e) -> p t e", e=NE0)))
            link(dve.tensor_tensor_scan(cum[:, :], tot[:, :], zero[:, :], 0.0, ALU.add, ALU.add))
            first, ends = small[:, 1, :], by_et(cum)[:, :, NT - 1]
            link(dve.memset(small[:, 1:8, :], 0.0))
            link(dve.tensor_copy(first[:, 1:NE0], ends[:, 0:NE0 - 1]))
            link(dve.tensor_tensor(small[:, 2, :], ends, first, ALU.subtract))
            link(dve.tensor_scalar(cnt[:, :], small[:, 2, :], float(FT - 1), None, ALU.add))
            link(dve.tensor_scalar(cnt[:, :], cnt[:, :], 8, None, ALU.logical_shift_right))
            link(dve.tensor_copy(small[:, 3, :], cnt[:, :]))
            link(dve.tensor_tensor_scan(small[:, 4, :], small[:, 3, :], small[:, 7, :], 0.0, ALU.add, ALU.add))
            link(dve.tensor_tensor(small[:, 5, :], small[:, 4, :], small[:, 3, :], ALU.subtract))
            link(dve.scalar_tensor_tensor(out=small[:, 6, :], in0=small[:, 5, :], scalar=float(FT), in1=first,
                                          op0=ALU.mult, op1=ALU.subtract))
            link(dve.tensor_tensor(cum[:, :], cum[:, :], tot[:, :], ALU.subtract))
            link(dve.tensor_tensor(by_et(cum), by_et(cum), small[:, 6, :].unsqueeze(2).broadcast_to([P, NE0, NT]),
                                   ALU.add))
            for k in range(3):
                part = by_te(key)[:, k * third:(k + 1) * third, :]
                link(dve.tensor_tensor(part, ranks[:, k, 0:third * NE0].rearrange("p (t e) -> p t e", e=NE0),
                                       by_et(cum)[:, :, k * third:(k + 1) * third].rearrange("p e t -> p t e"),
                                       ALU.add))
            link(dve.tensor_tensor(key[:, :], key[:, :], hot[:, :], ALU.mult))
            link(dve.tensor_reduce(sm[:, :], by_te(key), AX_X, ALU.add))
            link(dve.tensor_copy(dest[:, :], sm[:, :]))
            dve.wait_ge(consts, 4)
            link(dve.tensor_tensor(le[:, :, :], tid[:, :].unsqueeze(2).broadcast_to([P, NFT, NE0 - 1]),
                                   small[:, 4:5, 0:NE0 - 1].broadcast_to([P, NFT, NE0 - 1]), ALU.is_ge))
            link(dve.tensor_reduce(tef[:, :], le[:, :, :], AX_X, ALU.add))
            link(dve.tensor_copy(tile_expert[:, :], tef[:, :]))


def scatter_rows(nc, c, h, mean, rstd, dest, sorted_rows, weights):
    U = 6
    with Scope(nc, "scat") as s:
        xn = [s.sb(f"xn{u}", [P, XS]) for u in range(U)]
        at = [s.sb(f"at{u}", [P, 1], U32) for u in range(U)]
        number = s.sb("number", [P, NT])
        numbered, padded, w_in = s.sem("numbered"), s.sem("padded"), s.sem("w_in")
        normed, issued = s.sem("normed"), s.sem("issued")
        sent = [s.sem(f"sent{u}") for u in range(U)]
        block = s.block()

        @block.sync
        def _(sp):
            for e in range(NE0):
                sp.dma_start(weights[:, e * WB0:(e + 1) * WB0], c["ffn0_wb"][e * P:(e + 1) * P, :]).then_inc(w_in, 16)
            sp.wait_ge(w_in, 16 * NE0)

        @block.vector
        def _(dve):
            for u in range(U):
                dve.memset(xn[u][:, E:XS], 0.0).then_inc(padded, 1)
            dve.wait_ge(padded, U)
            dve.wait_ge(numbered, 1)

            def step(i, u):
                j = i * U + u
                wait_for(dve, sent[u], 16 * i)
                dve.tensor_copy(at[u][:, :], dest[:, bass.ds(j, 1)]).then_inc(normed, 1)
                dve.tensor_copy(xn[u][:, E:E + 1], number[:, bass.ds(j, 1)]).then_inc(normed, 1)
                dve.tensor_scalar(xn[u][:, 0:E], tile_of(h, j), mean[:, bass.ds(j, 1)], rstd[:, bass.ds(j, 1)],
                                  ALU.subtract, ALU.mult).then_inc(normed, 1)
            for u in range(U):
                step(0, u)
            with dve.Fori(1, NT // U) as i:
                for u in range(U):
                    step(i, u)

        @block.gpsimd
        def _(pool):
            pool.iota(number[:, :], pattern=[[P, NT]], base=0, channel_multiplier=1,
                      allow_small_or_imprecise_dtypes=True).then_inc(numbered, 1)
            with pool.Fori(0, NT // U) as i:
                for u in range(U):
                    pool.wait_ge(normed, 3 * (i * U + u + 1))
                    pool.sem_inc(issued, 1)
                    pool.indirect_dma_start(out=sorted_rows[:, :],
                                            out_offset=bass.IndirectOffsetOnAxis(ap=at[u][:, 0:1], axis=0),
                                            in_=xn[u][:, :], in_offset=None).then_inc(sent[u], 16)
            for u in range(U):
                pool.wait_ge(sent[u], 16 * (NT // U))


def sorted_ffn(nc, c, tile_expert, sorted_rows, weights, token_out):
    HC = H0 // P
    R = FT // P
    U = 4
    LOOPS = NFT // U
    assert NFT % U == 0
    with Scope(nc, "ffn0") as s:
        wb = [s.sb(f"wb{u}", [P, WB0]) for u in range(2)]
        x = [s.sb(f"x{u}", [P, R, XS]) for u in range(U)]
        at = [[s.sb(f"at{u}_{r}", [P, 1], U32) for r in range(R)] for u in range(U)]
        xt = [s.sb(f"xt{u}", [P, FT]) for u in range(2)]
        hid = [s.sb(f"hid{u}", [P, HC, FT]) for u in range(2)]
        y = [s.sb(f"y{u}", [P, R, E]) for u in range(U)]
        xps, yps = [s.ps(f"xps{u}", [P, 512]) for u in range(2)], [s.ps(f"yps{u}", [P, 512]) for u in range(2)]
        up = [s.ps(f"up{u}", [P, 2, 512]) for u in range(2)]
        x_in, sent = ([s.sem(f"{n}{u}") for u in range(U)] for n in ("x_in", "sent"))
        w_in, issued, index_in = s.sem("w_in"), s.sem("issued"), s.sem("index_in")
        turned, xt_in, upped, gelued, downed, y_in = (s.sem(n) for n in ("turned", "xt_in", "upped", "gelued", "downed", "y_in"))
        block = s.block()

        def run(eng, one):
            for c_ in range(U):
                one(0, c_)
            with eng.Fori(1, LOOPS - 1) as i:
                for c_ in range(U):
                    one(i, c_)
            for c_ in range(U):
                one(LOOPS - 1, c_)

        @block.sync
        def _(sp):
            def one(i, c_):
                t = U * i + c_
                wait_for(sp, index_in, R * (t - U + 1))
                sp.dma_start(x[c_][:, :, :], sorted_rows[bass.ds(t * FT, FT), :].rearrange("(p r) e -> p r e", r=R))\
                  .then_inc(x_in[c_], 16)
            run(sp, one)

        @block.gpsimd
        def _(pool):
            def one(i, c_):
                pool.wait_ge(y_in, U * i + c_ + 1)
                pool.sem_inc(issued, 1)
                for r in range(R):
                    pool.indirect_dma_start(out=token_out[:, :],
                                            out_offset=bass.IndirectOffsetOnAxis(ap=at[c_][r][:, 0:1], axis=0),
                                            in_=y[c_][:, r, :], in_offset=None).then_inc(sent[c_], 16)

            run(pool, one)
            for u in range(U):
                pool.wait_ge(sent[u], 16 * R * LOOPS)

        @block.tensor
        def _(pe):
            def turn(i, c_):
                t, u = U * i + c_, c_ % 2
                pe.wait_ge(x_in[c_], 16 * (i + 1))
                wait_for(pe, xt_in, t - 1)
                for r in range(R):
                    last = pe.transpose(xps[u][:, r * P:(r + 1) * P], x[c_][:, r, 0:E], c["ident"][:, :])
                last.then_inc(turned, 1)

            def widen(i, c_):
                t, u = U * i + c_, c_ % 2
                pe.wait_ge(w_in, t + 1)
                pe.wait_ge(xt_in, t + 1)
                wait_for(pe, gelued, HC * (t - 1))
                for m in range(HC):
                    pe.matmul(up[u][:, m // 2, (m % 2) * FT:(m % 2) * FT + FT], wb[u][:, m * P:(m + 1) * P],
                              xt[u][:, :], start=True, stop=True).then_inc(upped, 1)

            def narrow(i, c_):
                t, u = U * i + c_, c_ % 2
                pe.wait_ge(gelued, HC * (t + 1))
                wait_for(pe, y_in, t - 1)
                for r in range(R):
                    for m in range(HC):
                        last = pe.matmul(yps[u][:, r * E:(r + 1) * E], hid[u][:, m, r * P:(r + 1) * P],
                                         wb[u][:, H0 + m * E:H0 + (m + 1) * E], start=(m == 0), stop=(m == HC - 1))
                last.then_inc(downed, 1)

            def one(i, c_):
                widen(i, c_)
                after, before = neighbour(i, c_, 1, U, LOOPS), neighbour(i, c_, -1, U, LOOPS)
                if after:
                    turn(*after)
                if before:
                    narrow(*before)

            turn(0, 0)
            run(pe, one)
            narrow(LOOPS - 1, U - 1)

        @block.scalar
        def _(act):
            def one(i, c_):
                t, u = U * i + c_, c_ % 2
                wait_for(act, downed, t - 1)
                for m in range(HC):
                    act.wait_ge(upped, HC * t + 2 * (m // 2) + 2)
                    act.activation(hid[u][:, m, :], up[u][:, m // 2, (m % 2) * FT:(m % 2) * FT + FT], ACT.Gelu,
                                   bias=wb[u][:, 2 * H0 + m:2 * H0 + m + 1]).then_inc(gelued, 1)
            run(act, one)

        @block.vector
        def _(dve):
            def place(i, c_):
                t, u = U * i + c_, c_ % 2
                expert = dve.value_load(tile_expert[0:1, bass.ds(t, 1)], min_val=0, max_val=NE0 - 1)
                wait_for(dve, y_in, t - 1)
                dve.tensor_copy(wb[u][:, :], weights[:, bass.ds(expert * WB0, WB0)]).then_inc(w_in, 1)

            def evacuate(i, c_):
                t, u = U * i + c_, c_ % 2
                dve.wait_ge(turned, t + 1)
                wait_for(dve, upped, HC * (t - 1))
                dve.tensor_copy(xt[u][:, :], xps[u][:, 0:FT]).then_inc(xt_in, 1)
                wait_for(dve, sent[c_], 16 * R * i)
                for r in range(R):
                    dve.tensor_copy(at[c_][r][:, :], x[c_][:, r, E:E + 1]).then_inc(index_in, 1)

            def finish(i, c_):
                t, u = U * i + c_, c_ % 2
                dve.wait_ge(downed, t + 1)
                b2 = wb[u][:, 2 * H0 + 4:WB0].unsqueeze(1).broadcast_to([P, R, E])
                dve.tensor_tensor(y[c_][:, :, :], yps[u][:, 0:R * E].rearrange("p (r e) -> p r e", e=E), b2, ALU.add)\
                   .then_inc(y_in, 1)

            def one(i, c_):
                after, before = neighbour(i, c_, 1, U, LOOPS), neighbour(i, c_, -1, U, LOOPS)
                if after:
                    evacuate(*after)
                if before:
                    finish(*before)
                if after:
                    place(*after)

            place(0, 0)
            evacuate(0, 0)
            run(dve, one)
            finish(LOOPS - 1, U - 1)


def add_rows(nc, h, ratio, token_out, stats):
    W = 9
    U = 3
    LOADS = NT // W
    assert LOADS % U == 0
    with Scope(nc, "add") as s:
        y = [s.sb(f"y{u}", [P, W * E]) for u in range(U)]
        got = [s.sem(f"got{u}") for u in range(U)]
        added, counted = s.sem("added"), s.sem("counted")
        block = s.block()

        @block.sync
        def _(sp):
            def load(i, u):
                n = i * U + u
                wait_for(sp, added, W * (n - U + 1))
                sp.dma_start(y[u][:, :].rearrange("p (t e) -> p t e", e=E),
                             token_out[bass.ds(n * W * P, W * P), :].rearrange("(t p) e -> p t e", p=P))\
                  .then_inc(got[u], 16)
            for u in range(U):
                load(0, u)
            with sp.Fori(1, LOADS // U) as i:
                for u in range(U):
                    load(i, u)

        @block.vector
        def _(dve):
            with dve.Fori(0, LOADS // U) as i:
                for u in range(U):
                    dve.wait_ge(got[u], 16 * (i + 1))
                    first = (i * U + u) * W
                    for t in range(W + 1):
                        if t < W:
                            j = first + t
                            dve.scalar_tensor_tensor(out=tile_of(h, j), in0=y[u][:, t * E:(t + 1) * E],
                                                     scalar=ratio[:, bass.ds(j, 1)], in1=tile_of(h, j),
                                                     op0=ALU.mult, op1=ALU.add).then_inc(added, 1)
                        if t:
                            dve.wait_ge(added, first + t)
                            dve.bn_stats(stats[:, bass.ds((first + t - 1) * 6, 6)], tile_of(h, first + t - 1))\
                               .then_inc(counted, 1)


WIN, HOP = 20, 10
NW = (L - WIN) // HOP + 1
NB = L // HOP
WP = 32
NTC = B * L + 2 * WP


def turn_rows(nc, c, h, mean, scale, turned_rows, h_keep):
    W = 3
    N = W * P
    NG = NT // W
    with Scope(nc, "turn") as s:
        gb = s.sb("gb", [P, 2])
        xn = [s.sb(f"xn{u}", [P, N]) for u in range(2)]
        xps = [s.ps(f"xps{u}", [P, 512]) for u in range(2)]
        const_in, stored, cleared = s.sem("const_in"), s.sem("stored"), s.sem("cleared")
        normed, turned, placed = s.sem("normed"), s.sem("turned"), s.sem("placed")
        block = s.block()

        def run(eng, step):
            for u in range(2):
                step(u, u)
            with eng.Fori(1, NG // 2) as i:
                for u in range(2):
                    step(2 * i + u, u)

        @block.sync
        def _(sp):
            sp.dma_start(gb[:, :], c["at1_gb"]).then_inc(const_in, 16)
            q = NT // 6
            for k in range(6):
                sp.dma_start(h_keep[k * q * P:(k + 1) * q * P, :].rearrange("(t p) e -> p t e", p=P),
                             h[:, k * q * E:(k + 1) * q * E].rearrange("p (t e) -> p t e", e=E)).then_inc(stored, 16)
            sp.wait_ge(stored, 16 * 6)

        @block.gpsimd
        def _(pool):
            pool.memset(turned_rows[:, B * L:NTC], 0.0).then_inc(cleared, 1)

        @block.vector
        def _(dve):
            def step(g, u):
                wait_for(dve, turned, g - 1)
                for t in range(W):
                    j = W * g + t
                    dve.tensor_scalar(xn[u][:, t * E:(t + 1) * E], tile_of(h, j), mean[:, bass.ds(j, 1)],
                                      scale[:, bass.ds(j, 1)], ALU.subtract, ALU.mult).then_inc(normed, 1)
            run(dve, step)

        @block.tensor
        def _(pe):
            def step(g, u):
                pe.wait_ge(normed, W * (g + 1))
                wait_for(pe, placed, g - 1)
                for t in range(W):
                    last = pe.transpose(xps[u][:, t * P:(t + 1) * P], xn[u][:, t * P:(t + 1) * P], c["ident"][:, :])
                last.then_inc(turned, 1)
            run(pe, step)

        @block.scalar
        def _(act):
            act.wait_ge(const_in, 16)

            def step(g, u):
                act.wait_ge(turned, g + 1)
                by_image = turned_rows[:, 0:B * L].rearrange("p (b l) -> p l b", l=L)
                act.activation(by_image[:, bass.ds(2 * W * g, 2 * W), :],
                               xps[u][:, 0:N].rearrange("p (l b) -> p l b", b=B), ACT.Identity,
                               bias=gb[:, 1:2], scale=gb[:, 0:1]).then_inc(placed, 1)
            run(act, step)


def window_attention(nc, c, turned_rows, window_rows):
    GW = 4
    NGR = NB // GW
    Q8 = NH * HOP
    SB = 11
    KX = HOP * (NB + 7)
    HH = NH // 2
    VC = HH * HD
    with Scope(nc, "at1") as s:
        wq, wk, wv, wo = (s.sb(n, [P, E]) for n in ("wq", "wk", "wv", "wo"))
        cols = s.sb("cols", [P, 3 + NH + HH])
        bo, bias, bv = s.sb("bo", [P, E]), s.sb("bias", [P, E]), s.sb("bv", [P, P])
        xw = [s.sb(f"xw{u}", [P, NB, WP]) for u in range(2)]
        kx = [s.sb(f"kx{u}", [P, KX]) for u in range(2)]
        qs = s.sb("qs", [P, NB * HOP])
        qm = [s.sb(f"qm{u}", [P, NB, NH, HOP]) for u in range(2)]
        bm = s.sb("bm", [P, NB, 3])
        mx = s.sb("mx", [P, NB, 2])
        sums, inv = s.sb("sums", [P, 2, NB]), s.sb("inv", [P, 2, NB])
        pr = [s.sb(f"pr{u}", [P, 2, NB + 1, WP]) for u in range(2)]
        pt = [s.sb(f"pt{u}", [P, 2, HH, 2, HOP]) for u in range(2)]
        vb = [s.sb(f"vb{u}", [P, 2, GW, VC]) for u in range(2)]
        om = s.sb("om", [P, GW, E])
        ot = s.sb("ot", [P, GW, WP])
        y = [s.sb(f"y{u}", [P, NGR, E]) for u in range(2)]

        bank = s.ps("bank", [P, 8, 512])
        AV = bank[:, 3:5, 0:GW * VC].rearrange("p t (w c) -> p t w c", c=VC)
        V, PT = bank[:, 5, 0:E], bank[:, 5, E:E + 2 * Q8].rearrange("p (a k) -> p a k", a=2)
        OT, Y = bank[:, 6, 0:GW * Q8].rearrange("p (w k) -> p w k", w=GW), bank[:, 7, 0:E]

        const_in, cleared = s.sem("const_in"), s.sem("cleared")
        spread, qk_ps, k_in, q_in, masked = (s.sem(n) for n in ("spread", "qk_ps", "k_in", "q_in", "masked"))
        scored, blocked, maxed, shifted, raised = (s.sem(n) for n in ("scored", "blocked", "maxed", "shifted", "raised"))
        vt_ps, pt_in, vb_in, av_ps = (s.sem(n) for n in ("vt_ps", "pt_in", "vb_in", "av_ps"))
        summed, inverted, weighted = s.sem("summed"), s.sem("inverted"), s.sem("weighted")
        bv_in, bias_ps, bias_in, biased = s.sem("bv_in"), s.sem("bias_ps"), s.sem("bias_in"), s.sem("biased")
        om_in, ot_ps, ot_in, y_ps, y_in = (s.sem(n) for n in ("om_in", "ot_ps", "ot_in", "y_ps", "y_in"))
        stored = [s.sem(f"stored{u}") for u in range(2)]
        block = s.block()

        NCLEAR = 8
        banks = [(n, n * SB, min(SB, NB - n * SB)) for n in range(3)]

        def images(eng, one):
            one(0, 0, 0, True, False)
            one(1, 1, 0, False, False)
            with eng.Fori(1, B // 2 - 1) as i:
                for u in range(2):
                    one(2 * i + u, u, i, False, False)
            one(B - 2, 0, B // 2 - 1, False, False)
            one(B - 1, 1, B // 2 - 1, False, True)

        @block.sync
        def _(sp):
            for n, t in enumerate((wq, wk, wv, wo)):
                sp.dma_start(t[:, :], c["at1_w"][n, :, :]).then_inc(const_in, 16)
            sp.dma_start(cols[:, :], c["at1_cols"]).then_inc(const_in, 16)
            sp.dma_start(bo[:, :], c["at1_bo"]).then_inc(const_in, 16)

            def store(b, u, i, first, last):
                rows = window_rows[bass.ds(b * NW * WP, NW * WP), :]
                sp.wait_ge(biased, b + 1)
                full = (NGR - 1) * P
                sp.dma_start(rows[0:full, :].rearrange("(n p) e -> p n e", p=P), y[u][:, 0:NGR - 1, :])\
                  .then_inc(stored[u], 16)
                sp.dma_start(rows[full:NW * WP, :], y[u][0:NW * WP - full, NGR - 1, :]).then_inc(stored[u], 16)

            images(sp, store)
            for u in range(2):
                sp.wait_ge(stored[u], 32 * (B // 2))

        @block.gpsimd
        def _(pool):
            def spread_rows(b, u):
                wait_for(pool, y_ps, NGR * (b - 1))
                cols_ = turned_rows[:, bass.ds(b * L, NB * HOP + WP - HOP)]
                src = bass.AP(tensor=cols_.tensor, offset=cols_.offset, ap=[list(cols_.ap[0]), [HOP, NB], [1, WP]])
                pool.tensor_copy(xw[u][:, :, :], src).then_inc(spread, 1)

            def weigh(b, u, k):
                n, j0, nb = banks[k]
                pool.wait_ge(inverted, 3 * b + k + 1)
                part = pr[u][0:Q8, :, j0:j0 + nb, 0:WIN]
                pool.tensor_tensor(part, part, inv[0:Q8, :, j0:j0 + nb].unsqueeze(3).broadcast_to([Q8, 2, nb, WIN]),
                                   ALU.mult).then_inc(weighted, 1)

            def add_bias(b, u):
                pool.wait_ge(y_in, NGR * (b + 1))
                pool.tensor_tensor(y[u][:, :, :], y[u][:, :, :], bias[:, :].unsqueeze(1).broadcast_to([P, NGR, E]),
                                   ALU.add).then_inc(biased, 1)

            def one(b, u, i, first, last):
                if not first:
                    add_bias(b - 1, 1 - u)
                if not last:
                    spread_rows(b + 1, 1 - u)
                    for k in range(3):
                        weigh(b + 1, 1 - u, k)

            spread_rows(0, 0)
            for k in range(3):
                weigh(0, 0, k)
            pool.wait_ge(bias_in, 1)
            images(pool, one)
            add_bias(B - 1, 1)

        @block.tensor
        def _(pe):
            pe.wait_ge(const_in, 16 * 6)
            pe.wait_ge(cleared, NCLEAR)
            pe.wait_ge(bv_in, 1)
            pe.matmul(Y, bv[:, :], wo[:, :], start=True, stop=True).then_inc(bias_ps, 1)

            def project(b):
                wait_for(pe, shifted, 3 * b)
                src = turned_rows[:, bass.ds(b * L, L)]
                pe.matmul(bank[:, 0, 0:L], wk[:, :], src, start=True, stop=True).then_inc(qk_ps, 1)
                pe.matmul(bank[:, 1, 0:L], wq[:, :], src, start=True, stop=True).then_inc(qk_ps, 1)

            def score(b, u, k):
                pe.wait_ge(masked, NH * (b + 1))
                pe.wait_ge(k_in, b + 1)
                n, j0, nb = banks[k]
                for j in range(j0, j0 + nb):
                    last = pe.matmul(bank[0:Q8, n, 3 * HOP * (j - j0):3 * HOP * (j - j0) + 8 * HOP],
                                     qm[u][:, j, :, :], kx[u][:, HOP * j:HOP * (j + 8)], start=True, stop=True)
                last.then_inc(scored, 1)

            def turn(b, u, n):
                m = NGR * b + n
                pe.wait_ge(spread, b + 1)
                pe.wait_ge(weighted, 3 * (b + 1) if n >= 5 else 3 * b + (1 if n < 2 else 2))
                wait_for(pe, pt_in, 2 * m)
                wait_for(pe, vb_in, GW * m)
                pe.matmul(V, xw[u][:, GW * n:GW * (n + 1), :], wv[:, :], start=True, stop=True)
                pe.transpose(PT[:, 0, :], pr[u][0:Q8, 0, GW * n + 1:GW * n + 5, :], c["ident"][0:Q8, 0:Q8])
                pe.transpose(PT[:, 1, :], pr[u][0:Q8, 1, GW * n:GW * n + 4, :], c["ident"][0:Q8, 0:Q8])\
                  .then_inc(vt_ps, 1)

            def attend(b, n):
                m = NGR * b + n
                pe.wait_ge(pt_in, 2 * (m + 1))
                pe.wait_ge(vb_in, GW * (m + 1))
                for t in range(2):
                    wait_for(pe, om_in, 2 * m - 1 + t if not isinstance(m, int) or m else 0)
                    pe.matmul(AV[0:Q8, t, :, :], pt[n % 2][:, t, :, :, :], vb[n % 2][:, t, :, :],
                              start=True, stop=True).then_inc(av_ps, 1)

            def turn_heads(b, n):
                m = NGR * b + n
                pe.wait_ge(om_in, 2 * (m + 1))
                wait_for(pe, ot_in, m)
                for w in range(GW):
                    last = pe.transpose(OT[:, w, :], om[0:Q8, w, :], c["ident"][0:Q8, 0:Q8])
                last.then_inc(ot_ps, 1)

            def project_out(b, u, n):
                m = NGR * b + n
                pe.wait_ge(ot_in, m + 1)
                wait_for(pe, y_in, m)
                if isinstance(m, int) and m == 0:
                    pe.wait_ge(bias_in, 1)
                pe.matmul(Y, xw[u][:, GW * n:GW * (n + 1), :], c["ident"][:, :], start=True, stop=False)
                pe.matmul(Y, ot[:, :, :], wo[:, :], start=False, stop=True).then_inc(y_ps, 1)

            def one(b, u, i, first, last):
                for n in range(NGR):
                    attend(b, n)
                    if n < NGR - 1:
                        turn(b, u, n + 1)
                    elif not last:
                        turn(b + 1, 1 - u, 0)
                    if n == 1 and not last:
                        project(b + 1)
                    if 4 <= n < 7 and not last:
                        score(b + 1, 1 - u, n - 4)
                    if n:
                        project_out(b, u, n - 1)
                    elif not first:
                        project_out(b - 1, 1 - u, NGR - 1)
                    turn_heads(b, n)

            project(0)
            for k in range(3):
                score(0, 0, k)
            turn(0, 0, 0)
            images(pe, one)
            project_out(B - 1, 1, NGR - 1)

        @block.scalar
        def _(act):
            act.wait_ge(const_in, 16 * 6)
            act.wait_ge(cleared, NCLEAR)

            def keys(b, u):
                act.wait_ge(qk_ps, 2 * b + 1)
                wait_for(act, scored, 3 * (b - 1))
                act.activation(kx[u][:, HOP:HOP + L], bank[:, 0, 0:L], ACT.Identity, bias=cols[:, 1:2])\
                   .then_inc(k_in, 1)

            def raise_scores(b, u, k):
                for n, j0, nb in banks[k:k + 1]:
                    act.wait_ge(shifted, 3 * b + n + 1)
                    act.activation(pr[u][0:Q8, :, j0:j0 + nb, 0:WIN], pr[u][0:Q8, :, j0:j0 + nb, 0:WIN], ACT.Exp)\
                       .then_inc(raised, 1)

            def evacuate(b, n):
                m = NGR * b + n
                act.wait_ge(vt_ps, m + 1)
                wait_for(act, av_ps, 2 * (m - 1))
                for a in range(2):
                    act.activation(pt[n % 2][:, :, :, 1 - a, :],
                                   PT[:, a, :].rearrange("p (t g q) -> p t g q", t=2, q=HOP), ACT.Copy)\
                       .then_inc(pt_in, 1)
                for w in range(GW):
                    rows = slice(WP * w, WP * w + WP)
                    act.activation(vb[n % 2][rows, :, w, :], V[rows, :].rearrange("p (t k) -> p t k", t=2),
                                   ACT.Copy).then_inc(vb_in, 1)

            def keep(b, u, i, n):
                m = NGR * b + n
                act.wait_ge(y_ps, m + 1)
                if n == 0:
                    wait_for(act, stored[u], 32 * i)
                act.activation(y[u][:, n, :], Y, ACT.Copy).then_inc(y_in, 1)

            def one(b, u, i, first, last):
                for n in range(NGR):
                    if n < NGR - 1:
                        evacuate(b, n + 1)
                    elif not last:
                        evacuate(b + 1, 0)
                    if n:
                        keep(b, u, i, n - 1)
                    elif not first:
                        keep(b - 1, 1 - u, i - 1 + u, NGR - 1)
                    if n == 1 and not last:
                        keys(b + 1, 1 - u)
                    if 4 <= n < 7 and not last:
                        raise_scores(b + 1, 1 - u, n - 4)

            keys(0, 0)
            for k in range(3):
                raise_scores(0, 0, k)
            evacuate(0, 0)
            images(act, one)
            keep(B - 1, 1, B // 2 - 1, NGR - 1)

        @block.vector
        def _(dve):
            for t in kx:
                dve.memset(t[:, :], 0.0).then_inc(cleared, 1)
            for t in (om, ot):
                dve.memset(t[:, :, :], 0.0).then_inc(cleared, 1)
            for t in vb + pr:
                dve.memset(t[:, :, :, :], 0.0).then_inc(cleared, 1)
            dve.wait_ge(cleared, NCLEAR)
            dve.wait_ge(const_in, 16 * 6)
            dve.tensor_copy(bv[:, :], cols[:, 2:3].broadcast_to([P, P])).then_inc(bv_in, 1)
            dve.wait_ge(bias_ps, 1)
            dve.tensor_tensor(bias[:, :], Y, bo[:, :], ALU.add).then_inc(bias_in, 1)

            def mask(b, u, heads):
                if 0 in heads:
                    dve.wait_ge(qk_ps, 2 * b + 2)
                    wait_for(dve, masked, NH * b)
                    dve.tensor_scalar(qs[:, :], bank[:, 1, 0:NB * HOP], cols[:, 0:1], HD ** -0.5, ALU.add, ALU.mult)\
                       .then_inc(q_in, 1)
                    dve.wait_ge(q_in, b + 1)
                    wait_for(dve, scored, 3 * (b - 1))
                for n in heads:
                    dve.tensor_scalar(qm[u][:, :, n, :], qs[:, :].rearrange("p (j q) -> p j q", q=HOP),
                                      cols[:, 3 + n:4 + n], None, ALU.mult).then_inc(masked, 1)

            def softmax(b, u, k):
                if k == 0:
                    wait_for(dve, vt_ps, NGR * (b - 1))
                n, j0, nb = banks[k]
                sc = bank[0:Q8, n, 0:3 * HOP * nb].rearrange("p (j k q) -> p j k q", k=3, q=HOP)
                dve.wait_ge(scored, 3 * b + n + 1)
                wait_for(dve, maxed, 3 * b + n)
                dve.tensor_reduce(bm[0:Q8, j0:j0 + nb, :], sc, AX_X, ALU.max).then_inc(blocked, 1)
                dve.wait_ge(blocked, 3 * b + n + 1)
                wait_for(dve, shifted, 3 * b + n)
                dve.tensor_tensor(mx[0:Q8, j0:j0 + nb, :], bm[0:Q8, j0:j0 + nb, 0:2], bm[0:Q8, j0:j0 + nb, 1:3],
                                  ALU.max).then_inc(maxed, 1)
                dve.wait_ge(maxed, 3 * b + n + 1)
                base = bank[0:Q8, n, 0:3 * HOP * nb]
                both = bass.AP(tensor=base.tensor, offset=base.offset,
                               ap=[list(base.ap[0]), [HOP, 2], [3 * HOP, nb], [1, WIN]])
                dve.tensor_tensor(pr[u][0:Q8, :, j0:j0 + nb, 0:WIN], both,
                                  mx[0:Q8, j0:j0 + nb, :].rearrange("p j a -> p a j").unsqueeze(3)
                                  .broadcast_to([Q8, 2, nb, WIN]), ALU.subtract).then_inc(shifted, 1)

            def total(b, u, k):
                n, j0, nb = banks[k]
                dve.wait_ge(raised, 3 * b + k + 1)
                dve.tensor_reduce(sums[0:Q8, :, j0:j0 + nb], pr[u][0:Q8, :, j0:j0 + nb, 0:WIN], AX_X, ALU.add)\
                   .then_inc(summed, 1)
                dve.wait_ge(summed, 3 * b + k + 1)
                wait_for(dve, weighted, 3 * (b - 1) + k + 1)
                dve.reciprocal(inv[0:Q8, :, j0:j0 + nb], sums[0:Q8, :, j0:j0 + nb]).then_inc(inverted, 1)

            own = cols[0:Q8, 3 + NH:3 + NH + HH].unsqueeze(1).unsqueeze(3).broadcast_to([Q8, GW, HH, HD])

            def mask_heads(b, n):
                m = NGR * b + n
                for t in range(2):
                    dve.wait_ge(av_ps, 2 * m + t + 1)
                    wait_for(dve, ot_ps, m)
                    dve.tensor_tensor(om[0:Q8, :, VC * t:VC * (t + 1)].rearrange("p w (g d) -> p w g d", g=HH),
                                      AV[0:Q8, t, :, :].rearrange("p w (g d) -> p w g d", g=HH), own,
                                      ALU.mult).then_inc(om_in, 1)

            def add_heads(b, n):
                m = NGR * b + n
                dve.wait_ge(ot_ps, m + 1)
                wait_for(dve, y_ps, m)
                dve.tensor_reduce(ot[:, :, 0:WIN], OT.rearrange("p w (g q) -> p w q g", g=HH), AX_X, ALU.add)\
                   .then_inc(ot_in, 1)

            def one(b, u, i, first, last):
                for n in range(NGR):
                    mask_heads(b, n)
                    if 1 <= n < 4 and not last:
                        mask(b + 1, 1 - u, range(3 * (n - 1), min(3 * n, NH)))
                    if 4 <= n < 7 and not last:
                        softmax(b + 1, 1 - u, n - 4)
                    add_heads(b, n)
                    if 5 <= n < 8 and not last:
                        total(b + 1, 1 - u, n - 5)

            mask(0, 0, range(NH))
            for k in range(3):
                softmax(0, 0, k)
                total(0, 0, k)
            images(dve, one)


def combine_windows(nc, h, h_keep, mean, rstd, window_rows, stats):
    T = HOP // 2
    TAIL = NT - T * NB
    with Scope(nc, "comb") as s:
        wa, wb_ = ([s.sb(f"{n}{u}", [P, T * E]) for u in range(2)] for n in ("a", "b"))
        x = [s.sb(f"x{u}", [P, T * E]) for u in range(2)]
        t1 = [s.sb(f"t{u}", [P, T * E]) for u in range(2)]
        h_in = s.sem("h_in")
        a_in, b_in = ([s.sem(f"{n}_in{u}") for u in range(2)] for n in ("a", "b"))
        summed, normed, kept, halved, added, counted = (s.sem(n) for n in ("summed", "normed", "kept", "halved", "added", "counted"))
        block = s.block()
        PARTS = 8
        q = NT // PARTS + 1

        def load(eng, buf, sem, window, row0, b_):
            for pp in range(2):
                src = window_rows[bass.ds(window * B * WP, B * WP), :].rearrange("(b w) e -> b w e", w=WP)
                src = src[:, row0:row0 + HOP, :].rearrange("b (t k) e -> b k t e", k=2)[:, pp, :, :]
                eng.dma_start(buf[pp * B:(pp + 1) * B, :].rearrange("p (t e) -> p t e", e=E), src).then_inc(sem, 16)

        def blocks(eng, one):
            one(0, 0, 0)
            one(1, 1, 0)
            with eng.Fori(1, NB // 2 - 1) as i:
                for u in range(2):
                    one(2 * i + u, u, i)
            one(NB - 2, 0, NB // 2 - 1)
            one(NB - 1, 1, NB // 2 - 1)

        def has(k, window):
            return not (isinstance(k, int) and k == (NB - 1 if window == "a" else 0))

        @block.scalar
        def _(act):
            for n in range(PARTS):
                lo, hi = n * q, min(NT, (n + 1) * q)
                act.dma_start(h[:, lo * E:hi * E].rearrange("p (t e) -> p t e", e=E),
                              h_keep[lo * P:hi * P, :].rearrange("(t p) e -> p t e", p=P)).then_inc(h_in, 16)

        @block.sync
        def _(sp):
            def one(k, u, i):
                if has(k, "a"):
                    wait_for(sp, halved, k - 1)
                    load(sp, wa[u], a_in[u], k, 0, k)
                if has(k, "b"):
                    wait_for(sp, halved, k - 1)
                    load(sp, wb_[u], b_in[u], k - 1, HOP, k)
            blocks(sp, one)

        @block.gpsimd
        def _(pool):
            def one(k, u, i):
                if has(k, "a") and has(k, "b"):
                    pool.wait_ge(a_in[u], 32 * (i + 1))
                    pool.wait_ge(b_in[u], 32 * (i + u))
                    wait_for(pool, halved, k - 1)
                    pool.tensor_tensor(t1[u][:, :], wa[u][:, :], wb_[u][:, :], ALU.add).then_inc(summed, 1)
            blocks(pool, one)

        @block.vector
        def _(dve):
            dve.wait_ge(h_in, 16 * PARTS)

            def norms(j0, n, x_, before):
                for t in range(n):
                    dve.tensor_scalar(x_[:, t * E:(t + 1) * E], tile_of(h, j0 + t), mean[:, bass.ds(j0 + t, 1)],
                                      rstd[:, bass.ds(j0 + t, 1)], ALU.subtract, ALU.mult).then_inc(normed, 1)
                dve.wait_ge(normed, before + n)
                hh = h[:, bass.ds(j0 * E, n * E)]
                dve.tensor_tensor(hh, hh, x_[:, 0:n * E], ALU.add).then_inc(kept, 1)

            def one(k, u, i):
                wait_for(dve, halved, k)
                norms(k * T, T, x[u], k * T)
                dve.wait_ge(kept, k + 1)
                hh = h[:, bass.ds(k * T * E, T * E)]
                if has(k, "a") and has(k, "b"):
                    dve.wait_ge(summed, k)
                    ins = dve.scalar_tensor_tensor(out=hh, in0=t1[u][:, :], scalar=0.5, in1=hh, op0=ALU.mult, op1=ALU.add)
                else:
                    only, sem = (wa, a_in) if has(k, "a") else (wb_, b_in)
                    dve.wait_ge(sem[u], 32 * (i + 1))
                    ins = dve.tensor_tensor(hh, only[u][:, :], hh, ALU.add)
                ins.then_inc(halved, 1)
                dve.wait_ge(halved, k + 1)
                for t in range(T):
                    dve.bn_stats(stats[:, bass.ds((k * T + t) * 6, 6)], tile_of(h, k * T + t)).then_inc(counted, 1)

            blocks(dve, one)
            norms(NB * T, TAIL, x[0], NB * T)
            dve.wait_ge(kept, NB + 1)
            for t in range(TAIL):
                j = NB * T + t
                dve.bn_stats(stats[:, j * 6:j * 6 + 6], tile_of(h, j)).then_inc(counted, 1)


NE1 = 32
CAP = TOK // NE1
GE = 4
XG = E + NE1
HALF = L // 2
LO = 41
HI = 16
SLOTS = HI * LO


def expert_softmax(nc, logits, rows):
    with Scope(nc, "sm1") as s:
        mx, sm, inv = s.sb("mx", [P, NT]), s.sb("sm", [P, NT]), s.sb("inv", [P, NT])
        step, raised, stored = s.sem("step"), s.sem("raised"), s.sem("stored")
        block = s.block()
        lg = logits[:, :].rearrange("p (t e) -> p t e", e=NE1)
        wide = lambda a: a[:, :].unsqueeze(2).broadcast_to([P, NT, NE1])
        PARTS = 6
        q = NT // PARTS

        @block.vector
        def _(dve):
            n = [0]

            def link(ins):
                n[0] += 1
                ins.then_inc(step, 1)
                dve.wait_ge(step, n[0])

            link(dve.tensor_reduce(mx[:, :], lg, AX_X, ALU.max))
            link(dve.tensor_tensor(lg, lg, wide(mx), ALU.subtract))
            dve.wait_ge(raised, 1)
            link(dve.tensor_reduce(sm[:, :], lg, AX_X, ALU.add))
            link(dve.reciprocal(inv[:, :], sm[:, :]))
            link(dve.tensor_tensor(lg, lg, wide(inv), ALU.mult))

        @block.scalar
        def _(act):
            act.wait_ge(step, 2)
            act.activation(logits[:, :], logits[:, :], ACT.Exp).then_inc(raised, 1)

        @block.sync
        def _(sp):
            sp.wait_ge(step, 5)
            for k in range(PARTS):
                sp.dma_start(rows[k * q * P:(k + 1) * q * P, E:XG].rearrange("(t p) e -> p t e", p=P),
                             lg[:, k * q:(k + 1) * q, :]).then_inc(stored, 16)
            sp.wait_ge(stored, 16 * PARTS)


def choose_tokens(nc, c, rows, slot):
    N = HALF * NE1
    BITS = 30
    with Scope(nc, "top") as s:
        val, cum = s.sb("val", [P, N]), s.sb("cum", [P, N])
        sel, eq = s.sb("sel", [P, N]), s.sb("eq", [P, N])
        mask = s.sb("mask", [P, N], BF16)
        zero = s.sb("zero", [P, N], BF16)
        tri, ones = s.sb("tri", [P, P], BF16), s.sb("ones", [P, P], BF16)
        low, cand, take, bit = (s.sb(n, [P, NE1], I32) for n in ("low", "cand", "take", "bit"))
        cnt, need, first, base = (s.sb(n, [P, NE1]) for n in ("cnt", "need", "first", "base"))
        own = s.sb("own", [P, NE1])
        own16 = s.sb("own16", [P, 2 * NE1], BF16)
        total = s.ps("total", [P, 512])
        before = s.ps("before", [P, 512])
        val_in, consts, ready = s.sem("val_in"), s.sem("consts"), s.sem("ready")
        tried, masked, counted, step = s.sem("tried"), s.sem("masked"), s.sem("counted"), s.sem("step")
        own_in, prefixed = s.sem("own_in"), s.sem("prefixed")
        block = s.block()
        by_fe = lambda a: a[:, :].rearrange("p (f e) -> p f e", e=NE1)
        by_ef = lambda a: a[:, :].rearrange("p (e f) -> p e f", f=HALF)
        swapped = lambda a: by_fe(a).rearrange("p f e -> p e f")
        wide = lambda a: a.unsqueeze(1).broadcast_to([P, HALF, NE1])
        tall = lambda a: a.unsqueeze(2).broadcast_to([P, NE1, HALF])
        chunks = [(k, min(512, N - k)) for k in range(0, N, 512)]
        PARTS = 3
        third = HALF // PARTS

        @block.sync
        def _(sp):
            for half in range(2):
                for k in range(6):
                    q = HALF // 6
                    src = rows[(half * HALF + k * q) * B:(half * HALF + (k + 1) * q) * B, E:XG]
                    sp.dma_start(by_fe(val)[half::2, k * q:(k + 1) * q, :], src.rearrange("(f b) e -> b f e", b=B))\
                      .then_inc(val_in, 16)

        @block.gpsimd
        def _(pool):
            pool.memset(tri[:, :], 1.0).then_inc(consts, 1)
            pool.memset(ones[:, :], 1.0).then_inc(consts, 1)
            pool.wait_ge(consts, 2)
            pool.affine_select(out=tri[:, :], in_=tri[:, :], compare_op=ALU.is_gt, fill=0.0, base=0,
                               pattern=[[1, P]], channel_multiplier=-1).then_inc(consts, 1)

        @block.tensor
        def _(pe):
            pe.wait_ge(consts, 3)

            def count(n):
                wait_for(pe, counted, n)
                for k, w in chunks:
                    pe.wait_ge(masked, PARTS * n + min(PARTS, (k + w + third * NE1 - 1) // (third * NE1)))
                    last = pe.matmul(total[:, 0:w], ones[:, :], mask[:, k:k + w], start=(k == 0),
                                     stop=(k + w == N))
                last.then_inc(tried, 1)

            count(0)
            with pe.Fori(1, BITS) as n:
                count(n)
            count(BITS)
            for n in range(2):
                pe.wait_ge(own_in, n + 1)
                pe.matmul(before[:, 0:NE1], tri[:, :], own16[:, n * NE1:(n + 1) * NE1], start=True, stop=True).then_inc(prefixed, 1)

        @block.vector
        def _(dve):
            dve.memset(low[:, :], 0).then_inc(ready, 1)
            dve.memset(bit[:, :], 1 << (BITS - 1)).then_inc(ready, 1)
            dve.memset(zero[:, :], 0.0).then_inc(ready, 1)
            dve.memset(first[:, :], 0.0).then_inc(ready, 1)
            dve.wait_ge(ready, 4)
            dve.wait_ge(val_in, 16 * 12)
            STEPS = 5

            def compare(n, against, op):
                wait_for(dve, tried, n)
                for k in range(PARTS):
                    f = slice(k * third, (k + 1) * third)
                    dve.tensor_tensor(by_fe(mask)[:, f, :], by_fe(val)[:, f, :], wide(against)[:, f, :], op)\
                       .then_inc(masked, 1)

            def total_of(n):
                dve.wait_ge(tried, n + 1)
                dve.tensor_reduce(cnt[:, :], total[:, :].rearrange("p (f e) -> p e f", e=NE1), AX_X, ALU.add)\
                   .then_inc(counted, 1)
                dve.wait_ge(counted, n + 1)

            def one_bit(n):
                link = lambda k, ins: (ins.then_inc(step, 1), dve.wait_ge(step, STEPS * n + k))
                link(1, dve.tensor_tensor(cand[:, :], low[:, :], bit[:, :], ALU.bitwise_or))
                compare(n, cand[:, :].bitcast(F32), ALU.is_ge)
                total_of(n)
                link(2, dve.tensor_scalar(take[:, :], cnt[:, :], float(CAP), None, ALU.is_ge))
                link(3, dve.tensor_tensor(take[:, :], take[:, :], bit[:, :], ALU.mult))
                link(4, dve.tensor_tensor(low[:, :], low[:, :], take[:, :], ALU.bitwise_or))
                link(5, dve.tensor_scalar(bit[:, :], bit[:, :], 1, None, ALU.logical_shift_right))

            one_bit(0)
            with dve.Fori(1, BITS) as n:
                one_bit(n)

            m = [STEPS * BITS]

            def link(ins):
                m[0] += 1
                ins.then_inc(step, 1)
                dve.wait_ge(step, m[0])

            least = low[:, :].bitcast(F32)
            compare(BITS, least, ALU.is_gt)
            total_of(BITS)
            link(dve.tensor_scalar(need[:, :], cnt[:, :], -1.0, float(CAP), ALU.mult, ALU.add))
            link(dve.tensor_tensor(by_ef(eq), swapped(val), tall(least), ALU.is_equal))
            dve.wait_ge(masked, PARTS * (BITS + 1))
            link(dve.tensor_copy(by_ef(sel), swapped(mask)))

            def ranks(of, n):
                link(dve.tensor_tensor_scan(cum[:, :], of[:, :], zero[:, :], 0.0, ALU.add, ALU.add))
                link(dve.tensor_copy(first[:, 1:NE1], by_ef(cum)[:, 0:NE1 - 1, HALF - 1]))
                link(dve.tensor_tensor(own[:, :], by_ef(cum)[:, :, HALF - 1], first[:, :], ALU.subtract))
                dve.tensor_copy(own16[:, n * NE1:(n + 1) * NE1], own[:, :]).then_inc(own_in, 1)
                dve.wait_ge(prefixed, n + 1)
                link(dve.tensor_tensor(base[:, :], before[:, 0:NE1], first[:, :], ALU.subtract))
                link(dve.tensor_tensor(by_ef(cum), by_ef(cum), tall(base[:, :]), ALU.add))

            ranks(eq, 0)
            link(dve.tensor_tensor(by_ef(cum), by_ef(cum), tall(need[:, :]), ALU.is_le))
            link(dve.tensor_tensor(eq[:, :], eq[:, :], cum[:, :], ALU.mult))
            link(dve.tensor_tensor(sel[:, :], sel[:, :], eq[:, :], ALU.add))
            ranks(sel, 1)
            link(dve.tensor_scalar(sel[:, :], sel[:, :], -2.0 * SLOTS, 2.0 * SLOTS - 1, ALU.mult, ALU.add))
            link(dve.tensor_tensor(swapped(slot), by_ef(cum), by_ef(sel), ALU.add))


def list_tokens(nc, slot, lists):
    N = HALF * NE1
    NG = NE1 // GE
    FB = 2
    with Scope(nc, "list") as s:
        si, hi_i = s.sb("si", [P, N], I32), s.sb("hi_i", [P, N], I32)
        hi, lo = s.sb("hi", [P, N], BF16), s.sb("lo", [P, N], BF16)
        iota16, iota41, nf = s.sb("iota16", [P, HI]), s.sb("iota41", [P, LO]), s.sb("nf", [P, HALF])
        d16, d41, np_ = s.sb("d16", [P, HI], BF16), s.sb("d41", [P, LO], BF16), s.sb("np", [P, 1])
        hot = [s.sb(f"hot{u}", [P, FB, NE1, HI], BF16) for u in range(2)]
        left = [s.sb(f"left{u}", [P, FB, NG, 2, GE, HI], BF16) for u in range(2)]
        right = [s.sb(f"right{u}", [P, FB, NE1, LO], BF16) for u in range(2)]
        out = s.sb("out", [P, NG, GE * LO])
        acc = s.ps("acc", [P, NG, 512])
        consts, step, hot_in, left_in, right_in = (s.sem(n) for n in ("consts", "step", "hot_in", "left_in", "right_in"))
        product, out_in, stored = s.sem("product"), s.sem("out_in"), s.sem("stored")
        block = s.block()
        ng = HALF // FB

        def run(eng, one):
            for u in range(2):
                one(u, u)
            with eng.Fori(1, ng // 2) as i:
                for u in range(2):
                    one(2 * i + u, u)
            if ng % 2:
                one(ng - 1, 0)

        @block.gpsimd
        def _(pool):
            pool.iota(iota16[:, :], pattern=[[1, HI]], base=0, channel_multiplier=0,
                      allow_small_or_imprecise_dtypes=True).then_inc(consts, 1)
            pool.iota(iota41[:, :], pattern=[[1, LO]], base=0, channel_multiplier=0,
                      allow_small_or_imprecise_dtypes=True).then_inc(consts, 1)
            pool.iota(nf[:, :], pattern=[[1, HALF]], base=0, channel_multiplier=0,
                      allow_small_or_imprecise_dtypes=True).then_inc(consts, 1)
            pool.iota(np_[:, :], pattern=[[0, 1]], base=0, channel_multiplier=1,
                      allow_small_or_imprecise_dtypes=True).then_inc(consts, 1)

        @block.vector
        def _(dve):
            dve.wait_ge(consts, 4)
            n = [0]

            def link(ins):
                n[0] += 1
                ins.then_inc(step, 1)
                dve.wait_ge(step, n[0])

            link(dve.tensor_copy(d16[:, :], iota16[:, :]))
            link(dve.tensor_copy(d41[:, :], iota41[:, :]))
            link(dve.tensor_scalar(si[:, :], slot[:, :], 1599.0, None, ALU.mult))
            link(dve.tensor_scalar(hi_i[:, :], si[:, :], 16, None, ALU.logical_shift_right))
            link(dve.tensor_copy(hi[:, :], hi_i[:, :]))
            link(dve.scalar_tensor_tensor(out=lo[:, :], in0=hi_i[:, :], scalar=-float(LO), in1=slot[:, :],
                                          op0=ALU.mult, op1=ALU.add))

            def one(g, u):
                wait_for(dve, left_in, g - 1)
                wait_for(dve, product, g - 1)
                h_ = hi[:, bass.ds(g * FB * NE1, FB * NE1)].unsqueeze(2).broadcast_to([P, FB * NE1, HI])
                l_ = lo[:, bass.ds(g * FB * NE1, FB * NE1)].unsqueeze(2).broadcast_to([P, FB * NE1, LO])
                flat = lambda t: t[:, :, :, :].rearrange("p f e d -> p (f e) d")
                dve.tensor_tensor(flat(hot[u]), h_, d16[:, :].unsqueeze(1).broadcast_to([P, FB * NE1, HI]),
                                  ALU.is_equal).then_inc(hot_in, 1)
                dve.tensor_tensor(flat(right[u]), l_, d41[:, :].unsqueeze(1).broadcast_to([P, FB * NE1, LO]),
                                  ALU.is_equal).then_inc(right_in, 1)
            run(dve, one)
            dve.wait_ge(product, ng)
            dve.tensor_copy(out[:, :, :], acc[:, :, 0:GE * LO]).then_inc(out_in, 1)

        @block.scalar
        def _(act):
            act.wait_ge(consts, 4)

            def one(g, u):
                act.wait_ge(hot_in, g + 1)
                wait_for(act, product, g - 1)
                src = hot[u][:, :, :, :].rearrange("p f (g e) d -> p (f g) (e d)", g=NG)
                dst = left[u][:, :, :, :, :, :].rearrange("p f g a e d -> p (f g) a (e d)")
                act.activation(dst[:, :, 0, :], src, ACT.Copy, scale=np_[:, 0:1])
                for f in range(FB):
                    src = hot[u][:, f, :, :].rearrange("p (g e) d -> p g (e d)", g=NG)
                    dst = left[u][:, f, :, 1, :, :].rearrange("p g e d -> p g (e d)")
                    last = act.activation(dst, src, ACT.Copy, scale=nf[:, bass.ds(g * FB + f, 1)])
                last.then_inc(left_in, 1)
            run(act, one)

        @block.tensor
        def _(pe):
            def one(g, u, first=False, last_=False):
                pe.wait_ge(left_in, g + 1)
                pe.wait_ge(right_in, g + 1)
                for f in range(FB):
                    for m in range(NG):
                        last = pe.matmul(acc[:, m, 0:GE * LO],
                                         left[u][:, f, m, :, :, :].rearrange("p a e d -> p (a e d)"),
                                         right[u][:, f, GE * m:GE * (m + 1), :].rearrange("p e d -> p (e d)"),
                                         start=first and f == 0, stop=last_ and f == FB - 1)
                last.then_inc(product, 1)
            one(0, 0, True)
            one(1, 1)
            with pe.Fori(1, (ng - 1) // 2) as i:
                for u in range(2):
                    one(2 * i + u, u)
            for g in range(2 * ((ng - 1) // 2), ng):
                one(g, g % 2, False, g == ng - 1)

        @block.sync
        def _(sp):
            sp.wait_ge(out_in, 1)
            for a in range(2):
                for e in range(GE):
                    r0 = (a * GE + e) * HI
                    dst = lists[a, :, :].rearrange("(g e) (d l) -> e d g l", e=GE, l=LO)[e, :, :, :]
                    sp.dma_start(dst, out[r0:r0 + HI, :, e * LO:(e + 1) * LO]).then_inc(stored, 16)
            sp.wait_ge(stored, 16 * 2 * GE)


RC = 108
NC = CAP // RC
D1 = 341
D1C = 3
LASTC = 96
WU = 2 * P + LASTC
WE = WU + D1C


def list_rows(nc, c, lists, index):
    R = NE1 * NC // 2
    with Scope(nc, "lrow") as s:
        q, f = s.sb("q", [R, 2, RC]), s.sb("f", [R, 2, RC])
        qi, odd = s.sb("qi", [R, 2, RC], I32), s.sb("odd", [R, 2, RC], I32)
        ps = s.ps("ps", [P, 2, 512])
        loaded, step, turned = s.sem("loaded"), s.sem("step"), s.sem("turned")
        block = s.block()

        @block.sync
        def _(sp):
            for a, t in enumerate((q, f)):
                for m in range(2):
                    for e in range(NE1 // 2):
                        src = lists[a, m * (NE1 // 2) + e, 0:CAP].rearrange("(n r) -> n r", r=RC)
                        sp.dma_start(t[e * NC:(e + 1) * NC, m, :], src).then_inc(loaded, 16)

        @block.vector
        def _(dve):
            n = [0]

            def link(ins):
                n[0] += 1
                ins.then_inc(step, 1)
                dve.wait_ge(step, n[0])

            dve.wait_ge(loaded, 16 * 2 * NE1)
            link(dve.tensor_copy(qi[:, :, :], q[:, :, :]))
            link(dve.tensor_scalar(odd[:, :, :], qi[:, :, :], 1, None, ALU.bitwise_and))
            link(dve.tensor_scalar(qi[:, :, :], qi[:, :, :], 1, None, ALU.logical_shift_right))
            link(dve.tensor_copy(q[:, :, :], odd[:, :, :]))
            link(dve.scalar_tensor_tensor(out=f[:, :, :], in0=f[:, :, :], scalar=float(B), in1=qi[:, :, :],
                                          op0=ALU.mult, op1=ALU.add))
            link(dve.scalar_tensor_tensor(out=f[:, :, :], in0=q[:, :, :], scalar=float(HALF * B), in1=f[:, :, :],
                                          op0=ALU.mult, op1=ALU.add))
            dve.wait_ge(turned, 1)
            link(dve.tensor_copy(index[0:RC, :].rearrange("p (m k) -> p m k", m=2), ps[0:RC, :, 0:R]))

        @block.tensor
        def _(pe):
            pe.wait_ge(step, 6)
            for m in range(2):
                last = pe.transpose(ps[0:RC, m, 0:R], f[:, m, :], c["ident"][0:R, 0:R])
            last.then_inc(turned, 1)


def expert_choice_ffn(nc, c, index, rows, out):
    H3 = NC // 2
    N = H3 * RC
    UPG = 2 * GE
    XB = UPG
    with Scope(nc, "ffn1") as s:
        wu = [s.sb(f"wu{u}", [P, WE]) for u in range(2)]
        wd = [s.sb(f"wd{u}", [P, D1C * E]) for u in range(2)]
        at = [[s.sb(f"at{u}_{r}", [RC, 1], U32) for r in range(H3)] for u in range(XB)]
        x = [s.sb(f"x{u}", [RC, H3, XG]) for u in range(XB)]
        xt = [s.sb(f"xt{u}", [P, N]) for u in range(2)]
        hid = [s.sb(f"hid{u}", [P, D1C, N]) for u in range(2)]
        y = [s.sb(f"y{u}", [RC, H3, E]) for u in range(2)]
        up = [s.ps(f"up{u}", [P, D1C, 512]) for u in range(2)]
        xps, yps = s.ps("xps", [P, 512]), s.ps("yps", [P, 512])
        w_in = [s.sem(f"w_in{u}") for u in range(2)]
        got = [s.sem(f"got{u}") for u in range(XB)]
        sent = [s.sem(f"sent{par}") for par in range(2)]
        index_in, issued = s.sem("index_in"), s.sem("issued")
        primed, ones_set = s.sem("primed"), s.sem("ones_set")
        turned, xt_in, upped, raised, downed, y_in = (s.sem(n) for n in ("turned", "xt_in", "upped", "raised", "downed", "y_in"))
        block = s.block()
        GROUPS = NE1 // GE

        def run(eng, one):
            for c_ in range(UPG):
                one(0, c_)
            with eng.Fori(1, GROUPS - 1) as i:
                for c_ in range(UPG):
                    one(i, c_)
            for c_ in range(UPG):
                one(GROUPS - 1, c_)

        def unit(i, c_, ahead):
            return neighbour(i, c_, ahead, UPG, GROUPS)

        @block.sync
        def _(sp):
            def one(i, c_):
                if c_ % 2:
                    return
                v = c_ // 2
                u = v % 2
                wait_for(sp, downed, UPG * i + c_ - 2)
                sp.dma_start(wu[u][:, :], c["ffn1_wu"][bass.ds(i * P, P), :]).then_inc(w_in[u], 16)
                sp.dma_start(wd[u][:, :], c["ffn1_wd"][bass.ds((i * GE + v) * P, P), :]).then_inc(w_in[u], 16)
            run(sp, one)

        @block.gpsimd
        def _(pool):
            def gather(i, c_):
                pool.wait_ge(index_in, H3 * (UPG * i + c_ + 1))
                pool.sem_inc(issued, 1)
                for r in range(H3):
                    pool.indirect_dma_start(out=x[c_][:, r, :], out_offset=None, in_=rows[:, :],
                                            in_offset=bass.IndirectOffsetOnAxis(ap=at[c_][r][:, 0:1], axis=0))\
                        .then_inc(got[c_], 16)

            def one(i, c_):
                nxt = unit(i, c_, XB - 3)
                if nxt:
                    gather(*nxt)
                k = UPG * i + c_
                pool.wait_ge(y_in, k + 1)
                if c_ % 2 == 0:
                    for par in range(2):
                        wait_for(pool, sent[par], 16 * H3 * (GE * i + c_ // 2))
                pool.sem_inc(issued, 1)
                for r in range(H3):
                    pool.indirect_dma_start(out=out[:, :],
                                            out_offset=bass.IndirectOffsetOnAxis(ap=at[c_][r][:, 0:1], axis=0),
                                            in_=y[c_ % 2][:, r, :], in_offset=None, compute_op=ALU.add)\
                        .then_inc(sent[c_ % 2], 16)

            for c_ in range(XB - 3):
                gather(0, c_)
            run(pool, one)
            for par in range(2):
                pool.wait_ge(sent[par], 16 * H3 * NE1)

        @block.tensor
        def _(pe):
            pe.wait_ge(ones_set, 2)

            def turn(i, c_):
                k = UPG * i + c_
                pe.wait_ge(got[c_], 16 * H3 * (i + 1))
                wait_for(pe, xt_in, k)
                for r in range(H3):
                    last = pe.transpose(xps[:, r * RC:(r + 1) * RC], x[c_][:, r, 0:E], c["ident"][0:RC, 0:RC])
                last.then_inc(turned, 1)

            def widen(i, c_):
                k = UPG * i + c_
                v = c_ // 2
                pe.wait_ge(w_in[v % 2], 32 * (2 * i + v // 2 + 1))
                pe.wait_ge(xt_in, k + 1)
                wait_for(pe, raised, D1C * (k - 1))
                for m in range(D1C):
                    M = P if m < D1C - 1 else LASTC
                    pe.matmul(up[c_ % 2][0:M, m, 0:N], wu[v % 2][:, m * P:m * P + M], xt[c_ % 2][:, :],
                              start=True, stop=True).then_inc(upped, 1)

            def narrow(i, c_):
                k = UPG * i + c_
                u = c_ // 2 % 2
                pe.wait_ge(raised, D1C * (k + 1))
                wait_for(pe, y_in, k)
                for r in range(H3):
                    for m in range(D1C):
                        last = pe.matmul(yps[0:RC, r * E:(r + 1) * E], hid[c_ % 2][:, m, r * RC:(r + 1) * RC],
                                         wd[u][:, m * E:(m + 1) * E], start=(m == 0), stop=(m == D1C - 1))
                last.then_inc(downed, 1)

            def one(i, c_):
                widen(i, c_)
                nxt, before = unit(i, c_, 1), unit(i, c_, -1)
                if nxt:
                    turn(*nxt)
                if before:
                    narrow(*before)

            turn(0, 0)
            run(pe, one)
            narrow(GROUPS - 1, UPG - 1)

        @block.scalar
        def _(act):
            def one(i, c_):
                k = UPG * i + c_
                u = c_ // 2 % 2
                wait_for(act, downed, k - 1)
                for m in range(D1C):
                    M = P if m < D1C - 1 else LASTC
                    act.wait_ge(upped, D1C * k + m + 1)
                    act.activation(hid[c_ % 2][0:M, m, :], up[c_ % 2][0:M, m, 0:N], ACT.Silu,
                                   bias=wu[u][0:M, WU + m:WU + m + 1]).then_inc(raised, 1)
            act.wait_ge(ones_set, 2)
            run(act, one)

        @block.vector
        def _(dve):
            for u in range(2):
                dve.memset(hid[u][LASTC:P, D1C - 1, :], 0.0).then_inc(primed, 1)
            dve.wait_ge(primed, 2)
            for u in range(2):
                dve.memset(hid[u][LASTC:LASTC + 1, D1C - 1, :], 1.0).then_inc(ones_set, 1)

            def indices(i, c_):
                for r in range(H3):
                    dve.tensor_copy(at[c_][r][:, :],
                                    index[0:RC, bass.ds((UPG * i + c_) * H3 + r, 1)]).then_inc(index_in, 1)

            def one(i, c_):
                k = UPG * i + c_
                dve.wait_ge(turned, k + 1)
                wait_for(dve, upped, D1C * (k - 1))
                dve.tensor_copy(xt[c_ % 2][:, :], xps[:, 0:N]).then_inc(xt_in, 1)
                before = unit(i, c_, -1)
                if before:
                    finish(*before)

            def finish(i, c_):
                k = UPG * i + c_
                dve.wait_ge(downed, k + 1)
                wait_for(dve, sent[c_ % 2], 16 * H3 * (GE * i + c_ // 2))
                g = x[c_][:, :, bass.ds(E + GE * i + c_ // 2, 1)].broadcast_to([RC, H3, E])
                dve.tensor_tensor(y[c_ % 2][:, :, :], yps[0:RC, 0:H3 * E].rearrange("p (r e) -> p r e", e=E), g,
                                  ALU.mult).then_inc(y_in, 1)
                ahead = unit(i, c_, XB - 2)
                if ahead and unit(i, c_, -2):
                    indices(*ahead)

            for c_ in range(XB):
                indices(0, c_)
            run(dve, one)
            finish(GROUPS - 1, UPG - 1)
def early_fusion(nc, ap, out):
    dram = lambda name, shape: nc.dram_tensor(name, shape, F32).ap()
    sorted_rows, token_out = dram("sorted_rows", [NFT * FT, XS]), dram("token_out", [TOK + BLANK, E])
    h_keep, window_rows = dram("h_keep", [TOK, E]), dram("window_rows", [B * NW * WP, E])
    expert_rows, lists = dram("expert_rows", [TOK, XG]), dram("lists", [2, NE1, SLOTS])
    with Scope(nc, "all") as s:
        ident, stats = s.sb("ident", [P, P]), s.sb("stats", [P, NT * 6])
        mean, rstd, rstd2 = (s.sb(n, [P, NT]) for n in ("mean", "rstd", "rstd2"))
        make_identity(nc, ident)
        c = dict(ap)
        c["ident"] = ident
        with Scope(nc, "wide") as wide:
            turned_rows = wide.sb("turned_rows", [P, NTC])
            with Scope(nc, "front") as front:
                h = front.sb("h", [P, NT * E])
                embed_tokens(nc, ap["patches"], ap["text"], ap["tok_w"], ap["tok_b"], h, stats)
                finish_statistics(nc, "ln0", stats, mean, rstd)
                image_attention(nc, c, h, stats, mean, rstd, turned_rows, sorted_rows)
                with Scope(nc, "route") as r:
                    logits, ratio = r.sb("logits", [P, NT * NE0]), r.sb("ratio", [P, NT])
                    dest, tile_expert = r.sb("dest", [P, NT], U32), r.sb("tile_expert", [P, NFT], I32)
                    finish_statistics(nc, "ln1", stats, mean, rstd)
                    token_logits(nc, "lg0", c, h, mean, rstd, ap["ffn0_r"], ap["ffn0_br"], NE0, logits)
                    route_top1(nc, c, logits, dest, ratio, tile_expert, turned_rows)
                    scatter_rows(nc, c, h, mean, rstd, dest, sorted_rows, turned_rows)
                    sorted_ffn(nc, c, tile_expert, sorted_rows, turned_rows, token_out)
                    add_rows(nc, h, ratio, token_out, stats)
                finish_statistics(nc, "ln2", stats, mean, rstd, rstd2)
                turn_rows(nc, c, h, mean, rstd2, turned_rows, h_keep)
            window_attention(nc, c, turned_rows, window_rows)
        clear_semaphores(nc)
        with Scope(nc, "back") as back:
            logits = back.sb("logits1", [P, NT * NE1])
            h = back.sb("h1", [P, NT * E])
            combine_windows(nc, h, h_keep, mean, rstd, window_rows, stats)
            finish_statistics(nc, "ln3", stats, mean, rstd)
            token_logits(nc, "lg1", c, h, mean, rstd, ap["ffn1_r"], ap["ffn1_br"], NE1, logits, expert_rows, out)
            expert_softmax(nc, logits, expert_rows)
        index = s.sb("index", [P, NE1 * NC], U32)
        with Scope(nc, "choice") as choice:
            slot = choice.sb("slot", [P, HALF * NE1])
            choose_tokens(nc, c, expert_rows, slot)
            list_tokens(nc, slot, lists)
        list_rows(nc, c, lists, index)
        expert_choice_ffn(nc, c, index, expert_rows, out)


def tables():
    r = np.arange(P)
    heads = (r[:, None] // HD == np.arange(NH)[None]).astype(np.float32)
    inv = (1.0 / (np.float32(10000.0) ** (np.arange(0, HD, 2, dtype=np.float32) / np.float32(HD)))).astype(np.float32)
    angle = np.arange(B, dtype=np.float32)[:, None] * inv[None]
    angle = np.concatenate([angle, angle], -1).T
    cos, sin = np.tile(np.cos(angle), (NH, 1)), np.tile(np.sin(angle), (NH, 1))
    sign = np.where(r % HD < HD // 2, -1, 1).astype(np.float32)[:, None]
    qs = np.float32(HD ** -0.5)
    same = (r[:, None] % B == np.arange(B)[None]).astype(np.float32)
    none = np.zeros_like(same)
    row_head = (r[:, None] // WIN == np.arange(NH // 2)[None]).astype(np.float32)
    row_head[NH * HOP:] = 0
    return {"heads": heads, "rope": np.concatenate([cos * qs, sin * sign * qs, cos, sin * sign], 1).astype(np.float32),
            "sel": np.concatenate([same, none, none, same], 1), "row_head": row_head,
            "falling": np.broadcast_to(NE0 - np.arange(NE0, dtype=np.float32), (P, NE0))}


def layouts(i):
    t = tables()
    rows = lambda v: np.broadcast_to(v, (P, v.shape[-1]))
    turned = lambda names: [i[n].T for n in names]
    rot = np.arange(E).reshape(NH, 2, HD // 2)[:, ::-1].reshape(-1)
    o = {k: t[k] for k in ("rope", "sel", "falling")}
    x = i["x"].reshape(B, 3, 14, 16, 14, 16).transpose(2, 4, 0, 1, 3, 5).reshape(NPATCH * B // P, P, KP, P)
    o["patches"] = x.transpose(0, 3, 2, 1).reshape(-1, KP * P)
    o["text"] = i["txt"].transpose(1, 0, 2).reshape(NTEXT * B // P, P, E)
    o["tok_w"] = i["L0_tok_w"].T.reshape(KP, P, E).transpose(1, 0, 2).reshape(P, KP * E)
    o["tok_b"] = rows(i["L0_tok_b"])
    wq, wk, wv, wo = (i[f"L0_attn_W{n}"] for n in "qkvo")
    bq, bk, bv = (i[f"L0_attn_b{n}"] for n in "qkv")
    o["at0_w"] = np.stack([wq.T, wq[rot].T, wk.T, wk[rot].T, wv.T, wo.T])
    o["at0_cols"] = np.concatenate([np.stack([bq, bq[rot], bk, bk[rot], bv], 1), t["heads"]], 1)
    o["at0_bo"] = rows(i["L0_attn_bo"])
    o["ffn0_r"] = np.pad(i["L0_ffn_Wr"], ((0, 0), (0, P - NE0)))
    o["ffn0_br"] = rows(i["L0_ffn_br"])
    w2 = i["L0_ffn_W2"].reshape(NE0, H0 // P, P, E).transpose(0, 2, 1, 3).reshape(NE0, P, H0)
    b1 = i["L0_ffn_b1"].reshape(NE0, H0 // P, P).transpose(0, 2, 1)
    b2 = np.broadcast_to(i["L0_ffn_b2"][:, None], (NE0, P, E))
    o["ffn0_wb"] = np.concatenate([i["L0_ffn_W1"], w2, b1, b2], 2).reshape(NE0 * P, WB0)
    w_in, b_in = i["L1_attn_w_in"].reshape(3, E, E), i["L1_attn_b_in"].reshape(3, E)
    o["at1_w"] = np.stack([w_in[0].T, w_in[1].T, w_in[2].T, i["L1_attn_w_out"].T])
    o["at1_cols"] = np.concatenate([b_in.T, t["heads"], t["row_head"]], 1)
    o["at1_bo"] = rows(i["L1_attn_b_out"])
    o["at1_gb"] = np.stack([i["L1_attn_ln_g"], i["L1_attn_ln_b"]], 1)
    o["ffn1_r"] = np.pad(i["L1_ffn_W_router"], ((0, 0), (0, P - NE1)))
    o["ffn1_br"] = rows(i["L1_ffn_b_router"])
    ng = NE1 // GE
    w_up = np.pad(i["L1_ffn_W_up"], ((0, 0), (0, 0), (0, WU - D1)))
    b_up = np.pad(i["L1_ffn_b_up"], ((0, 0), (0, D1C * P - D1))).reshape(ng, D1C, P).transpose(0, 2, 1)
    o["ffn1_wu"] = np.concatenate([w_up, b_up], 2).reshape(ng * P, WE)
    zeros = lambda n: np.zeros((NE1, n, E), np.float32)
    w_down = np.concatenate([i["L1_ffn_W_down"], zeros(WU - D1), i["L1_ffn_b_down"][:, None],
                             zeros(D1C * P - WU - 1)], 1)
    o["ffn1_wd"] = w_down.reshape(NE1, D1C, P, E).transpose(0, 2, 1, 3).reshape(NE1 * P, D1C * E)
    return {k: np.ascontiguousarray(v) for k, v in o.items()}


def kernel(**inputs):
    import concourse.bacc as bacc
    from concourse.bass_utils import run_bass_kernel_spmd

    nc = bacc.Bacc("TRN2", target_bir_lowering=False, num_devices=1)
    arrays, ap = {}, {}
    for name, a in layouts({k: np.asarray(v) for k, v in inputs.items()}).items():
        arrays[f"in_{name}_dram"] = a
        ap[name] = nc.dram_tensor(f"in_{name}_dram", a.shape, mybir.dt.from_np(a.dtype), kind="ExternalInput").ap()
    out = nc.dram_tensor("out_0_dram", [TOK, E], F32, kind="ExternalOutput").ap()
    early_fusion(nc, ap, out)
    r = run_bass_kernel_spmd(nc, [arrays], core_ids=[0])
    return r.results[0]["out_0_dram"].reshape(L, B, E).transpose(1, 0, 2)
```

```python
from contextlib import ExitStack

import numpy as np

import concourse.bass as bass
from concourse import mybir

F32 = mybir.dt.float32
BF16 = mybir.dt.bfloat16
I32 = mybir.dt.int32
U32 = mybir.dt.uint32
ALU = mybir.AluOpType
ACT = mybir.ActivationFunctionType
AX_X = mybir.AxisListType.X

P = 128
B = 64
E = 128
NPATCH = 196
NTEXT = 128
L = NPATCH + NTEXT
TOK = B * L
NT = TOK // P
KP = 768 // P
NH = 8
HD = E // NH
EPS = 1e-5

NE0 = 8
FT = 256
NFT = TOK // FT + NE0 - 1
XS = E + 4
BLANK = 2048


def wait_for(eng, sem, count):
    if isinstance(count, int) and count <= 0:
        return
    eng.wait_ge(sem, count)


def neighbour(i, c, ahead, per, loops):
    i, c = i + (c + ahead) // per, (c + ahead) % per
    if isinstance(i, int) and (i < 0 or i >= loops):
        return None
    return i, c


def repeat(eng, first, end, body, unroll=1):
    assert (end - first) % unroll == 0
    with eng.Fori(0, (end - first) // unroll) as n:
        for m in range(unroll):
            body(n * unroll + (first + m))


class Scope:

    def __init__(self, nc, name):
        self.nc, self.name, self.stack = nc, name, ExitStack()

    def __enter__(self):
        self.stack.__enter__()
        return self

    def __exit__(self, *error):
        return self.stack.__exit__(*error)

    def sb(self, name, shape, dt=F32):
        return self.stack.enter_context(self.nc.sbuf_tensor(f"{self.name}_{name}", shape, dt))

    def ps(self, name, shape, dt=F32):
        return self.stack.enter_context(self.nc.psum_tensor(f"{self.name}_{name}", shape, dt))

    def sem(self, name):
        return self.stack.enter_context(self.nc.semaphore(f"{self.name}_{name}"))

    def block(self):
        return self.stack.enter_context(self.nc.Block())


def tile_of(h, j):
    return h[:, bass.ds(j * E, E)]


def clear_semaphores(nc):
    free = sorted(nc.released_uncleared_semaphores)
    with nc.Block() as block:
        @block.gpsimd
        def _(pool):
            pool.sem_clear(range(free[0], free[-1] + 1))


def make_identity(nc, ident):
    with Scope(nc, "id") as s:
        zeroed, done = s.sem("zeroed"), s.sem("done")
        block = s.block()

        @block.gpsimd
        def _(pool):
            pool.memset(ident[:, :], 0.0).then_inc(zeroed, 1)
            pool.wait_ge(zeroed, 1)
            pool.affine_select(out=ident[:, :], in_=ident[:, :], compare_op=ALU.not_equal, fill=1.0, base=0,
                               pattern=[[-1, P]], channel_multiplier=1).then_inc(done, 1)
            pool.wait_ge(done, 1)


def finish_statistics(nc, name, stats, mean, rstd, scale2=None):
    with Scope(nc, name) as s:
        t1, t2, v = s.sb("t1", [P, NT]), s.sb("t2", [P, NT]), s.sb("v", [P, NT])
        sd, var = s.sb("sd", [P, NT]), s.sb("var", [P, NT])
        step, root = s.sem("step"), s.sem("root")
        block = s.block()
        st = stats[:, :].rearrange("p (t k) -> p t k", k=6)

        @block.scalar
        def _(act):
            act.wait_ge(step, 7)
            act.activation(sd[:, :], v[:, :], ACT.Sqrt).then_inc(root, 1)
            if scale2 is not None:
                act.wait_ge(step, 15)
                act.activation(sd[:, :], v[:, :], ACT.Sqrt).then_inc(root, 1)

        @block.vector
        def _(dve):
            count = [0]

            def link(ins):
                count[0] += 1
                ins.then_inc(step, 1)
                dve.wait_ge(step, count[0])

            def invert(out, n):
                dve.wait_ge(root, n)
                link(dve.reciprocal(out[:, :], sd[:, :]))
                link(dve.tensor_tensor(t1[:, :], out[:, :], out[:, :], ALU.mult))
                link(dve.tensor_tensor(t1[:, :], t1[:, :], v[:, :], ALU.mult))
                link(dve.tensor_scalar(t1[:, :], t1[:, :], -0.5, 1.5, ALU.mult, ALU.add))
                link(dve.tensor_tensor(out[:, :], out[:, :], t1[:, :], ALU.mult))

            link(dve.tensor_tensor(t1[:, :], st[:, :, 1], st[:, :, 4], ALU.add))
            link(dve.tensor_scalar(mean[:, :], t1[:, :], 0.5, None, ALU.mult))
            link(dve.tensor_tensor(t2[:, :], st[:, :, 1], st[:, :, 4], ALU.subtract))
            link(dve.scalar_tensor_tensor(out=t1[:, :], in0=t2[:, :], scalar=0.25, in1=t2[:, :],
                                          op0=ALU.mult, op1=ALU.mult))
            link(dve.tensor_tensor(t2[:, :], st[:, :, 2], st[:, :, 5], ALU.add))
            link(dve.scalar_tensor_tensor(out=var[:, :], in0=t2[:, :], scalar=1.0 / E, in1=t1[:, :],
                                          op0=ALU.mult, op1=ALU.add))
            link(dve.tensor_scalar(v[:, :], var[:, :], EPS, None, ALU.add))
            invert(rstd, 1)
            if scale2 is not None:
                link(dve.tensor_tensor(t2[:, :], rstd[:, :], rstd[:, :], ALU.mult))
                link(dve.tensor_tensor(t2[:, :], t2[:, :], var[:, :], ALU.mult))
                link(dve.tensor_scalar(v[:, :], t2[:, :], EPS, None, ALU.add))
                invert(scale2, 2)
                link(dve.tensor_tensor(scale2[:, :], scale2[:, :], rstd[:, :], ALU.mult))


def embed_tokens(nc, patches, text, w, bias, h, stats):
    U = 7
    NPT = NPATCH * B // P
    assert NPT % U == 0
    with Scope(nc, "tok") as s:
        x = [s.sb(f"x{u}", [P, KP * P]) for u in range(U)]
        w_sb = s.sb("w", [P, KP * E])
        b_sb = s.sb("b", [P, E])
        acc = s.ps("acc", [P, U, 512])
        loaded = [s.sem(f"loaded{u}") for u in range(U)]
        weights, text_in = s.sem("weights"), s.sem("text_in")
        product, added, counted = s.sem("product"), s.sem("added"), s.sem("counted")
        block = s.block()

        @block.sync
        def _(sp):
            sp.dma_start(w_sb[:, :], w).then_inc(weights, 16)
            sp.dma_start(b_sb[:, :], bias).then_inc(weights, 16)
            for u in range(U):
                sp.dma_start(x[u][:, :], patches[u * P:(u + 1) * P, :]).then_inc(loaded[u], 16)
            with sp.Fori(1, NPT // U) as i:
                for u in range(U):
                    sp.wait_ge(product, (i - 1) * U + u + 1)
                    sp.dma_start(x[u][:, :], patches[bass.ds((i * U + u) * P, P), :]).then_inc(loaded[u], 16)

        @block.scalar
        def _(act):
            q = (NT - NPT) // 4
            for k in range(4):
                act.dma_start(h[:, (NPT + k * q) * E:(NPT + (k + 1) * q) * E].rearrange("p (t e) -> p t e", e=E),
                               text[k * q:(k + 1) * q, :, :].rearrange("t p e -> p t e")).then_inc(text_in, 16)
            act.wait_ge(text_in, 64)

        @block.tensor
        def _(pe):
            pe.wait_ge(weights, 32)

            def products(i, u):
                pe.wait_ge(loaded[u], (i + 1) * 16)
                wait_for(pe, added, (i - 1) * U + u + 1)
                for k in range(KP):
                    last = pe.matmul(acc[:, u, 0:E], x[u][:, k * P:(k + 1) * P], w_sb[:, k * E:(k + 1) * E],
                                     start=(k == 0), stop=(k == KP - 1))
                last.then_inc(product, 1)

            for u in range(U):
                products(0, u)
            with pe.Fori(1, NPT // U) as i:
                for u in range(U):
                    products(i, u)

        @block.vector
        def _(dve):
            with dve.Fori(0, NPT // U) as i:
                for u in range(U):
                    dve.wait_ge(product, i * U + u + 1)
                    dve.tensor_tensor(tile_of(h, i * U + u), acc[:, u, 0:E], b_sb[:, :], ALU.add)\
                       .then_inc(added, 1)
                    if u >= 1:
                        dve.wait_ge(added, i * U + u)
                        dve.bn_stats(stats[:, bass.ds((i * U + u - 1) * 6, 6)], tile_of(h, i * U + u - 1))\
                           .then_inc(counted, 1)
                dve.wait_ge(added, i * U + U)
                dve.bn_stats(stats[:, bass.ds((i * U + U - 1) * 6, 6)], tile_of(h, i * U + U - 1))\
                   .then_inc(counted, 1)
            dve.wait_ge(text_in, 64)
            with dve.Fori(NPT // 8, NT // 8) as i:
                for u in range(8):
                    dve.bn_stats(stats[:, bass.ds((i * 8 + 2 + u) * 6, 6)], tile_of(h, i * 8 + 2 + u))\
                       .then_inc(counted, 1)


def image_attention(nc, c, h, stats, mean, rstd, blank, sorted_rows):
    G = NT // 2
    N = 2 * P
    NP = 4
    with Scope(nc, "at0") as s:
        wq, wqr, wk, wkr, wv, wo = [s.sb(n, [P, E]) for n in ("wq", "wqr", "wk", "wkr", "wv", "wo")]
        cols = s.sb("cols", [P, 5 + NH])
        rope = s.sb("rope", [P, 4 * B])
        bo = s.sb("bo", [P, N])
        xn = s.sb("xn", [P, N])
        xt = s.sb("xt", [P, NP, 2, B])
        q1, q2, k1, k2 = [s.sb(n, [P, N]) for n in ("q1", "q2", "k1", "k2")]
        q, k = s.sb("q", [P, N]), s.sb("k", [P, N])
        qm = s.sb("qm", [P, NP, NH, B])
        vb = s.sb("vb", [P, NP, 2, P])
        mx = s.sb("mx", [P, NP, 4])
        pr = s.sb("pr", [P, NP, 4, B])
        pt = s.sb("pt", [P, NP, 2, P])
        rc = s.sb("rc", [P, NP, 2, 2])
        on = s.sb("on", [P, NP, E])
        even, ot = s.sb("even", [P, NP, B]), s.sb("ot", [P, N])

        bank = s.ps("bank", [P, 8, 512])
        S = [bank[:, n, :].rearrange("p (i t) -> p i t", t=P) for n in range(NP)]
        PT = bank[:, 0:2, :].rearrange("p a (b c d) -> p a b c d", b=2, c=2)
        AV = bank[:, 2:4, :].rearrange("p a (b c d) -> p a b c d", b=2, c=2)
        Q, QR, K, KR = bank[:, 4, 0:N], bank[:, 4, N:2 * N], bank[:, 5, 0:N], bank[:, 5, N:2 * N]
        V = bank[:, 6, :].rearrange("p (n e) -> p n e", n=NP)
        XT = bank[:, 4, 0:N]
        OT, Y = bank[:, 7, :].rearrange("p (n b) -> p n b", n=NP), bank[:, 7, 0:N]

        const_in, cleared, ones_set = s.sem("const_in"), s.sem("cleared"), s.sem("ones_set")
        blanked, blank_out = s.sem("blanked"), s.sem("blank_out")
        normed, xt_ps, xt_in = s.sem("normed"), s.sem("xt_ps"), s.sem("xt_in")
        qk_ps, v_ps, roped, qk_in, masked = s.sem("qk_ps"), s.sem("v_ps"), s.sem("roped"), s.sem("qk_in"), s.sem("masked")
        bias_added, v_in = s.sem("bias_added"), s.sem("v_in")
        scored, maxed, shifted, raised = s.sem("scored"), s.sem("maxed"), s.sem("shifted"), s.sem("raised")
        pt_ps, pt_in, av_ps, inverted, on_in = s.sem("pt_ps"), s.sem("pt_in"), s.sem("av_ps"), s.sem("inverted"), s.sem("on_in")
        ot_ps, even_in, ot_in, y_ps, h_in, counted = s.sem("ot_ps"), s.sem("even_in"), s.sem("ot_in"), s.sem("y_ps"), s.sem("h_in"), s.sem("counted")
        block = s.block()

        def run(eng, one):
            one(0, False, True, True)
            repeat(eng, 1, G - 2, lambda g: one(g, True, True, True), 3)
            one(G - 2, True, True, False)
            one(G - 1, True, False, False)

        @block.sync
        def _(sp):
            for n, t in enumerate((wq, wqr, wk, wkr, wv, wo)):
                sp.dma_start(t[:, :], c["at0_w"][n, :, :]).then_inc(const_in, 16)
            sp.dma_start(cols[:, :], c["at0_cols"]).then_inc(const_in, 16)
            sp.dma_start(rope[:, :], c["rope"]).then_inc(const_in, 16)
            for n in range(2):
                sp.dma_start(bo[:, n * E:(n + 1) * E], c["at0_bo"]).then_inc(const_in, 16)
            sp.wait_ge(const_in, 16 * 10)
            n = BLANK // P
            sp.wait_ge(blanked, 2)
            for k in range(NFT * FT // BLANK):
                sp.dma_start(sorted_rows[k * BLANK:(k + 1) * BLANK, :].rearrange("(p r) e -> p (r e)", p=P),
                             blank[:, 0:n * XS]).then_inc(blank_out, 16)
            sp.wait_ge(blank_out, 16 * (NFT * FT // BLANK))

        @block.gpsimd
        def _(pool):
            n = BLANK // P
            pool.memset(blank[:, 0:n * XS], 0.0).then_inc(blanked, 1)
            pool.wait_ge(blanked, 1)
            pool.iota(blank[:, 0:n * XS].rearrange("p (r e) -> p r e", e=XS)[:, :, E], pattern=[[1, n]], base=TOK,
                      channel_multiplier=n, allow_small_or_imprecise_dtypes=True).then_inc(blanked, 1)
            pool.memset(vb[:, :, :, :], 0.0).then_inc(cleared, 1)
            pool.memset(on[:, :, :], 0.0).then_inc(cleared, 1)
            pool.wait_ge(cleared, 2)
            for half in range(2):
                pool.memset(vb[64 * half:64 * half + 64, :, :, 64 * half + 32:64 * half + 33], 1.0)\
                    .then_inc(ones_set, 1)
                pool.wait_ge(ones_set, half + 1)
            pool.wait_ge(const_in, 16 * 10)

            def front(g):
                pool.wait_ge(normed, 2 * (g + 1))
                pool.tensor_tensor(h[:, bass.ds(g * N, N)], h[:, bass.ds(g * N, N)], bo[:, :], ALU.add)\
                    .then_inc(bias_added, 1)
                wait_for(pool, masked, NH * g)
                pool.wait_ge(roped, 4 * g + 2)
                pool.tensor_tensor(q[:, :], q1[:, :], q2[:, :], ALU.add).then_inc(qk_in, 1)
                wait_for(pool, scored, NP * g)
                pool.wait_ge(roped, 4 * g + 4)
                pool.tensor_tensor(k[:, :], k1[:, :], k2[:, :], ALU.add).then_inc(qk_in, 1)

            def one(g, before, after, later):
                if after:
                    front(g + 1)

            front(0)
            run(pool, one)

        @block.tensor
        def _(pe):
            pe.wait_ge(const_in, 16 * 10)

            def turn(g):
                pe.wait_ge(normed, 2 * (g + 1))
                wait_for(pe, roped, 4 * g)
                for t in range(2):
                    last = pe.transpose(XT[:, t * P:(t + 1) * P], xn[:, t * P:(t + 1) * P], c["ident"][:, :])
                last.then_inc(xt_ps, 1)

            def project(g):
                pe.wait_ge(xt_in, g + 1)
                wait_for(pe, roped, 4 * g)
                for ps, wt in ((Q, wq), (QR, wqr), (K, wk), (KR, wkr)):
                    pe.matmul(ps, wt[:, :], xt[:, :, 0, :], start=True, stop=True).then_inc(qk_ps, 1)

            def project_v(g):
                wait_for(pe, v_in, 2 * g)
                for n in range(NP):
                    last = pe.matmul(V[:, n, :], xt[:, n, :, :], wv[:, :], start=True, stop=True)
                last.then_inc(v_ps, 1)

            def score(g, positions):
                pe.wait_ge(masked, NH * (g + 1))
                pe.wait_ge(qk_in, 2 * (g + 1))
                for n in positions:
                    if n == 2:
                        wait_for(pe, on_in, 2 * g)
                    for i in range(4):
                        last = pe.matmul(S[n][:, i, :], qm[:, n, 2 * i:2 * i + 2, :],
                                         k[:, (n // 2) * P:(n // 2) * P + P], start=True, stop=True)
                    last.then_inc(scored, 1)

            def turn_heads(g):
                pe.wait_ge(on_in, 2 * (g + 1))
                wait_for(pe, h_in, g)
                for n in range(NP):
                    last = pe.transpose(OT[:, n, :], on[:, n, :], c["ident"][:, :])
                last.then_inc(ot_ps, 1)

            def project_out(g):
                pe.wait_ge(ot_in, g + 1)
                for t in range(2):
                    last = pe.matmul(Y[:, t * P:(t + 1) * P], ot[:, t * P:(t + 1) * P], wo[:, :],
                                     start=True, stop=True)
                last.then_inc(y_ps, 1)

            def turn_probabilities(g):
                pe.wait_ge(raised, NP * (g + 1))
                pe.wait_ge(shifted, NP * (g + 1))
                for n in range(NP):
                    for i in range(2):
                        last = pe.transpose(PT[:, n // 2, n % 2, i, :], pr[:, n, 2 * i:2 * i + 2, :],
                                            c["ident"][:, :])
                    if n % 2:
                        last.then_inc(pt_ps, 1)

            def attend(g):
                pe.wait_ge(v_in, 2 * (g + 1))
                for n in range(NP):
                    if n % 2 == 0:
                        pe.wait_ge(pt_in, 2 * g + n // 2 + 1)
                    for i in range(2):
                        last = pe.matmul(AV[:, n // 2, n % 2, i, :], pt[:, n, i, :], vb[:, n, i, :],
                                         start=True, stop=True)
                last.then_inc(av_ps, 1)

            def one(g, before, after, later):
                if after:
                    turn(g + 1)
                score(g, (0, 1))
                if before:
                    turn_heads(g - 1)
                score(g, (2, 3))
                if after:
                    project(g + 1)
                if before:
                    project_out(g - 1)
                turn_probabilities(g)
                if after:
                    project_v(g + 1)
                attend(g)

            turn(0)
            project(0)
            project_v(0)
            run(pe, one)
            turn_heads(G - 1)
            project_out(G - 1)

        @block.scalar
        def _(act):
            act.wait_ge(const_in, 16 * 10)
            act.wait_ge(ones_set, 2)

            def evacuate_v(g):
                act.wait_ge(v_ps, g + 1)
                wait_for(act, av_ps, g)
                for half in range(2):
                    rows = slice(64 * half, 64 * half + 64)
                    src = V[rows, :, :].rearrange("p n (i c) -> p (n i) c", c=64)[:, :, 32 * half:32 * half + 32]
                    dst = vb[rows, :, :, :].rearrange("p n i c -> p (n i) c")[:, :, 64 * half:64 * half + 32]
                    act.activation(dst, src, ACT.Copy).then_inc(v_in, 1)

            def front(g):
                act.wait_ge(xt_ps, g + 1)
                wait_for(act, v_ps, g)
                wait_for(act, qk_ps, 4 * g)
                act.activation(xt[:, :, :, :], XT.rearrange("p (n b) -> p n b", b=B).unsqueeze(2)
                               .broadcast_to([P, NP, 2, B]), ACT.Copy).then_inc(xt_in, 1)

            def keep_even(g):
                act.wait_ge(ot_ps, g + 1)
                wait_for(act, ot_in, g)
                act.activation(even[:, :, :], OT[:, :, 0:B], ACT.Identity, bias=cols[:, 4:5]).then_inc(even_in, 1)

            def one(g, before, after, later):
                if after:
                    front(g + 1)
                for n in range(NP):
                    if n == 2 and before:
                        keep_even(g - 1)
                    act.wait_ge(shifted, NP * g + n + 1)
                    act.activation(pr[:, n, :, :], pr[:, n, :, :], ACT.Exp).then_inc(raised, 1)
                wait_for(act, av_ps, g)
                for n in range(2):
                    act.wait_ge(pt_ps, 2 * g + n + 1)
                    act.activation(pt[:, 2 * n:2 * n + 2, :, :], PT[:, n, :, :, :], ACT.Copy).then_inc(pt_in, 1)
                if after:
                    evacuate_v(g + 1)

            front(0)
            evacuate_v(0)
            run(act, one)
            keep_even(G - 1)

        @block.vector
        def _(dve):
            dve.wait_ge(const_in, 16 * 10)
            dve.wait_ge(cleared, 2)
            tab = rope[:, :].rearrange("p (k b) -> p k b", k=4)

            def normalise(g):
                wait_for(dve, xt_ps, g)
                for t in range(2):
                    j = 2 * g + t
                    dve.tensor_scalar(xn[:, t * E:(t + 1) * E], tile_of(h, j), mean[:, bass.ds(j, 1)],
                                      rstd[:, bass.ds(j, 1)], ALU.subtract, ALU.mult).then_inc(normed, 1)

            def rotate(g):
                wait_for(dve, qk_in, 2 * g)
                for n, (ps, to) in enumerate(((Q, q1), (QR, q2), (K, k1), (KR, k2))):
                    dve.wait_ge(qk_ps, 4 * g + (2 if n < 2 else 4))
                    dve.scalar_tensor_tensor(out=to[:, :].rearrange("p (n b) -> p n b", b=B),
                                             in0=ps.rearrange("p (n b) -> p n b", b=B), scalar=cols[:, n:n + 1],
                                             in1=tab[:, n:n + 1, :].broadcast_to([P, NP, B]),
                                             op0=ALU.add, op1=ALU.mult).then_inc(roped, 1)

            def mask(g):
                dve.wait_ge(qk_in, 2 * g + 1)
                wait_for(dve, scored, NP * g)
                for n in range(NH):
                    dve.tensor_scalar(qm[:, :, n, :], q[:, :].rearrange("p (n b) -> p n b", b=B), cols[:, 5 + n:6 + n],
                                      None, ALU.mult).then_inc(masked, 1)

            def shift(g, positions):
                wait_for(dve, pt_ps, 2 * g)
                own = lambda n: S[n][:, :, (n % 2) * B:(n % 2) * B + B]
                for n in positions:
                    dve.wait_ge(scored, NP * g + n + 1)
                    dve.tensor_reduce(mx[:, n, :], own(n), AX_X, ALU.max).then_inc(maxed, 1)
                for n in positions:
                    dve.wait_ge(maxed, NP * g + n + 1)
                    dve.tensor_tensor(pr[:, n, :, :], own(n), mx[:, n, :].unsqueeze(2).broadcast_to([P, 4, B]),
                                      ALU.subtract).then_inc(shifted, 1)

            def weigh(g):
                dve.wait_ge(av_ps, g + 1)
                dve.reciprocal(rc[:, :, :, :].rearrange("p n i k -> p (n i) k"),
                               AV.rearrange("p a b c (k d) -> p (a b c) k d", k=2)[:, :, :, 32])\
                   .then_inc(inverted, 1)
                dve.wait_ge(inverted, g + 1)
                wait_for(dve, ot_ps, g)
                for par in range(2):
                    rows = slice(64 * par, 64 * par + 64)
                    src = AV.rearrange("p a b c (k d) -> p (a b c) k d", k=2)[rows, :, :, HD * par:HD * par + HD]
                    dst = on[rows, :, :].rearrange("p n (i k d) -> p (n i) k d", i=2, k=2)[:, :, :, HD * par:HD * par + HD]
                    inv = rc[rows, :, :, :].rearrange("p n i k -> p (n i) k").unsqueeze(3).broadcast_to([64, 8, 2, HD])
                    dve.tensor_tensor(dst, src, inv, ALU.mult).then_inc(on_in, 1)

            def add_parities(g):
                dve.wait_ge(even_in, g + 1)
                wait_for(dve, y_ps, g)
                dve.tensor_tensor(ot[:, :].rearrange("p (n b) -> p n b", b=B), OT[:, :, B:2 * B], even[:, :, :],
                                  ALU.add).then_inc(ot_in, 1)

            def finish(g):
                dve.wait_ge(y_ps, g + 1)
                dve.wait_ge(bias_added, g + 1)
                dve.tensor_tensor(h[:, bass.ds(g * N, N)], Y, h[:, bass.ds(g * N, N)], ALU.add).then_inc(h_in, 1)

            def count(g):
                dve.wait_ge(h_in, g + 1)
                for t in range(2):
                    dve.bn_stats(stats[:, bass.ds((2 * g + t) * 6, 6)], tile_of(h, 2 * g + t)).then_inc(counted, 1)

            def one(g, before, after, later):
                if before:
                    weigh(g - 1)
                shift(g, (0, 1))
                if before:
                    add_parities(g - 1)
                shift(g, (2, 3))
                if later:
                    normalise(g + 2)
                if after:
                    rotate(g + 1)
                if before:
                    finish(g - 1)
                if after:
                    mask(g + 1)
                if before:
                    count(g - 1)

            normalise(0)
            normalise(1)
            rotate(0)
            mask(0)
            run(dve, one)
            weigh(G - 1)
            add_parities(G - 1)
            finish(G - 1)
            count(G - 1)


def token_logits(nc, name, c, h, mean, rstd, w, bias, ne, logits, rows_out=None, h_out=None):
    W = 3
    N = W * P
    NG = NT // W
    with Scope(nc, name) as s:
        w_sb, b_sb = s.sb("w", [P, P]), s.sb("b", [P, ne])
        xn, xt = [s.sb(f"xn{u}", [P, N]) for u in range(2)], [s.sb(f"xt{u}", [P, N]) for u in range(2)]
        xps, lps = [s.ps(f"xps{u}", [P, 512]) for u in range(2)], [s.ps(f"lps{u}", [P, 512]) for u in range(2)]
        const_in, h_stored = s.sem("const_in"), s.sem("h_stored")
        stored = [s.sem(f"stored{u}") for u in range(2)]
        normed, turned, xt_in, product, added = (s.sem(n) for n in ("normed", "turned", "xt_in", "product", "added"))
        block = s.block()

        def run(eng, step):
            for u in range(2):
                step(u, u)
            repeat(eng, 1, NG // 2, lambda i: [step(2 * i + u, u, i) for u in range(2)], 2)

        @block.sync
        def _(sp):
            sp.dma_start(w_sb[:, :], w).then_inc(const_in, 16)
            sp.dma_start(b_sb[:, :], bias).then_inc(const_in, 16)
            if rows_out is not None:
                def step(g, u, i=0):
                    sp.wait_ge(normed, W * (g + 1))
                    dst = rows_out[bass.ds(g * N, N), 0:E].rearrange("(t p) e -> p t e", p=P)
                    sp.dma_start(dst, xn[u][:, :].rearrange("p (t e) -> p t e", e=E)).then_inc(stored[u], 16)
                run(sp, step)
                for u in range(2):
                    sp.wait_ge(stored[u], 16 * (NG // 2))

        @block.vector
        def _(dve):
            dve.wait_ge(const_in, 32)

            def norm(g, u, i=0):
                wait_for(dve, turned, g - 1)
                if rows_out is not None:
                    wait_for(dve, stored[u], 16 * i)
                for t in range(W):
                    j = W * g + t
                    dve.tensor_scalar(xn[u][:, t * E:(t + 1) * E], tile_of(h, j), mean[:, bass.ds(j, 1)],
                                      rstd[:, bass.ds(j, 1)], ALU.subtract, ALU.mult).then_inc(normed, 1)

            def add(g, u):
                dve.wait_ge(product, g + 1)
                lg = logits[:, bass.ds(g * W * ne, W * ne)].rearrange("p (t n) -> p t n", n=ne)
                dve.tensor_tensor(lg, lps[u][:, 0:N].rearrange("p (t n) -> p t n", n=P)[:, :, 0:ne],
                                  b_sb[:, :].unsqueeze(1).broadcast_to([P, W, ne]), ALU.add).then_inc(added, 1)

            norm(0, 0)
            norm(1, 1)

            def both(i):
                for u in range(2):
                    norm(2 * i + u, u, i)
                    add(2 * i + u - 2, u)
            repeat(dve, 1, NG // 2, both, 2)
            add(NG - 2, 0)
            add(NG - 1, 1)

        @block.tensor
        def _(pe):
            pe.wait_ge(const_in, 32)

            def turn(g, u, i=0):
                pe.wait_ge(normed, W * (g + 1))
                wait_for(pe, xt_in, g - 1)
                for t in range(W):
                    last = pe.transpose(xps[u][:, t * P:(t + 1) * P], xn[u][:, t * P:(t + 1) * P], c["ident"][:, :])
                last.then_inc(turned, 1)

            def multiply(g, u):
                pe.wait_ge(xt_in, g + 1)
                wait_for(pe, added, g - 1)
                for t in range(W):
                    last = pe.matmul(lps[u][:, t * P:(t + 1) * P], xt[u][:, t * P:(t + 1) * P], w_sb[:, :],
                                     start=True, stop=True)
                last.then_inc(product, 1)

            turn(0, 0)
            turn(1, 1)
            multiply(0, 0)
            turn(2, 0)
            multiply(1, 1)

            def both(i):
                for u in range(2):
                    turn(2 * i + u + 1, 1 - u)
                    multiply(2 * i + u, u)
            repeat(pe, 1, NG // 2 - 1, both, 5)
            turn(NG - 1, 1)
            multiply(NG - 2, 0)
            multiply(NG - 1, 1)

        @block.scalar
        def _(act):
            if h_out is not None:
                for k in range(6):
                    q = NT // 6
                    act.dma_start(h_out[k * q * P:(k + 1) * q * P, :].rearrange("(t p) e -> p t e", p=P),
                                  h[:, k * q * E:(k + 1) * q * E].rearrange("p (t e) -> p t e", e=E))\
                       .then_inc(h_stored, 16)

            def step(g, u, i=0):
                act.wait_ge(turned, g + 1)
                wait_for(act, product, g - 1)
                act.activation(xt[u][:, :], xps[u][:, 0:N], ACT.Copy).then_inc(xt_in, 1)
            run(act, step)
            if h_out is not None:
                act.wait_ge(h_stored, 16 * 6)


H0 = 512
WB0 = H0 + H0 + 4 + E


def route_top1(nc, c, logits, dest, ratio, tile_expert, room):
    N = NT * NE0
    with Scope(nc, "rt0") as s:
        mx, sm = s.sb("mx", [P, NT]), s.sb("sm", [P, NT])
        key, hot, ex, cum, tot = (room[:, n * N:(n + 1) * N] for n in range(5))
        hot16 = s.sb("hot16", [P, N], BF16)
        tri, ones = s.sb("tri", [P, P], BF16), s.sb("ones", [P, P], BF16)
        small = s.sb("small", [P, 8, NE0])
        zero = s.sb("zero", [P, N])
        cnt = s.sb("cnt", [P, NE0], I32)
        tid, le = s.sb("tid", [P, NFT]), s.sb("le", [P, NFT, NE0 - 1])
        tef = s.sb("tef", [P, NFT])
        ranks, totals = s.ps("ranks", [P, 3, 512]), s.ps("totals", [P, 3, 512])
        const_in, consts, step, raised, counted = (s.sem(n) for n in ("const_in", "consts", "step", "raised", "counted"))
        block = s.block()
        by_te = lambda a: a[:, :].rearrange("p (t e) -> p t e", e=NE0)
        by_et = lambda a: a[:, :].rearrange("p (e t) -> p e t", t=NT)

        @block.sync
        def _(sp):
            sp.dma_start(small[:, 0, :], c["falling"]).then_inc(const_in, 16)

        @block.gpsimd
        def _(pool):
            pool.memset(tri[:, :], 1.0).then_inc(consts, 1)
            pool.memset(ones[:, :], 1.0).then_inc(consts, 1)
            pool.wait_ge(consts, 2)
            pool.affine_select(out=tri[:, :], in_=tri[:, :], compare_op=ALU.is_gt, fill=0.0, base=0,
                               pattern=[[1, P]], channel_multiplier=-1).then_inc(consts, 1)
            pool.iota(tid[:, :], pattern=[[1, NFT]], base=0, channel_multiplier=0,
                      allow_small_or_imprecise_dtypes=True).then_inc(consts, 1)

        @block.tensor
        def _(pe):
            pe.wait_ge(consts, 4)
            pe.wait_ge(step, 6)
            third = N // 3
            for n in range(3):
                pe.matmul(ranks[:, n, 0:third], tri[:, :], hot16[:, n * third:(n + 1) * third], start=True, stop=True)
                last = pe.matmul(totals[:, n, 0:third], ones[:, :], hot16[:, n * third:(n + 1) * third],
                                 start=True, stop=True)
            last.then_inc(counted, 1)

        @block.scalar
        def _(act):
            act.wait_ge(step, 7)
            act.activation(ex[:, :], ex[:, :], ACT.Exp).then_inc(raised, 1)

        @block.vector
        def _(dve):
            n = [0]

            def link(ins):
                n[0] += 1
                ins.then_inc(step, 1)
                dve.wait_ge(step, n[0])

            dve.wait_ge(const_in, 16)
            mx_b = mx[:, :].unsqueeze(2).broadcast_to([P, NT, NE0])
            link(dve.tensor_reduce(mx[:, :], by_te(logits), AX_X, ALU.max))
            link(dve.tensor_tensor(by_te(key), by_te(logits), mx_b, ALU.is_ge))
            link(dve.tensor_tensor(by_te(key), by_te(key), small[:, 0:1, :].broadcast_to([P, NT, NE0]), ALU.mult))
            link(dve.tensor_reduce(sm[:, :], by_te(key), AX_X, ALU.max))
            link(dve.tensor_tensor(by_te(hot), by_te(key), sm[:, :].unsqueeze(2).broadcast_to([P, NT, NE0]),
                                   ALU.is_equal))
            link(dve.tensor_copy(hot16[:, :], hot[:, :]))
            link(dve.tensor_tensor(by_te(ex), by_te(logits), mx_b, ALU.subtract))
            link(dve.memset(zero[:, :], 0.0))
            dve.wait_ge(raised, 1)
            link(dve.tensor_reduce(sm[:, :], by_te(ex), AX_X, ALU.add))
            link(dve.reciprocal(mx[:, :], sm[:, :]))
            link(dve.reciprocal(sm[:, :], mx[:, :]))
            link(dve.tensor_tensor(ratio[:, :], mx[:, :], sm[:, :], ALU.mult))
            dve.wait_ge(counted, 1)
            third = NT // 3
            for k in range(3):
                dst = by_et(tot)[:, :, k * third:(k + 1) * third].rearrange("p e t -> p t e")
                link(dve.tensor_copy(dst, totals[:, k, 0:third * NE0].rearrange("p (t e) -> p t e", e=NE0)))
            link(dve.tensor_tensor_scan(cum[:, :], tot[:, :], zero[:, :], 0.0, ALU.add, ALU.add))
            first, ends = small[:, 1, :], by_et(cum)[:, :, NT - 1]
            link(dve.memset(small[:, 1:8, :], 0.0))
            link(dve.tensor_copy(first[:, 1:NE0], ends[:, 0:NE0 - 1]))
            link(dve.tensor_tensor(small[:, 2, :], ends, first, ALU.subtract))
            link(dve.tensor_scalar(cnt[:, :], small[:, 2, :], float(FT - 1), None, ALU.add))
            link(dve.tensor_scalar(cnt[:, :], cnt[:, :], 8, None, ALU.logical_shift_right))
            link(dve.tensor_copy(small[:, 3, :], cnt[:, :]))
            link(dve.tensor_tensor_scan(small[:, 4, :], small[:, 3, :], small[:, 7, :], 0.0, ALU.add, ALU.add))
            link(dve.tensor_tensor(small[:, 5, :], small[:, 4, :], small[:, 3, :], ALU.subtract))
            link(dve.scalar_tensor_tensor(out=small[:, 6, :], in0=small[:, 5, :], scalar=float(FT), in1=first,
                                          op0=ALU.mult, op1=ALU.subtract))
            link(dve.tensor_tensor(cum[:, :], cum[:, :], tot[:, :], ALU.subtract))
            link(dve.tensor_tensor(by_et(cum), by_et(cum), small[:, 6, :].unsqueeze(2).broadcast_to([P, NE0, NT]),
                                   ALU.add))
            for k in range(3):
                part = by_te(key)[:, k * third:(k + 1) * third, :]
                link(dve.tensor_tensor(part, ranks[:, k, 0:third * NE0].rearrange("p (t e) -> p t e", e=NE0),
                                       by_et(cum)[:, :, k * third:(k + 1) * third].rearrange("p e t -> p t e"),
                                       ALU.add))
            link(dve.tensor_tensor(key[:, :], key[:, :], hot[:, :], ALU.mult))
            link(dve.tensor_reduce(sm[:, :], by_te(key), AX_X, ALU.add))
            link(dve.tensor_copy(dest[:, :], sm[:, :]))
            dve.wait_ge(consts, 4)
            link(dve.tensor_tensor(le[:, :, :], tid[:, :].unsqueeze(2).broadcast_to([P, NFT, NE0 - 1]),
                                   small[:, 4:5, 0:NE0 - 1].broadcast_to([P, NFT, NE0 - 1]), ALU.is_ge))
            link(dve.tensor_reduce(tef[:, :], le[:, :, :], AX_X, ALU.add))
            link(dve.tensor_copy(tile_expert[:, :], tef[:, :]))


def scatter_rows(nc, c, h, mean, rstd, dest, sorted_rows, weights):
    U = 6
    with Scope(nc, "scat") as s:
        xn = [s.sb(f"xn{u}", [P, XS]) for u in range(U)]
        at = [s.sb(f"at{u}", [P, 1], U32) for u in range(U)]
        number = s.sb("number", [P, NT])
        numbered, padded, w_in = s.sem("numbered"), s.sem("padded"), s.sem("w_in")
        normed, issued = s.sem("normed"), s.sem("issued")
        sent = [s.sem(f"sent{u}") for u in range(U)]
        block = s.block()

        @block.sync
        def _(sp):
            for e in range(NE0):
                sp.dma_start(weights[:, e * WB0:(e + 1) * WB0], c["ffn0_wb"][e * P:(e + 1) * P, :]).then_inc(w_in, 16)
            sp.wait_ge(w_in, 16 * NE0)

        @block.vector
        def _(dve):
            for u in range(U):
                dve.memset(xn[u][:, E:XS], 0.0).then_inc(padded, 1)
            dve.wait_ge(padded, U)
            dve.wait_ge(numbered, 1)

            def step(i, u):
                j = i * U + u
                wait_for(dve, sent[u], 16 * i)
                dve.tensor_copy(at[u][:, :], dest[:, bass.ds(j, 1)]).then_inc(normed, 1)
                dve.tensor_copy(xn[u][:, E:E + 1], number[:, bass.ds(j, 1)]).then_inc(normed, 1)
                dve.tensor_scalar(xn[u][:, 0:E], tile_of(h, j), mean[:, bass.ds(j, 1)], rstd[:, bass.ds(j, 1)],
                                  ALU.subtract, ALU.mult).then_inc(normed, 1)
            for u in range(U):
                step(0, u)
            with dve.Fori(1, NT // U) as i:
                for u in range(U):
                    step(i, u)

        @block.gpsimd
        def _(pool):
            pool.iota(number[:, :], pattern=[[P, NT]], base=0, channel_multiplier=1,
                      allow_small_or_imprecise_dtypes=True).then_inc(numbered, 1)
            with pool.Fori(0, NT // U) as i:
                for u in range(U):
                    pool.wait_ge(normed, 3 * (i * U + u + 1))
                    pool.sem_inc(issued, 1)
                    pool.indirect_dma_start(out=sorted_rows[:, :],
                                            out_offset=bass.IndirectOffsetOnAxis(ap=at[u][:, 0:1], axis=0),
                                            in_=xn[u][:, :], in_offset=None).then_inc(sent[u], 16)
            for u in range(U):
                pool.wait_ge(sent[u], 16 * (NT // U))


def sorted_ffn(nc, c, tile_expert, sorted_rows, weights, token_out):
    HC = H0 // P
    R = FT // P
    U = 4
    LOOPS = NFT // U
    assert NFT % U == 0
    with Scope(nc, "ffn0") as s:
        wb = [weights[:, (NE0 + u) * WB0:(NE0 + u + 1) * WB0] for u in range(U)]
        x = [s.sb(f"x{u}", [P, R, XS]) for u in range(U)]
        at = [[s.sb(f"at{u}_{r}", [P, 1], U32) for r in range(R)] for u in range(U)]
        xt = [s.sb(f"xt{u}", [P, FT]) for u in range(2)]
        hid = [s.sb(f"hid{u}", [P, HC, FT]) for u in range(2)]
        y = [s.sb(f"y{u}", [P, R, E]) for u in range(U)]
        xps, yps = [s.ps(f"xps{u}", [P, 512]) for u in range(2)], [s.ps(f"yps{u}", [P, 512]) for u in range(2)]
        up = [s.ps(f"up{u}", [P, 2, 512]) for u in range(2)]
        x_in, sent = ([s.sem(f"{n}{u}") for u in range(U)] for n in ("x_in", "sent"))
        w_in, issued, index_in = s.sem("w_in"), s.sem("issued"), s.sem("index_in")
        turned, xt_in, upped, gelued, downed, y_in = (s.sem(n) for n in ("turned", "xt_in", "upped", "gelued", "downed", "y_in"))
        block = s.block()

        def run(eng, one):
            for c_ in range(U):
                one(0, c_)
            with eng.Fori(1, LOOPS - 1) as i:
                for c_ in range(U):
                    one(i, c_)
            for c_ in range(U):
                one(LOOPS - 1, c_)

        @block.sync
        def _(sp):
            def one(i, c_):
                t = U * i + c_
                wait_for(sp, index_in, R * (t - U + 1))
                sp.dma_start(x[c_][:, :, :], sorted_rows[bass.ds(t * FT, FT), :].rearrange("(p r) e -> p r e", r=R))\
                  .then_inc(x_in[c_], 16)
            run(sp, one)

        @block.gpsimd
        def _(pool):
            def one(i, c_):
                pool.wait_ge(y_in, U * i + c_ + 1)
                pool.sem_inc(issued, 1)
                for r in range(R):
                    pool.indirect_dma_start(out=token_out[:, :],
                                            out_offset=bass.IndirectOffsetOnAxis(ap=at[c_][r][:, 0:1], axis=0),
                                            in_=y[c_][:, r, :], in_offset=None).then_inc(sent[c_], 16)

            run(pool, one)
            for u in range(U):
                pool.wait_ge(sent[u], 16 * R * LOOPS)

        @block.tensor
        def _(pe):
            def turn(i, c_):
                t, u = U * i + c_, c_ % 2
                pe.wait_ge(x_in[c_], 16 * (i + 1))
                wait_for(pe, xt_in, t - 1)
                for r in range(R):
                    last = pe.transpose(xps[u][:, r * P:(r + 1) * P], x[c_][:, r, 0:E], c["ident"][:, :])
                last.then_inc(turned, 1)

            def widen(i, c_):
                t, u = U * i + c_, c_ % 2
                pe.wait_ge(w_in, t + 1)
                pe.wait_ge(xt_in, t + 1)
                wait_for(pe, gelued, HC * (t - 1))
                for m in range(HC):
                    pe.matmul(up[u][:, m // 2, (m % 2) * FT:(m % 2) * FT + FT], wb[c_][:, m * P:(m + 1) * P],
                              xt[u][:, :], start=True, stop=True).then_inc(upped, 1)

            def narrow(i, c_):
                t, u = U * i + c_, c_ % 2
                pe.wait_ge(gelued, HC * (t + 1))
                wait_for(pe, y_in, t - 1)
                for r in range(R):
                    for m in range(HC):
                        last = pe.matmul(yps[u][:, r * E:(r + 1) * E], hid[u][:, m, r * P:(r + 1) * P],
                                         wb[c_][:, H0 + m * E:H0 + (m + 1) * E], start=(m == 0), stop=(m == HC - 1))
                last.then_inc(downed, 1)

            def one(i, c_):
                widen(i, c_)
                after, before = neighbour(i, c_, 1, U, LOOPS), neighbour(i, c_, -1, U, LOOPS)
                if after:
                    turn(*after)
                if before:
                    narrow(*before)

            turn(0, 0)
            run(pe, one)
            narrow(LOOPS - 1, U - 1)

        @block.scalar
        def _(act):
            def one(i, c_):
                t, u = U * i + c_, c_ % 2
                wait_for(act, downed, t - 1)
                for m in range(HC):
                    act.wait_ge(upped, HC * t + 2 * (m // 2) + 2)
                    act.activation(hid[u][:, m, :], up[u][:, m // 2, (m % 2) * FT:(m % 2) * FT + FT], ACT.Gelu,
                                   bias=wb[c_][:, 2 * H0 + m:2 * H0 + m + 1]).then_inc(gelued, 1)
            run(act, one)

        @block.vector
        def _(dve):
            def place(i, c_):
                t = U * i + c_
                expert = dve.value_load(tile_expert[0:1, bass.ds(t, 1)], min_val=0, max_val=NE0 - 1)
                wait_for(dve, y_in, t - U + 1)
                dve.tensor_copy(wb[c_][:, :], weights[:, bass.ds(expert * WB0, WB0)]).then_inc(w_in, 1)

            def evacuate(i, c_):
                t, u = U * i + c_, c_ % 2
                dve.wait_ge(turned, t + 1)
                wait_for(dve, upped, HC * (t - 1))
                dve.tensor_copy(xt[u][:, :], xps[u][:, 0:FT]).then_inc(xt_in, 1)
                wait_for(dve, sent[c_], 16 * R * i)
                for r in range(R):
                    dve.tensor_copy(at[c_][r][:, :], x[c_][:, r, E:E + 1]).then_inc(index_in, 1)

            def finish(i, c_):
                t, u = U * i + c_, c_ % 2
                dve.wait_ge(downed, t + 1)
                b2 = wb[c_][:, 2 * H0 + 4:WB0].unsqueeze(1).broadcast_to([P, R, E])
                dve.tensor_tensor(y[c_][:, :, :], yps[u][:, 0:R * E].rearrange("p (r e) -> p r e", e=E), b2, ALU.add)\
                   .then_inc(y_in, 1)

            def one(i, c_):
                after, before = neighbour(i, c_, 1, U, LOOPS), neighbour(i, c_, -1, U, LOOPS)
                if after:
                    evacuate(*after)
                if before:
                    finish(*before)
                soon = neighbour(i, c_, 2, U, LOOPS)
                if soon:
                    place(*soon)

            place(0, 0)
            place(0, 1)
            evacuate(0, 0)
            run(dve, one)
            finish(LOOPS - 1, U - 1)


def add_rows(nc, h, ratio, token_out, stats):
    W = 9
    U = 3
    LOADS = NT // W
    assert LOADS % U == 0
    with Scope(nc, "add") as s:
        y = [s.sb(f"y{u}", [P, W * E]) for u in range(U)]
        got = [s.sem(f"got{u}") for u in range(U)]
        added, counted = s.sem("added"), s.sem("counted")
        block = s.block()

        @block.sync
        def _(sp):
            def load(i, u):
                n = i * U + u
                wait_for(sp, added, W * (n - U + 1))
                sp.dma_start(y[u][:, :].rearrange("p (t e) -> p t e", e=E),
                             token_out[bass.ds(n * W * P, W * P), :].rearrange("(t p) e -> p t e", p=P))\
                  .then_inc(got[u], 16)
            for u in range(U):
                load(0, u)
            with sp.Fori(1, LOADS // U) as i:
                for u in range(U):
                    load(i, u)

        @block.vector
        def _(dve):
            with dve.Fori(0, LOADS // U) as i:
                for u in range(U):
                    dve.wait_ge(got[u], 16 * (i + 1))
                    first = (i * U + u) * W
                    for t in range(W + 1):
                        if t < W:
                            j = first + t
                            dve.scalar_tensor_tensor(out=tile_of(h, j), in0=y[u][:, t * E:(t + 1) * E],
                                                     scalar=ratio[:, bass.ds(j, 1)], in1=tile_of(h, j),
                                                     op0=ALU.mult, op1=ALU.add).then_inc(added, 1)
                        if t:
                            dve.wait_ge(added, first + t)
                            dve.bn_stats(stats[:, bass.ds((first + t - 1) * 6, 6)], tile_of(h, first + t - 1))\
                               .then_inc(counted, 1)


WIN, HOP = 20, 10
NW = (L - WIN) // HOP + 1
NB = L // HOP
WP = 32
NTC = B * L + 2 * WP


def turn_rows(nc, c, h, mean, scale, turned_rows, h_keep):
    W = 3
    N = W * P
    NG = NT // W
    with Scope(nc, "turn") as s:
        gb = s.sb("gb", [P, 2])
        xn = [s.sb(f"xn{u}", [P, N]) for u in range(2)]
        xps = [s.ps(f"xps{u}", [P, 512]) for u in range(2)]
        const_in, stored, cleared = s.sem("const_in"), s.sem("stored"), s.sem("cleared")
        normed, turned, placed = s.sem("normed"), s.sem("turned"), s.sem("placed")
        block = s.block()

        def run(eng, step):
            for u in range(2):
                step(u, u)
            with eng.Fori(1, NG // 2) as i:
                for u in range(2):
                    step(2 * i + u, u)

        @block.sync
        def _(sp):
            sp.dma_start(gb[:, :], c["at1_gb"]).then_inc(const_in, 16)
            q = NT // 6
            for k in range(6):
                sp.dma_start(h_keep[k * q * P:(k + 1) * q * P, :].rearrange("(t p) e -> p t e", p=P),
                             h[:, k * q * E:(k + 1) * q * E].rearrange("p (t e) -> p t e", e=E)).then_inc(stored, 16)
            sp.wait_ge(stored, 16 * 6)

        @block.gpsimd
        def _(pool):
            pool.memset(turned_rows[:, B * L:NTC], 0.0).then_inc(cleared, 1)

        @block.vector
        def _(dve):
            def step(g, u):
                wait_for(dve, turned, g - 1)
                for t in range(W):
                    j = W * g + t
                    dve.tensor_scalar(xn[u][:, t * E:(t + 1) * E], tile_of(h, j), mean[:, bass.ds(j, 1)],
                                      scale[:, bass.ds(j, 1)], ALU.subtract, ALU.mult).then_inc(normed, 1)
            run(dve, step)

        @block.tensor
        def _(pe):
            def step(g, u):
                pe.wait_ge(normed, W * (g + 1))
                wait_for(pe, placed, g - 1)
                for t in range(W):
                    last = pe.transpose(xps[u][:, t * P:(t + 1) * P], xn[u][:, t * P:(t + 1) * P], c["ident"][:, :])
                last.then_inc(turned, 1)
            run(pe, step)

        @block.scalar
        def _(act):
            act.wait_ge(const_in, 16)

            def step(g, u):
                act.wait_ge(turned, g + 1)
                by_image = turned_rows[:, 0:B * L].rearrange("p (b l) -> p l b", l=L)
                act.activation(by_image[:, bass.ds(2 * W * g, 2 * W), :],
                               xps[u][:, 0:N].rearrange("p (l b) -> p l b", b=B), ACT.Identity,
                               bias=gb[:, 1:2], scale=gb[:, 0:1]).then_inc(placed, 1)
            run(act, step)


def window_attention(nc, c, turned_rows, window_rows):
    GW = 4
    NGR = NB // GW
    Q8 = NH * HOP
    NS = 2
    SB = NB // NS
    KX = HOP * (NB + 7)
    HH = NH // 2
    VC = HH * HD
    with Scope(nc, "at1") as s:
        wq, wk, wv, wo = (s.sb(n, [P, E]) for n in ("wq", "wk", "wv", "wo"))
        cols = s.sb("cols", [P, 3 + NH + HH])
        bo, bias, bv = s.sb("bo", [P, E]), s.sb("bias", [P, E]), s.sb("bv", [P, P])
        xw = [s.sb(f"xw{u}", [P, NB, WP]) for u in range(2)]
        kx = [s.sb(f"kx{u}", [P, KX]) for u in range(2)]
        qs = s.sb("qs", [P, NB * HOP])
        qm = [s.sb(f"qm{u}", [P, NB, NH, HOP]) for u in range(2)]
        bm = s.sb("bm", [P, NB, 3])
        mx = s.sb("mx", [P, NB, 2])
        sums, inv = s.sb("sums", [P, 2, NB]), s.sb("inv", [P, 2, NB])
        pr = [s.sb(f"pr{u}", [P, 2, NB + 1, WP]) for u in range(2)]
        pt = [s.sb(f"pt{u}", [P, 2, HH, 2, HOP]) for u in range(2)]
        vb = [s.sb(f"vb{u}", [P, 2, GW, VC]) for u in range(2)]
        om = s.sb("om", [P, GW, E])
        ot = s.sb("ot", [P, GW, WP])
        y = [s.sb(f"y{u}", [P, NGR, E]) for u in range(2)]

        bank = s.ps("bank", [P, 8, 512])
        AV = bank[:, 3:5, 0:GW * VC].rearrange("p t (w c) -> p t w c", c=VC)
        V, PT = bank[:, 2, 0:E], bank[:, 5, 0:2 * Q8].rearrange("p (a k) -> p a k", a=2)
        OT, Y = bank[:, 6, 0:GW * Q8].rearrange("p (w k) -> p w k", w=GW), bank[:, 7, 0:E]

        const_in, cleared = s.sem("const_in"), s.sem("cleared")
        spread, qk_ps, k_in, q_in, masked = (s.sem(n) for n in ("spread", "qk_ps", "k_in", "q_in", "masked"))
        scored, blocked, maxed, shifted, raised = (s.sem(n) for n in ("scored", "blocked", "maxed", "shifted", "raised"))
        pt_ps, v_ps, pt_in, vb_in, av_ps = (s.sem(n) for n in ("pt_ps", "v_ps", "pt_in", "vb_in", "av_ps"))
        summed, inverted, weighted = s.sem("summed"), s.sem("inverted"), s.sem("weighted")
        bv_in, bias_ps, bias_in, biased = s.sem("bv_in"), s.sem("bias_ps"), s.sem("bias_in"), s.sem("biased")
        om_in, ot_ps, ot_in, y_ps, y_in = (s.sem(n) for n in ("om_in", "ot_ps", "ot_in", "y_ps", "y_in"))
        stored = [s.sem(f"stored{u}") for u in range(2)]
        block = s.block()

        NCLEAR = 8
        banks = [(n, n * SB, min(SB, NB - n * SB)) for n in range(NS)]

        def images(eng, one):
            one(0, 0, 0, True, False)
            one(1, 1, 0, False, False)
            with eng.Fori(1, B // 2 - 1) as i:
                for u in range(2):
                    one(2 * i + u, u, i, False, False)
            one(B - 2, 0, B // 2 - 1, False, False)
            one(B - 1, 1, B // 2 - 1, False, True)

        @block.sync
        def _(sp):
            for n, t in enumerate((wq, wk, wv, wo)):
                sp.dma_start(t[:, :], c["at1_w"][n, :, :]).then_inc(const_in, 16)
            sp.dma_start(cols[:, :], c["at1_cols"]).then_inc(const_in, 16)
            sp.dma_start(bo[:, :], c["at1_bo"]).then_inc(const_in, 16)

            def store(b, u, i, first, last):
                rows = window_rows[bass.ds(b * NW * WP, NW * WP), :]
                sp.wait_ge(biased, b + 1)
                full = (NGR - 1) * P
                sp.dma_start(rows[0:full, :].rearrange("(n p) e -> p n e", p=P), y[u][:, 0:NGR - 1, :])\
                  .then_inc(stored[u], 16)
                sp.dma_start(rows[full:NW * WP, :], y[u][0:NW * WP - full, NGR - 1, :]).then_inc(stored[u], 16)

            images(sp, store)
            for u in range(2):
                sp.wait_ge(stored[u], 32 * (B // 2))

        @block.gpsimd
        def _(pool):
            def spread_rows(b, u):
                wait_for(pool, y_ps, NGR * (b - 1))
                cols_ = turned_rows[:, bass.ds(b * L, NB * HOP + WP - HOP)]
                src = bass.AP(tensor=cols_.tensor, offset=cols_.offset, ap=[list(cols_.ap[0]), [HOP, NB], [1, WP]])
                pool.tensor_copy(xw[u][:, :, :], src).then_inc(spread, 1)

            def mask(b, u):
                pool.wait_ge(q_in, b + 1)
                wait_for(pool, scored, NS * (b - 1))
                heads = cols[:, 3:3 + NH].unsqueeze(1).unsqueeze(3).broadcast_to([P, NB, NH, HOP])
                of = qs[:, :].rearrange("p (j q) -> p j q", q=HOP).unsqueeze(2).broadcast_to([P, NB, NH, HOP])
                pool.tensor_tensor(qm[u][:, :, :, :], of, heads, ALU.mult).then_inc(masked, 1)

            def weigh(b, u, k):
                n, j0, nb = banks[k]
                pool.wait_ge(inverted, NS * b + k + 1)
                part = pr[u][0:Q8, :, j0:j0 + nb, 0:WIN]
                pool.tensor_tensor(part, part, inv[0:Q8, :, j0:j0 + nb].unsqueeze(3).broadcast_to([Q8, 2, nb, WIN]),
                                   ALU.mult).then_inc(weighted, 1)

            def add_bias(b, u):
                pool.wait_ge(y_in, NGR * (b + 1))
                pool.tensor_tensor(y[u][:, :, :], y[u][:, :, :], bias[:, :].unsqueeze(1).broadcast_to([P, NGR, E]),
                                   ALU.add).then_inc(biased, 1)

            def one(b, u, i, first, last):
                if not last:
                    mask(b + 1, 1 - u)
                    spread_rows(b + 1, 1 - u)
                if not first:
                    add_bias(b - 1, 1 - u)
                if not last:
                    for k in range(NS):
                        weigh(b + 1, 1 - u, k)

            pool.wait_ge(const_in, 16 * 6)
            spread_rows(0, 0)
            mask(0, 0)
            for k in range(NS):
                weigh(0, 0, k)
            pool.wait_ge(bias_in, 1)
            images(pool, one)
            add_bias(B - 1, 1)

        @block.tensor
        def _(pe):
            pe.wait_ge(const_in, 16 * 6)
            pe.wait_ge(cleared, NCLEAR)
            pe.wait_ge(bv_in, 1)
            pe.matmul(Y, bv[:, :], wo[:, :], start=True, stop=True).then_inc(bias_ps, 1)

            def project(b):
                wait_for(pe, shifted, NS * b)
                src = turned_rows[:, bass.ds(b * L, L)]
                pe.matmul(bank[:, 0, 0:L], wk[:, :], src, start=True, stop=True).then_inc(qk_ps, 1)
                pe.matmul(bank[:, 1, 0:L], wq[:, :], src, start=True, stop=True).then_inc(qk_ps, 1)

            def score(b, u, part):
                pe.wait_ge(masked, b + 1)
                pe.wait_ge(k_in, b + 1)
                n, j0, nb = banks[part // 2]
                first = j0 + part % 2 * nb // 2
                for j in range(first, first + nb // 2):
                    at = 3 * HOP * (j - j0)
                    width = min(8 * HOP, 512 - at)
                    last = pe.matmul(bank[0:Q8, n, at:at + width], qm[u][:, j, :, :],
                                     kx[u][:, HOP * j:HOP * j + width], start=True, stop=True)
                if part % 2:
                    last.then_inc(scored, 1)

            def turn(b, u, n):
                m = NGR * b + n
                pe.wait_ge(weighted, NS * b + 1 + (GW * (n + 1) >= SB))
                wait_for(pe, pt_in, 2 * m)
                pe.transpose(PT[:, 0, :], pr[u][0:Q8, 0, GW * n + 1:GW * n + 5, :], c["ident"][0:Q8, 0:Q8])
                pe.transpose(PT[:, 1, :], pr[u][0:Q8, 1, GW * n:GW * n + 4, :], c["ident"][0:Q8, 0:Q8])\
                  .then_inc(pt_ps, 1)

            def values(b, u, n):
                m = NGR * b + n
                pe.wait_ge(spread, b + 1)
                wait_for(pe, vb_in, GW * m)
                pe.matmul(V, xw[u][:, GW * n:GW * (n + 1), :], wv[:, :], start=True, stop=True).then_inc(v_ps, 1)

            def attend(b, n):
                m = NGR * b + n
                pe.wait_ge(pt_in, 2 * (m + 1))
                pe.wait_ge(vb_in, GW * (m + 1))
                for t in range(2):
                    wait_for(pe, om_in, 2 * m - 1 + t if not isinstance(m, int) or m else 0)
                    pe.matmul(AV[0:Q8, t, :, :], pt[n % 2][:, t, :, :, :], vb[n % 2][:, t, :, :],
                              start=True, stop=True).then_inc(av_ps, 1)

            def turn_heads(b, n):
                m = NGR * b + n
                pe.wait_ge(om_in, 2 * (m + 1))
                wait_for(pe, ot_in, m)
                for w in range(GW):
                    last = pe.transpose(OT[:, w, :], om[0:Q8, w, :], c["ident"][0:Q8, 0:Q8])
                last.then_inc(ot_ps, 1)

            def project_out(b, u, n):
                m = NGR * b + n
                pe.wait_ge(ot_in, m + 1)
                wait_for(pe, y_in, m)
                if isinstance(m, int) and m == 0:
                    pe.wait_ge(bias_in, 1)
                pe.matmul(Y, xw[u][:, GW * n:GW * (n + 1), :], c["ident"][:, :], start=True, stop=False)
                pe.matmul(Y, ot[:, :, :], wo[:, :], start=False, stop=True).then_inc(y_ps, 1)

            def one(b, u, i, first, last):
                for n in range(NGR):
                    ahead = (b, u, n + 1) if n < NGR - 1 else (b + 1, 1 - u, 0)
                    there = n < NGR - 1 or not last
                    if there:
                        turn(*ahead)
                        values(*ahead)
                    attend(b, n)
                    if n == 0 and not last:
                        project(b + 1)
                    if 3 <= n < 3 + 2 * NS and not last:
                        score(b + 1, 1 - u, n - 3)
                    if n:
                        project_out(b, u, n - 1)
                    elif not first:
                        project_out(b - 1, 1 - u, NGR - 1)
                    turn_heads(b, n)

            project(0)
            for k in range(2 * NS):
                score(0, 0, k)
            turn(0, 0, 0)
            values(0, 0, 0)
            images(pe, one)
            project_out(B - 1, 1, NGR - 1)

        @block.scalar
        def _(act):
            act.wait_ge(const_in, 16 * 6)
            act.wait_ge(cleared, NCLEAR)

            def keys(b, u):
                act.wait_ge(qk_ps, 2 * b + 1)
                wait_for(act, scored, NS * (b - 1))
                act.activation(kx[u][:, HOP:HOP + L], bank[:, 0, 0:L], ACT.Identity, bias=cols[:, 1:2])\
                   .then_inc(k_in, 1)

            def raise_scores(b, u, k):
                for n, j0, nb in banks[k:k + 1]:
                    act.wait_ge(shifted, NS * b + n + 1)
                    act.activation(pr[u][0:Q8, :, j0:j0 + nb, 0:WIN], pr[u][0:Q8, :, j0:j0 + nb, 0:WIN], ACT.Exp)\
                       .then_inc(raised, 1)

            def evacuate(b, n):
                m = NGR * b + n
                act.wait_ge(pt_ps, m + 1)
                wait_for(act, av_ps, 2 * (m - 1))
                for a in range(2):
                    act.activation(pt[n % 2][:, :, :, 1 - a, :],
                                   PT[:, a, :].rearrange("p (t g q) -> p t g q", t=2, q=HOP), ACT.Copy)\
                       .then_inc(pt_in, 1)
                act.wait_ge(v_ps, m + 1)
                for w in range(GW):
                    rows = slice(WP * w, WP * w + WP)
                    act.activation(vb[n % 2][rows, :, w, :], V[rows, :].rearrange("p (t k) -> p t k", t=2),
                                   ACT.Copy).then_inc(vb_in, 1)

            def keep(b, u, i, n):
                m = NGR * b + n
                act.wait_ge(y_ps, m + 1)
                if n == 0:
                    wait_for(act, stored[u], 32 * i)
                act.activation(y[u][:, n, :], Y, ACT.Copy).then_inc(y_in, 1)

            def one(b, u, i, first, last):
                for n in range(NGR):
                    if n < NGR - 1:
                        evacuate(b, n + 1)
                    elif not last:
                        evacuate(b + 1, 0)
                    if n:
                        keep(b, u, i, n - 1)
                    elif not first:
                        keep(b - 1, 1 - u, i - 1 + u, NGR - 1)
                    if n == 0 and not last:
                        keys(b + 1, 1 - u)
                    if n in (4, 6) and not last:
                        raise_scores(b + 1, 1 - u, n // 2 - 2)

            keys(0, 0)
            for k in range(NS):
                raise_scores(0, 0, k)
            evacuate(0, 0)
            images(act, one)
            keep(B - 1, 1, B // 2 - 1, NGR - 1)

        @block.vector
        def _(dve):
            for t in kx:
                dve.memset(t[:, :], 0.0).then_inc(cleared, 1)
            for t in (om, ot):
                dve.memset(t[:, :, :], 0.0).then_inc(cleared, 1)
            for t in vb + pr:
                dve.memset(t[:, :, :, :], 0.0).then_inc(cleared, 1)
            dve.wait_ge(cleared, NCLEAR)
            dve.wait_ge(const_in, 16 * 6)
            dve.tensor_copy(bv[:, :], cols[:, 2:3].broadcast_to([P, P])).then_inc(bv_in, 1)
            dve.wait_ge(bias_ps, 1)
            dve.tensor_tensor(bias[:, :], Y, bo[:, :], ALU.add).then_inc(bias_in, 1)

            def scale_queries(b):
                dve.wait_ge(qk_ps, 2 * b + 2)
                wait_for(dve, masked, b)
                dve.tensor_scalar(qs[:, :], bank[:, 1, 0:NB * HOP], cols[:, 0:1], HD ** -0.5, ALU.add, ALU.mult)\
                   .then_inc(q_in, 1)

            def softmax(b, u, k):
                if k == 0:
                    wait_for(dve, pt_ps, NGR * (b - 1))
                n, j0, nb = banks[k]
                sc = bank[0:Q8, n, 0:3 * HOP * nb].rearrange("p (j k q) -> p j k q", k=3, q=HOP)
                dve.wait_ge(scored, NS * b + n + 1)
                wait_for(dve, maxed, NS * b + n)
                dve.tensor_reduce(bm[0:Q8, j0:j0 + nb, :], sc, AX_X, ALU.max).then_inc(blocked, 1)
                dve.wait_ge(blocked, NS * b + n + 1)
                wait_for(dve, shifted, NS * b + n)
                dve.tensor_tensor(mx[0:Q8, j0:j0 + nb, :], bm[0:Q8, j0:j0 + nb, 0:2], bm[0:Q8, j0:j0 + nb, 1:3],
                                  ALU.max).then_inc(maxed, 1)
                dve.wait_ge(maxed, NS * b + n + 1)
                base = bank[0:Q8, n, 0:3 * HOP * nb]
                both = bass.AP(tensor=base.tensor, offset=base.offset,
                               ap=[list(base.ap[0]), [HOP, 2], [3 * HOP, nb], [1, WIN]])
                dve.tensor_tensor(pr[u][0:Q8, :, j0:j0 + nb, 0:WIN], both,
                                  mx[0:Q8, j0:j0 + nb, :].rearrange("p j a -> p a j").unsqueeze(3)
                                  .broadcast_to([Q8, 2, nb, WIN]), ALU.subtract).then_inc(shifted, 1)

            def total(b, u, k):
                n, j0, nb = banks[k]
                dve.wait_ge(raised, NS * b + k + 1)
                dve.tensor_reduce(sums[0:Q8, :, j0:j0 + nb], pr[u][0:Q8, :, j0:j0 + nb, 0:WIN], AX_X, ALU.add)\
                   .then_inc(summed, 1)
                dve.wait_ge(summed, NS * b + k + 1)
                wait_for(dve, weighted, NS * (b - 1) + k + 1)
                dve.reciprocal(inv[0:Q8, :, j0:j0 + nb], sums[0:Q8, :, j0:j0 + nb]).then_inc(inverted, 1)

            own = cols[0:Q8, 3 + NH:3 + NH + HH].unsqueeze(1).unsqueeze(3).broadcast_to([Q8, GW, HH, HD])

            def mask_heads(b, n):
                m = NGR * b + n
                for t in range(2):
                    dve.wait_ge(av_ps, 2 * m + t + 1)
                    wait_for(dve, ot_ps, m)
                    dve.tensor_tensor(om[0:Q8, :, VC * t:VC * (t + 1)].rearrange("p w (g d) -> p w g d", g=HH),
                                      AV[0:Q8, t, :, :].rearrange("p w (g d) -> p w g d", g=HH), own,
                                      ALU.mult).then_inc(om_in, 1)

            def add_heads(b, n):
                m = NGR * b + n
                dve.wait_ge(ot_ps, m + 1)
                wait_for(dve, y_ps, m)
                dve.tensor_reduce(ot[:, :, 0:WIN], OT.rearrange("p w (g q) -> p w q g", g=HH), AX_X, ALU.add)\
                   .then_inc(ot_in, 1)

            def one(b, u, i, first, last):
                for n in range(NGR):
                    mask_heads(b, n)
                    if n == 0 and not last:
                        scale_queries(b + 1)
                    if n in (4, 6) and not last:
                        softmax(b + 1, 1 - u, n // 2 - 2)
                    add_heads(b, n)
                    if n in (5, 7) and not last:
                        total(b + 1, 1 - u, n // 2 - 2)

            scale_queries(0)
            for k in range(NS):
                softmax(0, 0, k)
                total(0, 0, k)
            images(dve, one)


def combine_windows(nc, h, h_keep, mean, rstd, window_rows, stats):
    T = HOP // 2
    TAIL = NT - T * NB
    with Scope(nc, "comb") as s:
        wa, wb_ = ([s.sb(f"{n}{u}", [P, T * E]) for u in range(2)] for n in ("a", "b"))
        keep, drop = s.sb("keep", [P, NT]), s.sb("drop", [P, NT])
        t1 = [s.sb(f"t{u}", [P, T * E]) for u in range(2)]
        h_in, tail_in, factors = [s.sem(f"h_in{u}") for u in range(2)], s.sem("tail_in"), s.sem("factors")
        a_in, b_in = ([s.sem(f"{n}_in{u}") for u in range(2)] for n in ("a", "b"))
        summed, kept, halved, counted = (s.sem(n) for n in ("summed", "kept", "halved", "counted"))
        block = s.block()

        def load(eng, buf, sem, window, row0):
            for pp in range(2):
                src = window_rows[bass.ds(window * B * WP, B * WP), :].rearrange("(b w) e -> b w e", w=WP)
                src = src[:, row0:row0 + HOP, :].rearrange("b (t k) e -> b k t e", k=2)[:, pp, :, :]
                eng.dma_start(buf[pp * B:(pp + 1) * B, :].rearrange("p (t e) -> p t e", e=E), src).then_inc(sem, 16)

        def blocks(eng, one):
            one(0, 0, 0)
            one(1, 1, 0)
            with eng.Fori(1, NB // 2 - 1) as i:
                for u in range(2):
                    one(2 * i + u, u, i)
            one(NB - 2, 0, NB // 2 - 1)
            one(NB - 1, 1, NB // 2 - 1)

        def has(k, window):
            return not (isinstance(k, int) and k == (NB - 1 if window == "a" else 0))

        @block.scalar
        def _(act):
            def fetch(j0, n, sem):
                act.dma_start(h[:, bass.ds(j0 * E, n * E)].rearrange("p (t e) -> p t e", e=E),
                              h_keep[bass.ds(j0 * P, n * P), :].rearrange("(t p) e -> p t e", p=P)).then_inc(sem, 16)

            def one(k, u, i):
                wait_for(act, h_in[u], 16 * i)
                fetch(k * T, T, h_in[u])
            fetch(NB * T, TAIL, tail_in)
            blocks(act, one)

        @block.sync
        def _(sp):
            def one(k, u, i):
                if has(k, "a"):
                    wait_for(sp, halved, k - 1)
                    load(sp, wa[u], a_in[u], k, 0)
                if has(k, "b"):
                    wait_for(sp, halved, k - 1)
                    load(sp, wb_[u], b_in[u], k - 1, HOP)
            blocks(sp, one)

        @block.gpsimd
        def _(pool):
            def one(k, u, i):
                if has(k, "a") and has(k, "b"):
                    pool.wait_ge(a_in[u], 32 * (i + 1))
                    pool.wait_ge(b_in[u], 32 * (i + u))
                    wait_for(pool, halved, k - 1)
                    pool.tensor_tensor(t1[u][:, :], wa[u][:, :], wb_[u][:, :], ALU.add).then_inc(summed, 1)
            blocks(pool, one)

        @block.vector
        def _(dve):
            dve.tensor_scalar(keep[:, :], rstd[:, :], 1.0, None, ALU.add).then_inc(factors, 1)
            dve.tensor_tensor(drop[:, :], mean[:, :], rstd[:, :], ALU.mult).then_inc(factors, 1)
            dve.wait_ge(factors, 2)

            def norms(j0, n):
                for t in range(n):
                    dve.tensor_scalar(tile_of(h, j0 + t), tile_of(h, j0 + t), keep[:, bass.ds(j0 + t, 1)],
                                      drop[:, bass.ds(j0 + t, 1)], ALU.mult, ALU.subtract).then_inc(kept, 1)
                dve.wait_ge(kept, j0 + n)

            def one(k, u, i):
                dve.wait_ge(h_in[u], 16 * (i + 1))
                norms(k * T, T)
                hh = h[:, bass.ds(k * T * E, T * E)]
                if has(k, "a") and has(k, "b"):
                    dve.wait_ge(summed, k)
                    ins = dve.scalar_tensor_tensor(out=hh, in0=t1[u][:, :], scalar=0.5, in1=hh, op0=ALU.mult, op1=ALU.add)
                else:
                    only, sem = (wa, a_in) if has(k, "a") else (wb_, b_in)
                    dve.wait_ge(sem[u], 32 * (i + 1))
                    ins = dve.tensor_tensor(hh, only[u][:, :], hh, ALU.add)
                ins.then_inc(halved, 1)
                dve.wait_ge(halved, k + 1)
                for t in range(T):
                    dve.bn_stats(stats[:, bass.ds((k * T + t) * 6, 6)], tile_of(h, k * T + t)).then_inc(counted, 1)

            blocks(dve, one)
            dve.wait_ge(tail_in, 16)
            norms(NB * T, TAIL)
            for t in range(TAIL):
                j = NB * T + t
                dve.bn_stats(stats[:, j * 6:j * 6 + 6], tile_of(h, j)).then_inc(counted, 1)


NE1 = 32
CAP = TOK // NE1
GE = 4
XG = E + NE1
HALF = L // 2
LO = 41
HI = 16
SLOTS = HI * LO


def expert_softmax(nc, logits, rows):
    with Scope(nc, "sm1") as s:
        mx, sm, inv = s.sb("mx", [P, NT]), s.sb("sm", [P, NT]), s.sb("inv", [P, NT])
        step, raised, stored = s.sem("step"), s.sem("raised"), s.sem("stored")
        block = s.block()
        lg = logits[:, :].rearrange("p (t e) -> p t e", e=NE1)
        wide = lambda a: a[:, :].unsqueeze(2).broadcast_to([P, NT, NE1])
        PARTS = 6
        q = NT // PARTS

        @block.vector
        def _(dve):
            n = [0]

            def link(ins):
                n[0] += 1
                ins.then_inc(step, 1)
                dve.wait_ge(step, n[0])

            link(dve.tensor_reduce(mx[:, :], lg, AX_X, ALU.max))
            link(dve.tensor_tensor(lg, lg, wide(mx), ALU.subtract))
            dve.wait_ge(raised, 1)
            link(dve.tensor_reduce(sm[:, :], lg, AX_X, ALU.add))
            link(dve.reciprocal(inv[:, :], sm[:, :]))
            link(dve.tensor_tensor(lg, lg, wide(inv), ALU.mult))

        @block.scalar
        def _(act):
            act.wait_ge(step, 2)
            act.activation(logits[:, :], logits[:, :], ACT.Exp).then_inc(raised, 1)

        @block.sync
        def _(sp):
            sp.wait_ge(step, 5)
            for k in range(PARTS):
                sp.dma_start(rows[k * q * P:(k + 1) * q * P, E:XG].rearrange("(t p) e -> p t e", p=P),
                             lg[:, k * q:(k + 1) * q, :]).then_inc(stored, 16)
            sp.wait_ge(stored, 16 * PARTS)


def choose_tokens(nc, c, rows, slot):
    N = HALF * NE1
    BITS = 30
    UPPER = BITS - 16
    with Scope(nc, "top") as s:
        val, cum = s.sb("val", [P, N]), s.sb("cum", [P, N])
        sel, eq = s.sb("sel", [P, N]), s.sb("eq", [P, N])
        mask = s.sb("mask", [P, N], BF16)
        zero = s.sb("zero", [P, N], BF16)
        top, cand16 = s.sb("top", [P, N], BF16), s.sb("cand16", [P, NE1], BF16)
        tri, ones = s.sb("tri", [P, P], BF16), s.sb("ones", [P, P], BF16)
        low, cand, take, bit_a, bit_b = (s.sb(n, [P, NE1], I32) for n in ("low", "cand", "take", "bit_a", "bit_b"))
        ofe, spread = s.sb("ofe", [P, NE1]), s.sb("spread", [P, P])
        cnt, need, first, base = (s.sb(n, [P, NE1]) for n in ("cnt", "need", "first", "base"))
        own = s.sb("own", [P, NE1])
        own16 = s.sb("own16", [P, 2 * NE1], BF16)
        partial, total = s.ps("partial", [P, 512]), s.ps("total", [P, 512])
        before = s.ps("before", [P, 512])
        val_in, consts, ready = s.sem("val_in"), s.sem("consts"), s.sem("ready")
        tried, masked, step = s.sem("tried"), s.sem("masked"), s.sem("step")
        added, spread_in, top_in, cand_in = (s.sem(n) for n in ("added", "spread_in", "top_in", "cand_in"))
        own_in, prefixed = s.sem("own_in"), s.sem("prefixed")
        block = s.block()
        by_fe = lambda a: a[:, :].rearrange("p (f e) -> p f e", e=NE1)
        by_ef = lambda a: a[:, :].rearrange("p (e f) -> p e f", f=HALF)
        swapped = lambda a: by_fe(a).rearrange("p f e -> p e f")
        wide = lambda a: a.unsqueeze(1).broadcast_to([P, HALF, NE1])
        tall = lambda a: a.unsqueeze(2).broadcast_to([P, NE1, HALF])
        chunks = [(k, P) for k in range(0, N - P - N % P, P)] + [(N - P - N % P, N % P), (N - P, P)]
        assert N % P and (N - P) % NE1 == 0
        PARTS = 3
        third = HALF // PARTS

        @block.sync
        def _(sp):
            for half in range(2):
                for k in range(6):
                    q = HALF // 6
                    src = rows[(half * HALF + k * q) * B:(half * HALF + (k + 1) * q) * B, E:XG]
                    sp.dma_start(by_fe(val)[half::2, k * q:(k + 1) * q, :], src.rearrange("(f b) e -> b f e", b=B))\
                      .then_inc(val_in, 16)

        @block.gpsimd
        def _(pool):
            pool.memset(tri[:, :], 1.0).then_inc(consts, 1)
            pool.memset(ones[:, :], 1.0).then_inc(consts, 1)
            pool.wait_ge(consts, 2)
            pool.affine_select(out=tri[:, :], in_=tri[:, :], compare_op=ALU.is_gt, fill=0.0, base=0,
                               pattern=[[1, P]], channel_multiplier=-1).then_inc(consts, 1)

        @block.tensor
        def _(pe):
            pe.wait_ge(consts, 3)

            def count(n):
                wait_for(pe, spread_in, n)
                for k, w in chunks:
                    pe.wait_ge(masked, PARTS * n + min(PARTS, (k + w + third * NE1 - 1) // (third * NE1)))
                    last = pe.matmul(partial[0:w, 0:1], mask[:, k:k + w], ones[:, 0:1], start=(k == 0),
                                     stop=(k + w == N))
                last.then_inc(added, 1)
                pe.wait_ge(spread_in, n + 1)
                pe.matmul(total[:, 0:NE1], spread[:, :], ofe[:, :], start=True, stop=True).then_inc(tried, 1)

            count(0)
            count(1)
            with pe.Fori(1, BITS // 2) as i:
                for u in range(2):
                    count(2 * i + u)
            count(BITS)
            for n in range(2):
                pe.wait_ge(own_in, n + 1)
                pe.matmul(before[:, 0:NE1], tri[:, :], own16[:, n * NE1:(n + 1) * NE1], start=True, stop=True).then_inc(prefixed, 1)

        @block.vector
        def _(dve):
            dve.memset(low[:, :], 0).then_inc(ready, 1)
            dve.memset(bit_a[:, :], 1 << (BITS - 1)).then_inc(ready, 1)
            dve.tensor_reduce(ofe[:, :], c["ident"][:, :].rearrange("p (f e) -> p e f", e=NE1), AX_X, ALU.add)\
               .then_inc(ready, 1)
            dve.memset(zero[:, :], 0.0).then_inc(ready, 1)
            dve.memset(first[:, :], 0.0).then_inc(ready, 1)
            dve.wait_ge(ready, 5)
            dve.wait_ge(val_in, 16 * 12)
            STEPS = 4

            dve.tensor_copy(top[:, :], val[:, :].bitcast(BF16)[:, 1::2]).then_inc(top_in, 1)
            dve.wait_ge(top_in, 1)

            def compare(n, against, op, val=val):
                wait_for(dve, tried, n)
                for k in range(PARTS):
                    f = slice(k * third, (k + 1) * third)
                    dve.tensor_tensor(by_fe(mask)[:, f, :], by_fe(val)[:, f, :], wide(against)[:, f, :], op)\
                       .then_inc(masked, 1)

            def spread_partial(n):
                dve.wait_ge(added, n + 1)
                dve.tensor_copy(spread[:, :], partial[:, 0:1].broadcast_to([P, P])).then_inc(spread_in, 1)
                dve.wait_ge(tried, n + 1)

            def one_bit(n, bit, next_bit, upper):
                link = lambda k, ins: (ins.then_inc(step, 1), dve.wait_ge(step, STEPS * n + k))
                link(1, dve.tensor_tensor(cand[:, :], low[:, :], bit[:, :], ALU.bitwise_or))
                if upper:
                    dve.tensor_copy(cand16[:, :], cand[:, :].bitcast(BF16)[:, 1::2]).then_inc(cand_in, 1)
                    dve.wait_ge(cand_in, n + 1)
                    compare(n, cand16[:, :], ALU.is_ge, top)
                else:
                    compare(n, cand[:, :].bitcast(F32), ALU.is_ge)
                link(2, dve.tensor_scalar(next_bit[:, :], bit[:, :], 1, None, ALU.logical_shift_right))
                spread_partial(n)
                link(3, dve.scalar_tensor_tensor(out=take[:, :], in0=total[:, 0:NE1], scalar=float(CAP),
                                                 in1=bit[:, :], op0=ALU.is_ge, op1=ALU.mult))
                link(4, dve.tensor_tensor(low[:, :], low[:, :], take[:, :], ALU.bitwise_or))

            one_bit(0, bit_a, bit_b, True)
            one_bit(1, bit_b, bit_a, True)
            with dve.Fori(1, UPPER // 2) as i:
                one_bit(2 * i, bit_a, bit_b, True)
                one_bit(2 * i + 1, bit_b, bit_a, True)
            with dve.Fori(UPPER // 2, BITS // 2) as i:
                one_bit(2 * i, bit_a, bit_b, False)
                one_bit(2 * i + 1, bit_b, bit_a, False)

            m = [STEPS * BITS]

            def link(ins):
                m[0] += 1
                ins.then_inc(step, 1)
                dve.wait_ge(step, m[0])

            least = low[:, :].bitcast(F32)
            compare(BITS, least, ALU.is_gt)
            spread_partial(BITS)
            link(dve.tensor_copy(cnt[:, :], total[:, 0:NE1]))
            link(dve.tensor_scalar(need[:, :], cnt[:, :], -1.0, float(CAP), ALU.mult, ALU.add))
            link(dve.tensor_tensor(by_ef(eq), swapped(val), tall(least), ALU.is_equal))
            dve.wait_ge(masked, PARTS * (BITS + 1))
            link(dve.tensor_copy(by_ef(sel), swapped(mask)))

            def ranks(of, n):
                link(dve.tensor_tensor_scan(cum[:, :], of[:, :], zero[:, :], 0.0, ALU.add, ALU.add))
                link(dve.tensor_copy(first[:, 1:NE1], by_ef(cum)[:, 0:NE1 - 1, HALF - 1]))
                link(dve.tensor_tensor(own[:, :], by_ef(cum)[:, :, HALF - 1], first[:, :], ALU.subtract))
                dve.tensor_copy(own16[:, n * NE1:(n + 1) * NE1], own[:, :]).then_inc(own_in, 1)
                dve.wait_ge(prefixed, n + 1)
                link(dve.tensor_tensor(base[:, :], before[:, 0:NE1], first[:, :], ALU.subtract))

            ranks(eq, 0)
            link(dve.tensor_tensor(need[:, :], need[:, :], base[:, :], ALU.subtract))
            link(dve.tensor_tensor(by_ef(cum), by_ef(cum), tall(need[:, :]), ALU.is_le))
            link(dve.tensor_tensor(eq[:, :], eq[:, :], cum[:, :], ALU.mult))
            link(dve.tensor_tensor(sel[:, :], sel[:, :], eq[:, :], ALU.add))
            ranks(sel, 1)
            link(dve.tensor_scalar(base[:, :], base[:, :], 2.0 * SLOTS - 1, None, ALU.add))
            link(dve.scalar_tensor_tensor(out=sel[:, :], in0=sel[:, :], scalar=-2.0 * SLOTS, in1=cum[:, :],
                                          op0=ALU.mult, op1=ALU.add))
            link(dve.tensor_tensor(swapped(slot), by_ef(sel), tall(base[:, :]), ALU.add))


def list_tokens(nc, slot, lists):
    N = HALF * NE1
    NG = NE1 // GE
    FB = 2
    with Scope(nc, "list") as s:
        si, hi_i = s.sb("si", [P, N], I32), s.sb("hi_i", [P, N], I32)
        hi, lo = s.sb("hi", [P, N], BF16), s.sb("lo", [P, N], BF16)
        iota16, iota41, nf = s.sb("iota16", [P, HI]), s.sb("iota41", [P, LO]), s.sb("nf", [P, HALF])
        d16, d41 = s.sb("d16", [P, NG, HI, GE], BF16), s.sb("d41", [P, LO, NE1], BF16)
        np_ = s.sb("np", [P, 1])
        hot = [s.sb(f"hot{u}", [P, FB, NG, HI, GE], BF16) for u in range(2)]
        left = [s.sb(f"left{u}", [P, FB, NG, 2, HI * GE], BF16) for u in range(2)]
        right = [s.sb(f"right{u}", [P, FB, LO, NE1], BF16) for u in range(2)]
        out = s.sb("out", [P, NG, GE, LO])
        acc = s.ps("acc", [P, NG, 512])
        consts, step, hot_in, left_in, right_in = (s.sem(n) for n in ("consts", "step", "hot_in", "left_in", "right_in"))
        owner_in = s.sem("owner_in")
        product, out_in, stored = s.sem("product"), s.sem("out_in"), s.sem("stored")
        block = s.block()
        ng = HALF // FB

        def run(eng, one):
            for u in range(2):
                one(u, u)
            with eng.Fori(1, ng // 2) as i:
                for u in range(2):
                    one(2 * i + u, u)
            if ng % 2:
                one(ng - 1, 0)

        @block.gpsimd
        def _(pool):
            pool.iota(iota16[:, :], pattern=[[1, HI]], base=0, channel_multiplier=0,
                      allow_small_or_imprecise_dtypes=True).then_inc(consts, 1)
            pool.iota(iota41[:, :], pattern=[[1, LO]], base=0, channel_multiplier=0,
                      allow_small_or_imprecise_dtypes=True).then_inc(consts, 1)
            pool.iota(nf[:, :], pattern=[[1, HALF]], base=0, channel_multiplier=0,
                      allow_small_or_imprecise_dtypes=True).then_inc(consts, 1)
            pool.iota(np_[:, :], pattern=[[0, 1]], base=0, channel_multiplier=1,
                      allow_small_or_imprecise_dtypes=True).then_inc(consts, 1)
            pool.wait_ge(consts, 4)

            def one(g, u):
                pool.wait_ge(hot_in, FB * (g + 1))
                wait_for(pool, product, g - 1)
                pool.tensor_tensor(left[u][:, 1, :, 0, :], hot[u][:, 1, :, :, :].rearrange("p g d e -> p g (d e)"),
                                   np_[:, 0:1].unsqueeze(1).broadcast_to([P, NG, HI * GE]), ALU.mult)\
                    .then_inc(owner_in, 1)
            run(pool, one)

        @block.vector
        def _(dve):
            dve.wait_ge(consts, 4)
            n = [0]

            def link(ins):
                n[0] += 1
                ins.then_inc(step, 1)
                dve.wait_ge(step, n[0])

            link(dve.tensor_copy(d16[:, :, :, :], iota16[:, :].unsqueeze(1).unsqueeze(3).broadcast_to([P, NG, HI, GE])))
            link(dve.tensor_copy(d41[:, :, :], iota41[:, :].unsqueeze(2).broadcast_to([P, LO, NE1])))
            link(dve.tensor_scalar(si[:, :], slot[:, :], 1599.0, None, ALU.mult))
            link(dve.tensor_scalar(hi_i[:, :], si[:, :], 16, None, ALU.logical_shift_right))
            link(dve.tensor_copy(hi[:, :], hi_i[:, :]))
            link(dve.scalar_tensor_tensor(out=lo[:, :], in0=hi_i[:, :], scalar=-float(LO), in1=slot[:, :],
                                          op0=ALU.mult, op1=ALU.add))

            def one(g, u):
                wait_for(dve, left_in, g - 1)
                wait_for(dve, owner_in, g - 1)
                wait_for(dve, product, g - 1)
                column = lambda of, f: of[:, bass.ds((g * FB + f) * NE1, NE1)]
                for f in range(FB):
                    own = column(hi, f).rearrange("p (g e) -> p g e", e=GE).unsqueeze(2)
                    dve.tensor_tensor(hot[u][:, f, :, :, :], own.broadcast_to([P, NG, HI, GE]), d16[:, :, :, :],
                                      ALU.is_equal).then_inc(hot_in, 1)
                for f in range(FB):
                    dve.tensor_tensor(right[u][:, f, :, :], column(lo, f).unsqueeze(1).broadcast_to([P, LO, NE1]),
                                      d41[:, :, :], ALU.is_equal).then_inc(right_in, 1)
            run(dve, one)
            dve.wait_ge(product, ng)
            dve.tensor_copy(out[:, :, :, :].rearrange("p g e l -> p g l e"),
                            acc[:, :, 0:GE * LO].rearrange("p g (l e) -> p g l e", e=GE)).then_inc(out_in, 1)

        @block.scalar
        def _(act):
            act.wait_ge(consts, 4)

            def one(g, u):
                act.wait_ge(hot_in, FB * (g + 1))
                wait_for(act, product, g - 1)
                for f in range(FB):
                    if f == 0:
                        act.activation(left[u][:, f, :, 0, :], hot[u][:, f, :, :, :].rearrange("p g d e -> p g (d e)"),
                                       ACT.Copy, scale=np_[:, 0:1])
                    last = act.activation(left[u][:, f, :, 1, :], hot[u][:, f, :, :, :].rearrange("p g d e -> p g (d e)"),
                                          ACT.Copy, scale=nf[:, bass.ds(g * FB + f, 1)])
                last.then_inc(left_in, 1)
            run(act, one)

        @block.tensor
        def _(pe):
            def one(g, u, first=False, last_=False):
                pe.wait_ge(left_in, g + 1)
                pe.wait_ge(owner_in, g + 1)
                pe.wait_ge(right_in, FB * (g + 1))
                for f in range(FB):
                    for m in range(NG):
                        last = pe.matmul(acc[:, m, 0:GE * LO],
                                         left[u][:, f, m, :, :].rearrange("p a k -> p (a k)"),
                                         right[u][:, f, :, GE * m:GE * (m + 1)],
                                         start=first and f == 0, stop=last_ and f == FB - 1)
                last.then_inc(product, 1)
            one(0, 0, True)
            one(1, 1)
            with pe.Fori(1, (ng - 1) // 2) as i:
                for u in range(2):
                    one(2 * i + u, u)
            for g in range(2 * ((ng - 1) // 2), ng):
                one(g, g % 2, False, g == ng - 1)

        @block.sync
        def _(sp):
            sp.wait_ge(out_in, 1)
            for a in range(2):
                for e in range(GE):
                    r0 = a * HI * GE
                    dst = lists[a, :, :].rearrange("(g e) (d l) -> e d g l", e=GE, l=LO)[e, :, :, :]
                    sp.dma_start(dst, out[r0 + e:r0 + HI * GE:GE, :, e, :]).then_inc(stored, 16)
            sp.wait_ge(stored, 16 * 2 * GE)


RC = 108
NC = CAP // RC
D1 = 341
D1C = 3
LASTC = 96
WU = 2 * P + LASTC
WE = WU + D1C


def list_rows(nc, c, lists, index):
    R = NE1 * NC // 2
    with Scope(nc, "lrow") as s:
        q, f = s.sb("q", [R, 2, RC]), s.sb("f", [R, 2, RC])
        qi, odd = s.sb("qi", [R, 2, RC], I32), s.sb("odd", [R, 2, RC], I32)
        ps = s.ps("ps", [P, 2, 512])
        loaded, step, turned = s.sem("loaded"), s.sem("step"), s.sem("turned")
        block = s.block()

        @block.sync
        def _(sp):
            for a, t in enumerate((q, f)):
                for m in range(2):
                    half = slice(m * (NE1 // 2), (m + 1) * (NE1 // 2))
                    sp.dma_start(t[:, m, :], lists[a, half, 0:CAP].rearrange("e (n r) -> e n r", r=RC))\
                      .then_inc(loaded, 16)

        @block.vector
        def _(dve):
            n = [0]

            def link(ins):
                n[0] += 1
                ins.then_inc(step, 1)
                dve.wait_ge(step, n[0])

            dve.wait_ge(loaded, 16 * 4)
            link(dve.tensor_copy(qi[:, :, :], q[:, :, :]))
            link(dve.tensor_scalar(odd[:, :, :], qi[:, :, :], 1, None, ALU.bitwise_and))
            link(dve.tensor_scalar(qi[:, :, :], qi[:, :, :], 1, None, ALU.logical_shift_right))
            link(dve.tensor_copy(q[:, :, :], odd[:, :, :]))
            link(dve.scalar_tensor_tensor(out=f[:, :, :], in0=f[:, :, :], scalar=float(B), in1=qi[:, :, :],
                                          op0=ALU.mult, op1=ALU.add))
            link(dve.scalar_tensor_tensor(out=f[:, :, :], in0=q[:, :, :], scalar=float(HALF * B), in1=f[:, :, :],
                                          op0=ALU.mult, op1=ALU.add))
            dve.wait_ge(turned, 1)
            link(dve.tensor_copy(index[0:RC, :].rearrange("p (m k) -> p m k", m=2), ps[0:RC, :, 0:R]))

        @block.tensor
        def _(pe):
            pe.wait_ge(step, 6)
            for m in range(2):
                last = pe.transpose(ps[0:RC, m, 0:R], f[:, m, :], c["ident"][0:R, 0:R])
            last.then_inc(turned, 1)


def expert_choice_ffn(nc, c, index, rows, out):
    H3 = NC // 2
    N = H3 * RC
    UPG = 2 * GE
    XB = UPG
    with Scope(nc, "ffn1") as s:
        wu = [s.sb(f"wu{u}", [P, WE]) for u in range(2)]
        wd = [s.sb(f"wd{u}", [P, D1C * E]) for u in range(2)]
        at = [[s.sb(f"at{u}_{r}", [RC, 1], U32) for r in range(H3)] for u in range(XB)]
        x = [s.sb(f"x{u}", [RC, H3, XG]) for u in range(XB)]
        xt = [s.sb(f"xt{u}", [P, N]) for u in range(2)]
        hid = [s.sb(f"hid{u}", [P, D1C, N]) for u in range(2)]
        y = [s.sb(f"y{u}", [RC, H3, E]) for u in range(2)]
        up = [s.ps(f"up{u}", [P, D1C, 512]) for u in range(2)]
        xps, yps = s.ps("xps", [P, 512]), s.ps("yps", [P, 512])
        w_in = [s.sem(f"w_in{u}") for u in range(2)]
        got = [s.sem(f"got{u}") for u in range(XB)]
        sent = [s.sem(f"sent{par}") for par in range(2)]
        index_in, issued = s.sem("index_in"), s.sem("issued")
        primed, ones_set = s.sem("primed"), s.sem("ones_set")
        turned, xt_in, upped, raised, downed, y_in = (s.sem(n) for n in ("turned", "xt_in", "upped", "raised", "downed", "y_in"))
        block = s.block()
        GROUPS = NE1 // GE

        def run(eng, one):
            for c_ in range(UPG):
                one(0, c_)
            with eng.Fori(1, GROUPS - 1) as i:
                for c_ in range(UPG):
                    one(i, c_)
            for c_ in range(UPG):
                one(GROUPS - 1, c_)

        def unit(i, c_, ahead):
            return neighbour(i, c_, ahead, UPG, GROUPS)

        @block.sync
        def _(sp):
            def one(i, c_):
                if c_ % 2:
                    return
                v = c_ // 2
                u = v % 2
                wait_for(sp, downed, UPG * i + c_ - 2)
                sp.dma_start(wu[u][:, :], c["ffn1_wu"][bass.ds(i * P, P), :]).then_inc(w_in[u], 16)
                sp.dma_start(wd[u][:, :], c["ffn1_wd"][bass.ds((i * GE + v) * P, P), :]).then_inc(w_in[u], 16)
            run(sp, one)

        @block.gpsimd
        def _(pool):
            def gather(i, c_):
                pool.wait_ge(index_in, H3 * (UPG * i + c_ + 1))
                pool.sem_inc(issued, 1)
                for r in range(H3):
                    pool.indirect_dma_start(out=x[c_][:, r, :], out_offset=None, in_=rows[:, :],
                                            in_offset=bass.IndirectOffsetOnAxis(ap=at[c_][r][:, 0:1], axis=0))\
                        .then_inc(got[c_], 16)

            def one(i, c_):
                nxt = unit(i, c_, XB - 3)
                if nxt:
                    gather(*nxt)
                k = UPG * i + c_
                pool.wait_ge(y_in, k + 1)
                if c_ % 2 == 0:
                    for par in range(2):
                        wait_for(pool, sent[par], 16 * H3 * (GE * i + c_ // 2))
                pool.sem_inc(issued, 1)
                for r in range(H3):
                    pool.indirect_dma_start(out=out[:, :],
                                            out_offset=bass.IndirectOffsetOnAxis(ap=at[c_][r][:, 0:1], axis=0),
                                            in_=y[c_ % 2][:, r, :], in_offset=None, compute_op=ALU.add)\
                        .then_inc(sent[c_ % 2], 16)

            for c_ in range(XB - 3):
                gather(0, c_)
            run(pool, one)
            for par in range(2):
                pool.wait_ge(sent[par], 16 * H3 * NE1)

        @block.tensor
        def _(pe):
            pe.wait_ge(ones_set, 2)

            def turn(i, c_):
                k = UPG * i + c_
                pe.wait_ge(got[c_], 16 * H3 * (i + 1))
                wait_for(pe, xt_in, k)
                for r in range(H3):
                    last = pe.transpose(xps[:, r * RC:(r + 1) * RC], x[c_][:, r, 0:E], c["ident"][0:RC, 0:RC])
                last.then_inc(turned, 1)

            def widen(i, c_):
                k = UPG * i + c_
                v = c_ // 2
                pe.wait_ge(w_in[v % 2], 32 * (2 * i + v // 2 + 1))
                pe.wait_ge(xt_in, k + 1)
                wait_for(pe, raised, D1C * (k - 1))
                for m in range(D1C):
                    M = P if m < D1C - 1 else LASTC
                    pe.matmul(up[c_ % 2][0:M, m, 0:N], wu[v % 2][:, m * P:m * P + M], xt[c_ % 2][:, :],
                              start=True, stop=True).then_inc(upped, 1)

            def narrow(i, c_):
                k = UPG * i + c_
                u = c_ // 2 % 2
                pe.wait_ge(raised, D1C * (k + 1))
                wait_for(pe, y_in, k)
                for r in range(H3):
                    for m in range(D1C):
                        last = pe.matmul(yps[0:RC, r * E:(r + 1) * E], hid[c_ % 2][:, m, r * RC:(r + 1) * RC],
                                         wd[u][:, m * E:(m + 1) * E], start=(m == 0), stop=(m == D1C - 1))
                last.then_inc(downed, 1)

            def one(i, c_):
                widen(i, c_)
                nxt, before = unit(i, c_, 1), unit(i, c_, -1)
                if nxt:
                    turn(*nxt)
                if before:
                    narrow(*before)

            turn(0, 0)
            run(pe, one)
            narrow(GROUPS - 1, UPG - 1)

        @block.scalar
        def _(act):
            def one(i, c_):
                k = UPG * i + c_
                u = c_ // 2 % 2
                wait_for(act, downed, k - 1)
                for m in range(D1C):
                    M = P if m < D1C - 1 else LASTC
                    act.wait_ge(upped, D1C * k + m + 1)
                    act.activation(hid[c_ % 2][0:M, m, :], up[c_ % 2][0:M, m, 0:N], ACT.Silu,
                                   bias=wu[u][0:M, WU + m:WU + m + 1]).then_inc(raised, 1)
            act.wait_ge(ones_set, 2)
            run(act, one)

        @block.vector
        def _(dve):
            for u in range(2):
                dve.memset(hid[u][LASTC:P, D1C - 1, :], 0.0).then_inc(primed, 1)
            dve.wait_ge(primed, 2)
            for u in range(2):
                dve.memset(hid[u][LASTC:LASTC + 1, D1C - 1, :], 1.0).then_inc(ones_set, 1)

            def indices(i, c_):
                for r in range(H3):
                    dve.tensor_copy(at[c_][r][:, :],
                                    index[0:RC, bass.ds((UPG * i + c_) * H3 + r, 1)]).then_inc(index_in, 1)

            def one(i, c_):
                k = UPG * i + c_
                dve.wait_ge(turned, k + 1)
                wait_for(dve, upped, D1C * (k - 1))
                dve.tensor_copy(xt[c_ % 2][:, :], xps[:, 0:N]).then_inc(xt_in, 1)
                before = unit(i, c_, -1)
                if before:
                    finish(*before)

            def finish(i, c_):
                k = UPG * i + c_
                dve.wait_ge(downed, k + 1)
                wait_for(dve, sent[c_ % 2], 16 * H3 * (GE * i + c_ // 2))
                g = x[c_][:, :, bass.ds(E + GE * i + c_ // 2, 1)].broadcast_to([RC, H3, E])
                dve.tensor_tensor(y[c_ % 2][:, :, :], yps[0:RC, 0:H3 * E].rearrange("p (r e) -> p r e", e=E), g,
                                  ALU.mult).then_inc(y_in, 1)
                ahead = unit(i, c_, XB - 2)
                if ahead and unit(i, c_, -2):
                    indices(*ahead)

            for c_ in range(XB):
                indices(0, c_)
            run(dve, one)
            finish(GROUPS - 1, UPG - 1)
def early_fusion(nc, ap, out):
    dram = lambda name, shape: nc.dram_tensor(name, shape, F32).ap()
    sorted_rows, token_out = dram("sorted_rows", [NFT * FT, XS]), dram("token_out", [TOK + BLANK, E])
    h_keep, window_rows = dram("h_keep", [TOK, E]), dram("window_rows", [B * NW * WP, E])
    expert_rows, lists = dram("expert_rows", [TOK, XG]), dram("lists", [2, NE1, SLOTS])
    with Scope(nc, "all") as s:
        ident, stats = s.sb("ident", [P, P]), s.sb("stats", [P, NT * 6])
        mean, rstd, rstd2 = (s.sb(n, [P, NT]) for n in ("mean", "rstd", "rstd2"))
        make_identity(nc, ident)
        c = dict(ap)
        c["ident"] = ident
        with Scope(nc, "wide") as wide:
            turned_rows = wide.sb("turned_rows", [P, NTC])
            with Scope(nc, "front") as front:
                h = front.sb("h", [P, NT * E])
                embed_tokens(nc, ap["patches"], ap["text"], ap["tok_w"], ap["tok_b"], h, stats)
                finish_statistics(nc, "ln0", stats, mean, rstd)
                image_attention(nc, c, h, stats, mean, rstd, turned_rows, sorted_rows)
                with Scope(nc, "route") as r:
                    logits, ratio = r.sb("logits", [P, NT * NE0]), r.sb("ratio", [P, NT])
                    dest, tile_expert = r.sb("dest", [P, NT], U32), r.sb("tile_expert", [P, NFT], I32)
                    finish_statistics(nc, "ln1", stats, mean, rstd)
                    token_logits(nc, "lg0", c, h, mean, rstd, ap["ffn0_r"], ap["ffn0_br"], NE0, logits)
                    route_top1(nc, c, logits, dest, ratio, tile_expert, turned_rows)
                    scatter_rows(nc, c, h, mean, rstd, dest, sorted_rows, turned_rows)
                    sorted_ffn(nc, c, tile_expert, sorted_rows, turned_rows, token_out)
                    add_rows(nc, h, ratio, token_out, stats)
                finish_statistics(nc, "ln2", stats, mean, rstd, rstd2)
                turn_rows(nc, c, h, mean, rstd2, turned_rows, h_keep)
            window_attention(nc, c, turned_rows, window_rows)
        clear_semaphores(nc)
        with Scope(nc, "back") as back:
            logits = back.sb("logits1", [P, NT * NE1])
            h = back.sb("h1", [P, NT * E])
            combine_windows(nc, h, h_keep, mean, rstd, window_rows, stats)
            finish_statistics(nc, "ln3", stats, mean, rstd)
            token_logits(nc, "lg1", c, h, mean, rstd, ap["ffn1_r"], ap["ffn1_br"], NE1, logits, expert_rows, out)
            expert_softmax(nc, logits, expert_rows)
        index = s.sb("index", [P, NE1 * NC], U32)
        with Scope(nc, "choice") as choice:
            slot = choice.sb("slot", [P, HALF * NE1])
            choose_tokens(nc, c, expert_rows, slot)
            list_tokens(nc, slot, lists)
        list_rows(nc, c, lists, index)
        expert_choice_ffn(nc, c, index, expert_rows, out)


def tables():
    r = np.arange(P)
    heads = (r[:, None] // HD == np.arange(NH)[None]).astype(np.float32)
    inv = (1.0 / (np.float32(10000.0) ** (np.arange(0, HD, 2, dtype=np.float32) / np.float32(HD)))).astype(np.float32)
    angle = np.arange(B, dtype=np.float32)[:, None] * inv[None]
    angle = np.concatenate([angle, angle], -1).T
    cos, sin = np.tile(np.cos(angle), (NH, 1)), np.tile(np.sin(angle), (NH, 1))
    sign = np.where(r % HD < HD // 2, -1, 1).astype(np.float32)[:, None]
    qs = np.float32(HD ** -0.5)
    row_head = (r[:, None] // WIN == np.arange(NH // 2)[None]).astype(np.float32)
    row_head[NH * HOP:] = 0
    return {"heads": heads, "rope": np.concatenate([cos * qs, sin * sign * qs, cos, sin * sign], 1).astype(np.float32),
            "row_head": row_head,
            "falling": np.broadcast_to(NE0 - np.arange(NE0, dtype=np.float32), (P, NE0))}


def layouts(i):
    t = tables()
    rows = lambda v: np.broadcast_to(v, (P, v.shape[-1]))
    rot = np.arange(E).reshape(NH, 2, HD // 2)[:, ::-1].reshape(-1)
    o = {k: t[k] for k in ("rope", "falling")}
    x = i["x"].reshape(B, 3, 14, 16, 14, 16).transpose(2, 4, 0, 1, 3, 5).reshape(NPATCH * B // P, P, KP, P)
    o["patches"] = x.transpose(0, 3, 2, 1).reshape(-1, KP * P)
    o["text"] = i["txt"].transpose(1, 0, 2).reshape(NTEXT * B // P, P, E)
    o["tok_w"] = i["L0_tok_w"].T.reshape(KP, P, E).transpose(1, 0, 2).reshape(P, KP * E)
    o["tok_b"] = rows(i["L0_tok_b"])
    wq, wk, wv, wo = (i[f"L0_attn_W{n}"] for n in "qkvo")
    bq, bk, bv = (i[f"L0_attn_b{n}"] for n in "qkv")
    o["at0_w"] = np.stack([wq.T, wq[rot].T, wk.T, wk[rot].T, wv.T, wo.T])
    o["at0_cols"] = np.concatenate([np.stack([bq, bq[rot], bk, bk[rot], bv], 1), t["heads"]], 1)
    o["at0_bo"] = rows(i["L0_attn_bo"])
    o["ffn0_r"] = np.pad(i["L0_ffn_Wr"], ((0, 0), (0, P - NE0)))
    o["ffn0_br"] = rows(i["L0_ffn_br"])
    w2 = i["L0_ffn_W2"].reshape(NE0, H0 // P, P, E).transpose(0, 2, 1, 3).reshape(NE0, P, H0)
    b1 = i["L0_ffn_b1"].reshape(NE0, H0 // P, P).transpose(0, 2, 1)
    b2 = np.broadcast_to(i["L0_ffn_b2"][:, None], (NE0, P, E))
    o["ffn0_wb"] = np.concatenate([i["L0_ffn_W1"], w2, b1, b2], 2).reshape(NE0 * P, WB0)
    w_in, b_in = i["L1_attn_w_in"].reshape(3, E, E), i["L1_attn_b_in"].reshape(3, E)
    o["at1_w"] = np.stack([w_in[0].T, w_in[1].T, w_in[2].T, i["L1_attn_w_out"].T])
    o["at1_cols"] = np.concatenate([b_in.T, t["heads"], t["row_head"]], 1)
    o["at1_bo"] = rows(i["L1_attn_b_out"])
    o["at1_gb"] = np.stack([i["L1_attn_ln_g"], i["L1_attn_ln_b"]], 1)
    o["ffn1_r"] = np.pad(i["L1_ffn_W_router"], ((0, 0), (0, P - NE1)))
    o["ffn1_br"] = rows(i["L1_ffn_b_router"])
    ng = NE1 // GE
    w_up = np.pad(i["L1_ffn_W_up"], ((0, 0), (0, 0), (0, WU - D1)))
    b_up = np.pad(i["L1_ffn_b_up"], ((0, 0), (0, D1C * P - D1))).reshape(ng, D1C, P).transpose(0, 2, 1)
    o["ffn1_wu"] = np.concatenate([w_up, b_up], 2).reshape(ng * P, WE)
    zeros = lambda n: np.zeros((NE1, n, E), np.float32)
    w_down = np.concatenate([i["L1_ffn_W_down"], zeros(WU - D1), i["L1_ffn_b_down"][:, None],
                             zeros(D1C * P - WU - 1)], 1)
    o["ffn1_wd"] = w_down.reshape(NE1, D1C, P, E).transpose(0, 2, 1, 3).reshape(NE1 * P, D1C * E)
    return {k: np.ascontiguousarray(v) for k, v in o.items()}


def kernel(**inputs):
    import concourse.bacc as bacc
    from concourse.bass_utils import run_bass_kernel_spmd

    nc = bacc.Bacc("TRN2", target_bir_lowering=False, num_devices=1)
    arrays, ap = {}, {}
    for name, a in layouts({k: np.asarray(v) for k, v in inputs.items()}).items():
        arrays[f"in_{name}_dram"] = a
        ap[name] = nc.dram_tensor(f"in_{name}_dram", a.shape, mybir.dt.from_np(a.dtype), kind="ExternalInput").ap()
    out = nc.dram_tensor("out_0_dram", [TOK, E], F32, kind="ExternalOutput").ap()
    early_fusion(nc, ap, out)
    r = run_bass_kernel_spmd(nc, [arrays], core_ids=[0])
    return r.results[0]["out_0_dram"].reshape(L, B, E).transpose(1, 0, 2)
```
